# Optimizing a Trainium2 kernel written in Bass

```python
import numpy as np
import jax
import jax.numpy as jnp

def _softmax(x, axis=-1):
    return jax.nn.softmax(x, axis=axis)

def _gelu(x):
    return jax.nn.gelu(x, approximate=True)

def _silu(x):
    return jax.nn.silu(x)

def _sigmoid(x):
    return jax.nn.sigmoid(x)

def _layernorm(x, axis=-1, eps=1e-05):
    m = jnp.mean(x, axis=axis, keepdims=True)
    v = jnp.var(x, axis=axis, keepdims=True)
    return (x - m) / jnp.sqrt(v + eps)

def _scatter_add(tgt, idx, src, axis=0):
    return tgt.at[idx].add(src)

def _segment_sum(src, seg, n):
    return jax.ops.segment_sum(src, seg, n)
kernel_name = 'mk_adaln_d1_jaxref_r4_4d9074'

def setup_inputs(seed: int=0):
    np.random.seed(seed)
    _w = jnp.asarray

    def _L0_attn_setup():
        import jax, jax.numpy as jnp
        import numpy as np
        D_MODEL = 256
        NHEAD = 16
        HEAD_DIM = D_MODEL // NHEAD
        LN_EPS = 1e-05

        def _ema_scan(lam, v):
            a = jnp.broadcast_to(lam, v.shape)

            def combine(e1, e2):
                a1, b1 = e1
                a2, b2 = e2
                return (a1 * a2, a2 * b1 + b2)
            _, state = jax.lax.associative_scan(combine, (a, v), axis=1)
            return state
        key = jax.random.key(seed)
        ks = jax.random.split(key, 6)
        B, S = (4, 1024)
        x = jax.random.normal(ks[0], (B, S, D_MODEL), dtype=jnp.float32)
        scale = 0.02
        Wq = jax.random.normal(ks[1], (D_MODEL, D_MODEL), dtype=jnp.float32) * scale
        Wv = jax.random.normal(ks[2], (D_MODEL, D_MODEL), dtype=jnp.float32) * scale
        Wo = jax.random.normal(ks[3], (D_MODEL, D_MODEL), dtype=jnp.float32) * scale
        Wg = jax.random.normal(ks[4], (D_MODEL, D_MODEL), dtype=jnp.float32) * scale
        beta = jnp.full((NHEAD,), -0.2, dtype=jnp.float32)
        ln_gamma = jnp.ones((D_MODEL,), dtype=jnp.float32)
        ln_beta = jnp.zeros((D_MODEL,), dtype=jnp.float32)
        return {'x': x, 'Wq': Wq, 'Wv': Wv, 'Wo': Wo, 'Wg': Wg, 'beta': beta, 'ln_gamma': ln_gamma, 'ln_beta': ln_beta}
    _L0_attn_in = _L0_attn_setup()

    def _L0_ffn_setup():
        import jax, jax.numpy as jnp
        import numpy as np
        E = 8
        K = 2
        CF = 1.2
        D = 256
        F = 1024
        B, S = (4, 256)
        key = jax.random.key(seed)
        ks = jax.random.split(key, 4)

        def init(k, shape, fan_in):
            return jax.random.normal(k, shape, jnp.float32) * (1.0 / np.sqrt(fan_in))
        return {'x': jax.random.normal(ks[0], (B, S, D), jnp.float32), 'Wg': init(ks[1], (D, E), D), 'bg': jnp.zeros((E,), jnp.float32), 'W1': init(ks[2], (E, D, F), D), 'b1': jnp.zeros((E, F), jnp.float32), 'W2': init(ks[3], (E, F, D), F), 'b2': jnp.zeros((E, D), jnp.float32)}
    _L0_ffn_in = _L0_ffn_setup()
    _L0_c = _w((lambda *s: np.random.randn(*s).astype(np.float32) * 0.05)(4, 256))
    _L0_wmod = _w((lambda *s: np.random.randn(*s).astype(np.float32) * 0.05)(256, 6 * 256) * 256 ** (-0.5))
    _d = {'L0_attn_x': _L0_attn_in['x'], 'L0_attn_Wq': _L0_attn_in['Wq'], 'L0_attn_Wv': _L0_attn_in['Wv'], 'L0_attn_Wo': _L0_attn_in['Wo'], 'L0_attn_Wg': _L0_attn_in['Wg'], 'L0_attn_beta': _L0_attn_in['beta'], 'L0_attn_ln_gamma': _L0_attn_in['ln_gamma'], 'L0_attn_ln_beta': _L0_attn_in['ln_beta'], 'L0_ffn_Wg': _L0_ffn_in['Wg'], 'L0_ffn_bg': _L0_ffn_in['bg'], 'L0_ffn_W1': _L0_ffn_in['W1'], 'L0_ffn_b1': _L0_ffn_in['b1'], 'L0_ffn_W2': _L0_ffn_in['W2'], 'L0_ffn_b2': _L0_ffn_in['b2'], 'L0_c': _L0_c, 'L0_wmod': _L0_wmod}
    _x0 = _d['L0_attn_x']
    _d['L0_attn_x'] = jax.random.normal(jax.random.fold_in(jax.random.key(seed), 1), (4, 1024, 256), dtype=_x0.dtype)
    del _x0
    return _d

def reference(L0_attn_x, L0_attn_Wq, L0_attn_Wv, L0_attn_Wo, L0_attn_Wg, L0_attn_beta, L0_attn_ln_gamma, L0_attn_ln_beta, L0_ffn_Wg, L0_ffn_bg, L0_ffn_W1, L0_ffn_b1, L0_ffn_W2, L0_ffn_b2, L0_c, L0_wmod):

    def _L0_attn_ref(x, Wq, Wv, Wo, Wg, beta, ln_gamma, ln_beta):
        import jax, jax.numpy as jnp
        import numpy as np
        D_MODEL = 256
        NHEAD = 16
        HEAD_DIM = D_MODEL // NHEAD
        LN_EPS = 1e-05

        def _ema_scan(lam, v):
            a = jnp.broadcast_to(lam, v.shape)

            def combine(e1, e2):
                a1, b1 = e1
                a2, b2 = e2
                return (a1 * a2, a2 * b1 + b2)
            _, state = jax.lax.associative_scan(combine, (a, v), axis=1)
            return state
        B, S, _ = x.shape
        q = (x @ Wq.T).reshape(B, S, NHEAD, HEAD_DIM)
        v = (x @ Wv.T).reshape(B, S, NHEAD, HEAD_DIM)
        lam = jax.nn.sigmoid(beta).reshape(1, 1, NHEAD, 1).astype(v.dtype)
        state = _ema_scan(lam, v)
        y = (q * state).reshape(B, S, D_MODEL)
        mu = jnp.mean(y, axis=-1, keepdims=True)
        var = jnp.mean(jnp.square(y - mu), axis=-1, keepdims=True)
        y = (y - mu) * jax.lax.rsqrt(var + LN_EPS) * ln_gamma + ln_beta
        gate = jax.nn.silu(x @ Wg.T)
        y = y * gate
        return y @ Wo.T

    def _L0_ffn_ref(x, Wg, bg, W1, b1, W2, b2):
        import jax, jax.numpy as jnp
        import numpy as np
        E = 8
        K = 2
        CF = 1.2
        D = 256
        F = 1024
        B, S = (4, 256)
        Bx, Sx, Dx = x.shape
        T = Bx * Sx
        xt = x.reshape(T, Dx)
        logits = xt @ Wg + bg
        probs = jax.nn.softmax(logits, axis=-1)
        gate_vals, exp_idx = jax.lax.top_k(probs, K)
        gate_vals = gate_vals / jnp.sum(gate_vals, axis=-1, keepdims=True)
        capacity = int(np.ceil(CF * T * K / E))
        eidx = exp_idx.T.reshape(-1)
        gv = gate_vals.T.reshape(-1)
        oh = jax.nn.one_hot(eidx, E, dtype=jnp.int32)
        pos = jnp.sum((jnp.cumsum(oh, axis=0) - oh) * oh, axis=-1)
        keep = pos < capacity
        pos_c = jnp.where(keep, pos, capacity)
        xk = jnp.tile(xt, (K, 1))
        buf = jnp.zeros((E, capacity + 1, Dx), x.dtype)
        buf = buf.at[eidx, pos_c].add(jnp.where(keep[:, None], xk, 0.0))
        buf = buf[:, :capacity]
        h = jax.nn.gelu(jnp.einsum('ecd,edf->ecf', buf, W1) + b1[:, None, :], approximate=True)
        ye = jnp.einsum('ecf,efd->ecd', h, W2) + b2[:, None, :]
        ye = jnp.concatenate([ye, jnp.zeros((E, 1, Dx), ye.dtype)], axis=1)
        gathered = ye[eidx, pos_c] * (gv * keep.astype(gv.dtype))[:, None]
        out = jnp.sum(gathered.reshape(K, T, Dx), axis=0)
        return out.reshape(Bx, Sx, Dx)
    x = L0_attn_x
    mod = (_silu(L0_c) @ L0_wmod).reshape(L0_c.shape[0], 6, 1, -1)
    sa, ca, ga, sb, cb, gb = (mod[:, 0], mod[:, 1], mod[:, 2], mod[:, 3], mod[:, 4], mod[:, 5])
    ga = (2 * (ga >= 0) - 1) * jnp.maximum(jnp.abs(ga), 0.25)
    gb = (2 * (gb >= 0) - 1) * jnp.maximum(jnp.abs(gb), 0.25)
    h = _layernorm(x, axis=-1) * (1 + ca) + sa
    x = x + ga * _L0_attn_ref(h, L0_attn_Wq, L0_attn_Wv, L0_attn_Wo, L0_attn_Wg, L0_attn_beta, L0_attn_ln_gamma, L0_attn_ln_beta)
    h = _layernorm(x, axis=-1) * (1 + cb) + sb
    x = x + gb * _L0_ffn_ref(h, L0_ffn_Wg, L0_ffn_bg, L0_ffn_W1, L0_ffn_b1, L0_ffn_W2, L0_ffn_b2)
    return x

_drawn_inputs = setup_inputs


def setup_inputs(seed=0):
    import zlib

    import numpy as np

    out = dict(_drawn_inputs(seed))
    spreads = {'L0_attn_beta': (-0.20000000298023224, 0.6),
     'L0_attn_ln_gamma': (1.0, 0.6),
     'L0_attn_ln_beta': (0.0, 0.8),
     'L0_ffn_bg': (0.0, 0.295),
     'L0_ffn_b1': (0.0, 0.619),
     'L0_ffn_b2': (0.0, 0.431)}
    factors = {'L0_attn_Wq': 3.449, 'L0_attn_Wv': 3.349, 'L0_attn_Wo': 3.384, 'L0_attn_Wg': 3.439}
    for name, (base, spread) in spreads.items():
        noise = np.random.default_rng([zlib.crc32(name.encode()), seed]).standard_normal(out[name].shape)
        drawn = base * np.exp(spread * noise) if base else spread * noise
        out[name] = jnp.asarray(drawn.astype(out[name].dtype))
    for name, factor in factors.items():
        out[name] = (out[name] * factor).astype(out[name].dtype)
    return out
```

```python
from contextlib import ExitStack

import concourse.bass as bass
from concourse import mybir

F32 = mybir.dt.float32
F32R = mybir.dt.float32r
BF16 = mybir.dt.bfloat16
I32 = mybir.dt.int32
U32 = mybir.dt.uint32
ALU = mybir.AluOpType
ACT = mybir.ActivationFunctionType
AX_X = mybir.AxisListType.X

P = 128


def adaln_block(nc, x, attn_wT, ln_gamma, ln_beta, beta_ch, router_w, router_b, w1, b1, w2, b2, cT, wmod, out):
    B, S, D = x.shape
    E, _, F = w1.shape
    TOKENS = B * S
    KD = D // P
    KF = F // P
    TILES = TOKENS // P
    TG = 2
    GT = TG * P
    GROUPS = TILES // TG
    GPB = S // GT
    EPS = 1e-5
    TOPK = 2
    CAP = -((-12 * TOKENS * TOPK) // (10 * E))
    ET = -(-CAP // P)
    J = TOPK * TILES
    LAST_COLS = CAP + CAP % 2 - (ET - 1) * P
    CHUNKS = [(0, 2, 2 * P), (7, 3, 2 * P + LAST_COLS), (2, 3, 3 * P), (5, 2, 2 * P)]
    NCH = len(CHUNKS)
    TILES_BEFORE = [sum(n for _, n, _ in CHUNKS[:c]) for c in range(NCH + 1)]
    assert TILES_BEFORE[-1] == ET
    MAXC = [max(CHUNKS[c][2] for c in range(NCH) if c % 2 == r) for r in range(2)]
    NEG = -3.0e38

    x_t = x.rearrange("b (t p) d -> p (b t) d", p=P)
    out_t = out.rearrange("b (t p) d -> p (b t) d", p=P)
    h2_dram = nc.dram_tensor("h2_rows", [TOKENS, D], F32, kind="Internal").ap()
    y_dram = nc.dram_tensor("y_rows", [TOPK * TOKENS, D], F32, kind="Internal").ap()
    mod_dram = nc.dram_tensor("mod_rows", [B, 4 * D], F32, kind="Internal").ap()
    h2_t = h2_dram.rearrange("(t p) d -> p t d", p=P)
    y_t = y_dram.rearrange("(t p) d -> p t d", p=P)

    keep = ExitStack()
    with keep:
        def sem(name):
            return keep.enter_context(nc.semaphore(name))

        def sb(name, shape, dt=F32, stack=keep):
            return stack.enter_context(nc.sbuf_tensor(name, shape, dt))

        psum = keep.enter_context(nc.psum_tensor("psum", [P, 8, 512], F32))

        X = sb("X", [P, TILES, D])
        LG = sb("LG", [P, TILES, E])
        gate1 = sb("gate1", [P, TILES])
        gate2 = sb("gate2", [P, TILES])
        GB = sb("GB", [P, B, D])
        W1raw = sb("W1raw", [P, KD, F])
        W2raw = sb("W2raw", [P, KF, D])
        b1c = sb("b1c", [P, E, KF])
        b2r = sb("b2r", [P, E, D])
        ident = sb("ident", [P, P])
        gidx = sb("gidx", [P, E, ET], I32)
        sidx = sb("sidx", [P, E, ET], I32)

        early = ExitStack()
        wraw = sb("wraw", [P, 4, KD, D], F32, early)
        wos = sb("wos", [P, KD, D], F32, early)
        wm = sb("wm", [P, KD, 6 * D], F32, early)
        modr = sb("modr", [B, 4, D], F32, early)
        mag = sb("mag", [B, 2, D], F32, early)
        modraw = sb("modraw", [B, 2, D], F32, early)
        sgn = sb("sgn", [B, 2, D], F32, early)
        early.close()

        W1hi = sb("W1hi", [P, KD, F], F32R)
        W1lo = sb("W1lo", [P, KD, F], F32R)
        W2hi = sb("W2hi", [P, KF, D], F32R)
        W2lo = sb("W2lo", [P, KF, D], F32R)

        sa_ = ExitStack()
        zeros = sb("zeros", [P, 256], F32, sa_)
        ct = sb("ct", [P, KD, B], F32, sa_)
        sct = sb("sct", [P, KD, B], F32, sa_)
        lamraw = sb("lamraw", [P, KD], F32, sa_)
        whi = sb("whi", [P, 3, KD, D], F32R, sa_)
        wlo = sb("wlo", [P, 3, KD, D], F32R, sa_)
        wohi = sb("wohi", [P, B, KD, D], F32R, sa_)
        wolo = sb("wolo", [P, B, KD, D], F32R, sa_)
        MB = sb("MB", [P, B, 3, D], F32, sa_)
        modc = sb("modc", [P, 2, KD, B], F32, sa_)
        gcol = sb("gcol", [P, KD], F32, sa_)
        bcol = sb("bcol", [P, KD], F32, sa_)
        go = sb("go", [P, 1], F32, sa_)
        lam = sb("lam", [P, KD], F32, sa_)
        lamt = sb("lamt", [P, KD, GT], F32, sa_)
        neghalf = sb("neghalf", [P, TG], F32, sa_)
        rw = sb("rw", [P, KD, E], F32, sa_)
        rb = sb("rb", [P, E], F32, sa_)
        state = sb("state", [P, KD, 2 * GT + 1], F32, sa_)

        def two(name, shape, dt=F32):
            return [sb(f"{name}{r}", shape, dt, sa_) for r in range(2)]

        st = {n: two(f"st_{n}", [P, TG, 6]) for n in "xyh"}
        mv = {n: two(f"mv_{n}", [P, TG, 2]) for n in "xyh"}
        ve = {n: two(f"ve_{n}", [P, TG]) for n in "xyh"}
        nm = {n: two(f"nm_{n}", [P, TG]) for n in "xyh"}
        rs = {n: two(f"rs_{n}", [P, TG]) for n in "xyh"}
        nr = {n: two(f"nr_{n}", [P, TG]) for n in "xy"}
        xn = two("xn", [P, TG, D])
        h32 = two("h32_", [P, KD, GT])
        hhi = two("hhi", [P, KD, GT], F32R)
        hlo = two("hlo", [P, KD, GT], F32R)
        ysb = two("ysb", [P, KD, GT])
        gate = two("gate_", [P, KD, GT])
        yn = two("yn", [P, TG, D])
        z = two("z", [P, KD, GT])
        zg = two("zg", [P, KD, GT])
        zghi = two("zghi", [P, KD, GT], F32R)
        zglo = two("zglo", [P, KD, GT], F32R)
        xn2 = two("xn2_", [P, TG, D])
        x1 = two("x1_", [P, TG, D])
        h2 = two("h2_", [P, TG, D])
        h2T = two("h2T", [P, KD, GT])
        sa_.close()


        sr = ExitStack()
        rt = {n: sb(f"rt_{n}", [P, TILES, E], F32, sr) for n in ("eq1", "sc1", "oh1", "lg2", "eq2", "sc2", "oh2")}
        rm = {n: sb(f"rm_{n}", [P, TILES], F32, sr) for n in ("m1", "i1", "m2", "i2", "dl", "ex", "se")}
        OH = sb("OH", [P, J, E], BF16, sr)
        csum = sb("csum", [P, J, E], F32, sr)
        posa = sb("posa", [P, J, E], F32, sr)
        posb = sb("posb", [P, J, E], F32, sr)
        posc = sb("posc", [P, J, E], F32, sr)
        ohe = sb("ohe", [P, J, E], F32, sr)
        onesj = sb("onesj", [P, J], F32, sr)
        pos = sb("pos", [P, J], F32, sr)
        e10 = sb("e10", [P, J], F32, sr)
        kept = sb("kept", [P, J], F32, sr)
        posi = sb("posi", [P, J], I32, sr)
        hii = sb("hii", [P, J], I32, sr)
        loi = sb("loi", [P, J], I32, sr)
        lof = sb("lof", [P, J], F32, sr)
        hif = sb("hif", [P, J], F32, sr)
        colf = sb("colf", [P, J], F32, sr)
        coff = sb("coff", [P, J], F32, sr)
        col = sb("col", [P, J], F32, sr)
        ioi = sb("ioi", [P, P], I32, sr)
        io = sb("io", [P, P], F32, sr)
        eio = sb("eio", [P, E], F32, sr)
        erank = sb("erank", [P, E], F32, sr)
        pci = sb("pci", [P, 1], I32, sr)
        pcol = sb("pcol", [P, 1], F32, sr)
        jp1 = sb("jp1", [P, J], F32, sr)
        before = sb("before", [P, P], BF16, sr)
        onesb = sb("onesb", [P, P], BF16, sr)
        NC = E * ET
        JC = 16
        ohlo = sb("ohlo", [P, J, P], BF16, sr)
        oheq = sb("oheq", [P, J, NC], BF16, sr)
        ohcp = sb("ohcp", [P, J, 2, NC], BF16, sr)
        tabp = sb("tabp", [P, 2 * NC], F32, sr)
        tabj, tabv, tabe, tabs = (sb(n, [P, NC], F32, sr) for n in ("tabj", "tabv", "tabe", "tabs"))
        tabi = sb("tabi", [P, NC], I32, sr)
        sr.close()

        sf = ExitStack()
        xg = sb("xg", [P, ET, D], F32, sf)
        hThi = [sb(f"hThi{r}", [P, KD, MAXC[r]], F32R, sf) for r in range(2)]
        hTlo = [sb(f"hTlo{r}", [P, KD, MAXC[r]], F32R, sf) for r in range(2)]
        ghi = [sb(f"ghi{r}", [P, KF, MAXC[r]], F32R, sf) for r in range(2)]
        glo = [sb(f"glo{r}", [P, KF, MAXC[r]], F32R, sf) for r in range(2)]
        NG = 4
        g32 = [sb(f"g32_{r}", [P, max(MAXC)], F32, sf) for r in range(NG)]
        yb = sb("yb", [P, ET, D], F32, sf)
        gcur = sb("gcur", [P, ET], I32, sf)
        scur = sb("scur", [P, ET], I32, sf)
        sf.close()

        sl = ExitStack()
        NT = 4
        def pair(name):
            return [sb(f"{name}{r}", [P, NT, D], F32, sl) for r in range(2)]
        y0, y1, yg, ys, yw, yo = (pair(n) for n in ("y0_", "y1_", "yg_", "ys_", "yw_", "yo_"))
        sl.close()

        s_x = sem("x_in")
        s_attnw = sem("attn_weights_in")
        s_mod_in = sem("mod_inputs_in")
        s_small = sem("small_inputs_in")
        s_modout = sem("mod_rows_out")
        s_mb = sem("mod_broadcast_in")
        s_w1 = sem("w1_in")
        s_w2 = sem("w2_in")
        s_b2 = sem("b2_in")
        s_zero = sem("y_rows_zeroed")
        s_h2out = [sem(f"h2_out{r}") for r in range(2)]
        s_gat = [sem(f"gathered{c}") for c in range(NCH)]
        s_sca = [sem(f"scattered{c}") for c in range(NCH)]
        s_yin = [sem(f"y_in{r}") for r in range(2)]
        s_out = [sem(f"out{r}") for r in range(2)]
        (s_pc, s_sct, s_modps, s_modcps, s_modrow, s_modc, s_lam, s_lamt, s_whi, s_wlo, s_wo, s_wohi, s_zeros,
         s_w1hi, s_w1lo, s_w2hi, s_w2lo) = (sem(n) for n in (
            "pool_constants", "silu_c", "mod_rows_psum", "mod_cols_psum", "mod_rows", "mod_cols", "decay", "decay_tile",
            "attn_w_hi", "attn_w_lo", "wo_scaled_lo", "wo_hi", "zero_tile", "w1_hi", "w1_lo", "w2_hi", "w2_lo"))
        s_st = {n: sem(f"stats_{n}") for n in "xyh"}
        s_mv = {n: sem(f"meanvar_{n}") for n in "xyh"}
        s_rs = {n: sem(f"rstd_{n}") for n in "xyh"}
        (s_xn, s_xT, s_h32, s_hhi, s_hlo, s_v, s_q, s_g, s_state, s_y, s_gate, s_yT, s_yn, s_ynT, s_z, s_zg, s_zghi,
         s_zglo, s_o, s_x1, s_xn2, s_h2m, s_h2, s_h2T, s_h2Ts, s_lg, s_lgs) = (sem(n) for n in (
            "xn", "xT", "h32", "h_hi", "h_lo", "v_psum", "q_psum", "g_psum", "state", "y", "gate", "yT", "yn", "ynT",
            "z", "zg", "zg_hi", "zg_lo", "o_psum", "x1", "xn2", "h2_scaled", "h2", "h2T_psum", "h2T", "logits_psum",
            "logits"))
        s_go = sem("constants_ready")
        s_tick = sem("waits_held")
        s_modt, s_rc, s_dl, s_ohd, s_cs, s_ybz, s_x1c = (sem(n) for n in (
            "mod_parts", "routing_constants", "logit_delta", "chosen_experts", "tile_sums", "y_tile_cleared", "x1_kept"))
        (s_rv, s_exp, s_cnt, s_oh, s_ohp, s_ohj, s_slots, s_idx) = (sem(n) for n in (
            "routing_steps", "exp_delta", "counts_psum", "onehots", "onehots_p", "onehots_j", "slots_psum", "index_tables"))
        (s_tr, s_thi, s_tlo, s_w1ps, s_gelu, s_ghi, s_glo, s_w2ps, s_yb, s_gcur, s_scur) = (sem(n) for n in (
            "rowsT_psum", "rowsT_hi", "rowsT_lo", "w1_psum", "gelu", "gelu_hi", "gelu_lo", "w2_psum", "y_tile",
            "gather_indices", "scatter_indices"))
        (s_yg, s_ys, s_yw, s_yo) = (sem(n) for n in ("y0_gated", "y_sum", "y_scaled", "out_tile"))

        def need(eng, s, count):
            if not isinstance(count, int) or count > 0:
                eng.wait_ge(s, count)

        def hold(eng):
            eng.sem_inc(s_tick, 1)

        def f32(ap):
            return ap.bitcast(F32)

        def product(eng, dst, terms, done=None):
            n = len(terms)
            for i, (lh, ll, rh, rl) in enumerate(terms):
                eng.matmul(dst, lh, rh, start=(i == 0), stop=False)
                eng.matmul(dst, lh, rl, start=False, stop=False)
                mm = eng.matmul(dst, ll, rh, start=False, stop=(i == n - 1))
            if done is not None:
                mm.then_inc(done, 1)

        def sweep(eng, step):
            for s in range(-2, 4):
                step(s, s % 2)
            with eng.Fori(2, GROUPS // 2 - 1) as i:
                step(2 * i, 0)
                step(2 * i + 1, 1)
            for s in range(GROUPS - 2, GROUPS + 2):
                step(s, s % 2)

        def has(g):
            return not isinstance(g, int) or 0 <= g < GROUPS

        def stats(eng, n, g, r, src):
            hold(eng)
            for t in range(TG):
                eng.bn_stats(st[n][r][:, t, :], src[t]).then_inc(s_st[n], 1)
            eng.wait_ge(s_st[n], TG * g + TG)
            need(eng, s_rs[n], RSN[n] * (g - 1))
            hold(eng)
            for t in range(TG):
                eng.bn_aggr(mv[n][r][:, t, :], st[n][r][:, t, :]).then_inc(s_mv[n], 1)

        RSN = {"x": 4, "y": 4, "h": 3}

        def rstd(eng, n, g, r):
            eng.wait_ge(s_mv[n], TG * g + TG)
            hold(eng)
            eng.tensor_scalar(ve[n][r][:], mv[n][r][:, :, 1], EPS, None, ALU.add).then_inc(s_rs[n], 1)
            eng.tensor_scalar(nm[n][r][:], mv[n][r][:, :, 0], -1.0, None, ALU.mult).then_inc(s_rs[n], 1)
            eng.wait_ge(s_rs[n], RSN[n] * g + 2)
            eng.tensor_tensor(rs[n][r][:], ve[n][r][:], neghalf[:], ALU.pow).then_inc(s_rs[n], 1)
            if n != "h":
                eng.wait_ge(s_rs[n], RSN[n] * g + 3)
                eng.tensor_tensor(nr[n][r][:], nm[n][r][:], rs[n][r][:], ALU.mult).then_inc(s_rs[n], 1)

        BX, BV, BQ, BG, BY, BN, BO, BH = range(8)

        def bank(b):
            return psum[:, b, :].rearrange("p (k n) -> p k n", k=2)

        block = keep.enter_context(nc.Block())

        @block.sync
        def _(sp):
            sp.dma_start(X[:, 0:4, :], x_t[:, 0:4, :]).then_inc(s_x, 16)
            sp.dma_start(wraw[:], attn_wT).then_inc(s_attnw, 16)
            sp.wait_ge(s_modrow, 4)
            sp.dma_start(mod_dram, modr[:].rearrange("b j d -> b (j d)")).then_inc(s_modout, 16)
            sp.wait_ge(s_modout, 16)
            mod_rows = mod_dram.rearrange("b (j d) -> b j d", j=4)
            sp.dma_start(MB[:], mod_rows[:, 0:3, :].partition_broadcast(P)).then_inc(s_mb, 16)
            sp.dma_start(GB[:], mod_rows[:, 3, :].partition_broadcast(P)).then_inc(s_mb, 16)
            with sp.Fori(1, TILES // 4) as i:
                sp.wait_ge(s_x, 16 * i)
                sp.dma_start(X[:, bass.ds(4 * i, 4), :], x_t[:, bass.ds(4 * i, 4), :]).then_inc(s_x, 16)
            sp.wait_ge(s_x, 16 * (TILES // 4))
            sp.wait_ge(s_zeros, 1)
            sp.dma_start(y_dram.rearrange("(p r c) d -> p r (c d)", p=P, c=1),
                         zeros[:].unsqueeze(1).broadcast_to([P, TOPK * TOKENS // P, D])).then_inc(s_zero, 16)
            sp.dma_start(W1raw[:], w1[0].rearrange("(k p) f -> p k f", p=P)).then_inc(s_w1, 16)
            sp.dma_start(W2raw[:], w2[0].rearrange("(k p) d -> p k d", p=P)).then_inc(s_w2, 16)
            sp.dma_start(b2r[:], b2.partition_broadcast(P)).then_inc(s_b2, 16)

            def store_h2(g, r):
                sp.wait_ge(s_h2, TG * (g + 1))
                need(sp, s_h2out[r], 16 * (g // 2))
                sp.dma_start(h2_t[:, bass.ds(TG * g, TG), :], h2[r][:]).then_inc(s_h2out[r], 16)

            store_h2(0, 0)
            store_h2(1, 1)
            with sp.Fori(1, GROUPS // 2) as i:
                store_h2(2 * i, 0)
                store_h2(2 * i + 1, 1)

            with sp.Fori(1, E) as e:
                sp.wait_ge(s_w1hi, KD * e)
                sp.wait_ge(s_w1lo, KD * e)
                sp.dma_start(W1raw[:], w1[e].rearrange("(k p) f -> p k f", p=P)).then_inc(s_w1, 16)
                sp.wait_ge(s_w2hi, KD * e)
                sp.wait_ge(s_w2lo, KD * e)
                sp.dma_start(W2raw[:], w2[e].rearrange("(k p) d -> p k d", p=P)).then_inc(s_w2, 16)

            for c, (_, n, _) in enumerate(CHUNKS):
                sp.wait_ge(s_sca[c], 16 * n * E)

            def load_y(g, r):
                if not isinstance(g, int):
                    sp.wait_ge(s_yg, NT * (g - 1))
                    sp.wait_ge(s_ys, NT * (g - 1))
                sp.dma_start(y0[r][:], y_t[:, bass.ds(NT * g, NT), :]).then_inc(s_yin[r], 16)
                sp.dma_start(y1[r][:], y_t[:, bass.ds(TILES + NT * g, NT), :]).then_inc(s_yin[r], 16)

            load_y(0, 0)
            load_y(1, 1)
            with sp.Fori(1, TILES // NT // 2) as i:
                load_y(2 * i, 0)
                load_y(2 * i + 1, 1)

        @block.gpsimd
        def _(pool):
            pool.memset(zeros[:], 0.0).then_inc(s_zeros, 1)
            pool.memset(ident[:], 0.0).then_inc(s_pc, 1)
            pool.wait_ge(s_pc, 1)
            pool.affine_select(out=ident[:], in_=ident[:], compare_op=ALU.not_equal, fill=1.0, base=0,
                               pattern=[[-1, P]], channel_multiplier=1).then_inc(s_pc, 1)
            pool.memset(neghalf[:], -0.5).then_inc(s_pc, 1)
            pool.memset(state[:, :, 2 * GT:2 * GT + 1], 0.0).then_inc(s_pc, 1)
            pool.wait_ge(s_pc, 4)
            pool.memset(go[:], 0.0).then_inc(s_go, 1)
            pool.wait_ge(s_zeros, 1)
            pool.wait_ge(s_lam, 1)
            for k in range(KD):
                pool.tensor_scalar(lamt[:, k, :], zeros[:, 0:GT], lam[:, k:k + 1], 0.0, ALU.add, ALU.add)\
                    .then_inc(s_lamt, 1)

            def scale_wo(b):
                if b == 0:
                    pool.wait_ge(s_attnw, 16)
                    pool.wait_ge(s_mb, 32)
                need(pool, s_wohi, b)
                for k in range(KD):
                    pool.tensor_tensor(wos[:, k, :], wraw[:, 3, k, :], MB[:, b, 0, :], ALU.mult).then_inc(s_wo, 1)
                pool.wait_ge(s_wohi, b + 1)
                pool.wait_ge(s_wo, 3 * b + 2)
                pool.tensor_tensor(wolo[:, b], wos[:], f32(wohi[:, b]), ALU.subtract).then_inc(s_wo, 1)

            def split_first(i):
                if i < KD:
                    pool.wait_ge(s_w1, 16)
                    pool.wait_ge(s_w1hi, i + 1)
                    pool.tensor_tensor(W1lo[:, i, :], W1raw[:, i, :], f32(W1hi[:, i, :]), ALU.subtract)\
                        .then_inc(s_w1lo, 1)
                else:
                    i -= KD
                    h = slice(i * KF // 2, (i + 1) * KF // 2)
                    pool.wait_ge(s_w2, 16)
                    pool.wait_ge(s_w2hi, i + 1)
                    pool.tensor_tensor(W2lo[:, h, :], W2raw[:, h, :], f32(W2hi[:, h, :]), ALU.subtract)\
                        .then_inc(s_w2lo, 1)

            def step(s, r):
                if has(s):
                    need(pool, s_yn, TG * (s - 1))
                    rstd(pool, "y", s, r)
                g, q = s - 1, 1 - r
                if has(g):
                    need(pool, s_h2, TG * (g - 1))
                    rstd(pool, "h", g, q)
                    pool.wait_ge(s_rs["h"], RSN["h"] * g + RSN["h"])
                    hold(pool)
                    for t in range(TG):
                        pool.tensor_scalar(xn2[q][:, t, :], x1[q][:, t, :], nm["h"][q][:, t:t + 1],
                                           rs["h"][q][:, t:t + 1], ALU.add, ALU.mult).then_inc(s_xn2, 1)
                    if isinstance(g, int) and g == 0:
                        pool.wait_ge(s_mb, 16 * 2)
                    b = g // GPB
                    pool.wait_ge(s_xn2, TG * g + TG)
                    for t in range(TG):
                        pool.tensor_tensor(xn2[q][:, t, :], xn2[q][:, t, :], MB[:, b, 2, :], ALU.mult)\
                            .then_inc(s_h2m, 1)
                    need(pool, s_h2T, g - 1)
                    need(pool, s_h2out[q], 16 * (g // 2))
                    pool.wait_ge(s_h2m, TG * g + TG)
                    for t in range(TG):
                        pool.tensor_tensor(h2[q][:, t, :], xn2[q][:, t, :], MB[:, b, 1, :], ALU.add)\
                            .then_inc(s_h2, 1)
                    pool.tensor_copy(X[:, bass.ds(TG * g, TG), :], x1[q][:]).then_inc(s_x1c, 1)
                if has(s + 2):
                    need(pool, s_xn, TG * (s + 1))
                    rstd(pool, "x", s + 2, r)
                if isinstance(s, int) and 0 <= s < B:
                    scale_wo(s)
                if isinstance(s, int) and s >= GROUPS - 2:
                    split_first(s - (GROUPS - 2))

            sweep(pool, step)

            pool.wait_ge(s_rv, 1)
            pool.iota(ioi[:], pattern=[[1, P]], base=0, channel_multiplier=0).then_inc(s_rc, 1)
            pool.iota(pci[:], pattern=[[0, 1]], base=0, channel_multiplier=1).then_inc(s_rc, 1)
            pool.memset(onesb[:], 1.0).then_inc(s_rc, 1)
            pool.memset(before[:], 1.0).then_inc(s_rc, 1)
            pool.memset(onesj[:], 1.0).then_inc(s_rc, 1)
            pool.wait_ge(s_rc, 5)
            pool.tensor_copy(io[:], ioi[:]).then_inc(s_rc, 1)
            pool.tensor_copy(pcol[:], pci[:]).then_inc(s_rc, 1)
            pool.affine_select(out=before[:], in_=before[:], compare_op=ALU.is_gt, fill=0.0, base=0,
                               pattern=[[1, P]], channel_multiplier=-1).then_inc(s_rc, 1)
            pool.wait_ge(s_rc, 8)
            pool.tensor_scalar(eio[:], io[:, 0:E], float(ET), 0.0, ALU.mult, ALU.add).then_inc(s_rc, 1)
            pool.tensor_scalar(erank[:], io[:, 0:E], -1.0, float(E), ALU.mult, ALU.add).then_inc(s_rc, 1)
            pool.tensor_scalar(jp1[:], io[:, 0:J], 1.0, 0.0, ALU.add, ALU.add).then_inc(s_rc, 1)
            pool.wait_ge(s_rc, 11)
            for n in range(J // JC):
                js = slice(n * JC, n * JC + JC)
                pool.wait_ge(s_oh, 2 * n + 2)
                pool.tensor_tensor(ohcp[:, js, 1, :], oheq[:, js, :],
                                   jp1[:, js].unsqueeze(2).broadcast_to([P, JC, NC]), ALU.mult).then_inc(s_ohj, 1)

            pool.wait_ge(s_idx, 1)
            pool.memset(yb[:, ET - 1, :], 0.0).then_inc(s_ybz, 1)
            for r in range(2):
                pool.wait_ge(s_h2out[r], 16 * (GROUPS // 2))
            pool.wait_ge(s_zero, 16)

            def gather(e, c):
                t0, n, _ = CHUNKS[c]
                need(pool, s_gat[c], 16 * n * e)
                pool.tensor_copy(gcur[:, t0:t0 + n], gidx[:, e, t0:t0 + n]).then_inc(s_gcur, 1)
                pool.wait_ge(s_gcur, NCH * e + c + 1)
                need(pool, s_tr, NCH * (e - 1) + c + 1)
                hold(pool)
                for t in range(t0, t0 + n):
                    pool.indirect_dma_start(
                        out=xg[:, t, :], out_offset=None, in_=h2_dram,
                        in_offset=bass.IndirectOffsetOnAxis(ap=gcur[:, t:t + 1].bitcast(U32), axis=0),
                        bounds_check=TOKENS - 1, oob_is_err=False).then_inc(s_gat[c], 16)

            def scatter(e, c):
                t0, n, _ = CHUNKS[c]
                need(pool, s_sca[c], 16 * n * e)
                pool.tensor_copy(scur[:, t0:t0 + n], sidx[:, e, t0:t0 + n]).then_inc(s_scur, 1)
                pool.wait_ge(s_scur, NCH * e + c + 1)
                for i in range(n):
                    t = t0 + i
                    pool.wait_ge(s_yb, ET * e + TILES_BEFORE[c] + i + 1)
                    hold(pool)
                    pool.indirect_dma_start(
                        out=y_dram, out_offset=bass.IndirectOffsetOnAxis(ap=scur[:, t:t + 1].bitcast(U32), axis=0),
                        in_=yb[:, t, :], in_offset=None,
                        bounds_check=TOPK * TOKENS - 1, oob_is_err=False).then_inc(s_sca[c], 16)

            def expert(e, first, last):
                for c in range(NCH):
                    if not last:
                        gather(e + 1, c)
                    if c > 0:
                        scatter(e, c - 1)
                    elif not first:
                        scatter(e - 1, NCH - 1)

            for c in range(NCH):
                gather(0, c)
            expert(0, True, False)
            expert(1, False, False)
            with pool.Fori(2, E - 1) as e:
                expert(e, False, False)
            expert(E - 1, False, True)
            scatter(E - 1, NCH - 1)

            def scale_y(g, r):
                pool.wait_ge(s_ys, NT * (g + 1))
                need(pool, s_yo, g - 1)
                pool.tensor_tensor(yw[r][:], ys[r][:], GB[:, g * NT * P // S, :].unsqueeze(1).broadcast_to([P, NT, D]),
                                   ALU.mult).then_inc(s_yw, 1)

            scale_y(0, 0)
            scale_y(1, 1)
            with pool.Fori(1, TILES // NT // 2) as i:
                scale_y(2 * i, 0)
                scale_y(2 * i + 1, 1)

        @block.scalar
        def _(act):
            act.dma_start(ct[:], cT).then_inc(s_mod_in, 16)
            act.dma_start(wm[:], wmod.rearrange("(k p) n -> p k n", p=P)).then_inc(s_mod_in, 16)
            act.dma_start(lamraw[:], beta_ch).then_inc(s_small, 16)
            act.dma_start(gcol[:], ln_gamma).then_inc(s_small, 16)
            act.dma_start(bcol[:], ln_beta).then_inc(s_small, 16)
            act.dma_start(rw[:], router_w).then_inc(s_small, 16)
            act.dma_start(rb[:], router_b.partition_broadcast(P)).then_inc(s_small, 16)
            act.dma_start(b1c[:], b1).then_inc(s_small, 16)
            act.wait_ge(s_small, 16 * 6)
            act.activation(lam[:], lamraw[:], ACT.Sigmoid).then_inc(s_lam, 1)
            act.wait_ge(s_mod_in, 32)
            act.activation(sct[:], ct[:], ACT.Silu).then_inc(s_sct, 1)
            act.wait_ge(s_attnw, 16)
            for w in range(3):
                act.activation(whi[:, w], wraw[:, w], ACT.Copy).then_inc(s_whi, 1)

            def step(s, r):
                q = 1 - r
                g = s - 1
                if has(g):
                    act.wait_ge(s_ynT, g + 1)
                    need(act, s_zg, g - 1)
                    for k in range(KD):
                        act.activation(z[q][:, k, :], bank(BN)[:, k, :], ACT.Identity, bias=bcol[:, k:k + 1],
                                       scale=gcol[:, k:k + 1]).then_inc(s_z, 1)
                g = s + 1
                if has(g):
                    act.wait_ge(s_rs["x"], RSN["x"] * (g + 1))
                    need(act, s_xT, g - 1)
                    hold(act)
                    for t in range(TG):
                        act.activation(xn[q][:, t, :], X[:, TG * g + t, :], ACT.Identity, bias=nr["x"][q][:, t:t + 1],
                                       scale=rs["x"][q][:, t:t + 1]).then_inc(s_xn, 1)
                g = s
                if has(g):
                    act.wait_ge(s_g, g + 1)
                    need(act, s_zg, g - 1)
                    act.activation(gate[r][:], bank(BG), ACT.Silu).then_inc(s_gate, 1)
                g = s - 1
                if has(g):
                    act.wait_ge(s_zg, g + 1)
                    need(act, s_o, g - 1)
                    act.activation(zghi[q][:], zg[q][:], ACT.Copy).then_inc(s_zghi, 1)
                g = s + 1
                if has(g):
                    b = g // GPB
                    act.wait_ge(s_xT, g + 1)
                    need(act, s_hlo, g - 1)
                    if isinstance(g, int) and g == 0:
                        act.wait_ge(s_modc, 2)
                    hold(act)
                    for k in range(KD):
                        act.activation(h32[q][:, k, :], bank(BX)[:, k, :], ACT.Identity,
                                       bias=modc[:, 0, k, bass.ds(b, 1)], scale=modc[:, 1, k, bass.ds(b, 1)])\
                            .then_inc(s_h32, 1)
                    act.wait_ge(s_h32, KD * (g + 1))
                    need(act, s_g, g - 1)
                    act.activation(hhi[q][:], h32[q][:], ACT.Copy).then_inc(s_hhi, 1)
                g = s - 2
                if has(g):
                    act.wait_ge(s_h2T, g + 1)
                    need(act, s_lg, g - 1)
                    act.activation(h2T[r][:], bank(BH), ACT.Copy).then_inc(s_h2Ts, 1)
                g = s
                if has(g):
                    act.wait_ge(s_rs["y"], RSN["y"] * (g + 1))
                    need(act, s_ynT, g - 1)
                    for t in range(TG):
                        act.activation(yn[r][:, t, :], bank(BY)[:, t, :], ACT.Identity, bias=nr["y"][r][:, t:t + 1],
                                       scale=rs["y"][r][:, t:t + 1]).then_inc(s_yn, 1)
                if isinstance(s, int) and 0 <= s < B:
                    act.wait_ge(s_wo, 3 * s + 2)
                    act.activation(wohi[:, s], wos[:], ACT.Copy).then_inc(s_wohi, 1)
                if isinstance(s, int) and s >= GROUPS - 2:
                    i = s - (GROUPS - 2)
                    if i < KD:
                        act.wait_ge(s_w1, 16)
                        act.activation(W1hi[:, i, :], W1raw[:, i, :], ACT.Copy).then_inc(s_w1hi, 1)
                    else:
                        half = slice((i - KD) * KF // 2, (i - KD + 1) * KF // 2)
                        act.wait_ge(s_w2, 16)
                        act.activation(W2hi[:, half, :], W2raw[:, half, :], ACT.Copy).then_inc(s_w2hi, 1)

            sweep(act, step)

            act.wait_ge(s_dl, 1)
            act.activation(rm["ex"][:], rm["dl"][:], ACT.Exp).then_inc(s_exp, 1)
            act.wait_ge(s_rc, 11)
            for n in range(J // JC):
                js = slice(n * JC, n * JC + JC)
                act.wait_ge(s_oh, 2 * n + 2)
                act.activation(ohcp[:, js, 0, :], oheq[:, js, :], ACT.Copy, scale=pcol[:, 0:1]).then_inc(s_ohp, 1)

            def rows_hi(e, c):
                _, _, n = CHUNKS[c]
                q = NCH * e + c
                act.wait_ge(s_tr, q + 1)
                need(act, s_w1ps, KF * (q - 1))
                for k in range(KD):
                    act.activation(hThi[c % 2][:, k, 0:n], psum[:, 6 + k, 0:n], ACT.Copy).then_inc(s_thi, 1)

            def expert(e, first, last):
                for c in range(NCH):
                    _, _, n = CHUNKS[c]
                    q = NCH * e + c
                    for m in range(KF):
                        act.wait_ge(s_w1ps, KF * q + m + 1)
                        need(act, s_glo, KF * q + m + 1 - NG)
                        hold(act)
                        act.activation(g32[m % NG][:, 0:n], psum[:, m % 4, 0:n], ACT.Gelu_apprx_tanh,
                                       bias=b1c[:, e, m:m + 1]).then_inc(s_gelu, 1)
                    if c == NCH - 1 and not last:
                        act.wait_ge(s_w1, 16 * (e + 2))
                        act.wait_ge(s_w1ps, KF * NCH * (e + 1))
                        for k in range(KD):
                            act.activation(W1hi[:, k, :], W1raw[:, k, :], ACT.Copy).then_inc(s_w1hi, 1)
                    if c + 1 < NCH:
                        rows_hi(e, c + 1)
                    elif not last:
                        rows_hi(e + 1, 0)
                    if c == 0 and not first:
                        act.wait_ge(s_w2, 16 * (e + 1))
                        act.wait_ge(s_w2ps, ET * e)
                        for k in range(2):
                            half = slice(k * KF // 2, (k + 1) * KF // 2)
                            act.activation(W2hi[:, half, :], W2raw[:, half, :], ACT.Copy).then_inc(s_w2hi, 1)

            act.wait_ge(s_idx, 1)
            rows_hi(0, 0)
            expert(0, True, False)
            with act.Fori(1, E - 1) as e:
                expert(e, False, False)
            expert(E - 1, False, True)

            def gate_y(g, r):
                act.wait_ge(s_yin[r], 32 * (g // 2 + 1))
                need(act, s_ys, NT * (g - 1))
                hold(act)
                for t in range(NT):
                    act.activation(yg[r][:, t, :], y0[r][:, t, :], ACT.Copy, scale=gate1[:, bass.ds(NT * g + t, 1)])\
                        .then_inc(s_yg, 1)

            def store(g, r):
                act.wait_ge(s_yo, g + 1)
                need(act, s_out[r], 16 * (g // 2))
                act.dma_start(out_t[:, bass.ds(NT * g, NT), :], yo[r][:]).then_inc(s_out[r], 16)

            gate_y(0, 0)
            gate_y(1, 1)
            store(0, 0)
            gate_y(2, 0)
            store(1, 1)
            gate_y(3, 1)
            with act.Fori(2, TILES // NT // 2) as i:
                store(2 * i - 2, 0)
                gate_y(2 * i, 0)
                store(2 * i - 1, 1)
                gate_y(2 * i + 1, 1)
            for g in (TILES // NT - 2, TILES // NT - 1):
                store(g, g % 2)
            for r in range(2):
                act.wait_ge(s_out[r], 16 * (TILES // NT // 2))

        @block.tensor
        def _(pe):
            pe.wait_ge(s_sct, 1)
            for n in range(1, 3):
                for k in range(KD):
                    mm = pe.matmul(psum[0:B, n, :], sct[:, k, :], wm[:, k, n * 512:(n + 1) * 512],
                                   start=(k == 0), stop=(k == KD - 1))
            mm.then_inc(s_modps, 1)
            for j in range(2):
                for m in range(KD):
                    for k in range(KD):
                        mm = pe.matmul(psum[:, 3, (j * KD + m) * B:(j * KD + m + 1) * B],
                                       wm[:, k, j * D + m * P:j * D + (m + 1) * P], sct[:, k, :],
                                       start=(k == 0), stop=(k == KD - 1))
            mm.then_inc(s_modcps, 1)
            pe.wait_ge(s_pc, 4)
            pe.wait_ge(s_modrow, 4)
            pe.wait_ge(s_modc, 2)

            def turn(dst, src, r):
                for k in range(KD):
                    for t in range(TG):
                        last = pe.transpose(dst[:, k, t * P:(t + 1) * P], src[:, t, k * P:(k + 1) * P], ident[:])
                return last

            def project(w, g, r, done, dst):
                for m in range(KD):
                    ms = slice(m * P, (m + 1) * P)
                    product(pe, dst[:, m, :], [(whi[:, w, k, ms], wlo[:, w, k, ms], hhi[r][:, k, :], hlo[r][:, k, :])
                                               for k in range(KD)], done if m == KD - 1 else None)

            def step(s, r):
                q = 1 - r
                g = s
                if has(g):
                    if isinstance(g, int) and g == 0:
                        pe.wait_ge(s_wlo, 3)
                    pe.wait_ge(s_hhi, g + 1)
                    pe.wait_ge(s_hlo, g + 1)
                    need(pe, s_state, KD * g)
                    project(1, g, r, s_v, bank(BV))
                    need(pe, s_y, g)
                    project(0, g, r, s_q, bank(BQ))
                g = s - 1
                if has(g):
                    pe.wait_ge(s_yn, TG * (g + 1))
                    need(pe, s_z, KD * g)
                    turn(bank(BN), yn[q], q).then_inc(s_ynT, 1)
                g = s
                if has(g):
                    need(pe, s_gate, g)
                    project(2, g, r, s_g, bank(BG))
                    pe.wait_ge(s_y, g + 1)
                    need(pe, s_yn, TG * g)
                    turn(bank(BY), ysb[r], r).then_inc(s_yT, 1)
                g = s + 1
                if has(g):
                    pe.wait_ge(s_xn, TG * (g + 1))
                    need(pe, s_h32, KD * g)
                    need(pe, s_lgs, g - 3)
                    turn(bank(BX), xn[q], q).then_inc(s_xT, 1)
                g = s - 2
                if has(g):
                    pe.wait_ge(s_h2, TG * (g + 1))
                    need(pe, s_h2Ts, g)
                    turn(bank(BH), h2[r], r).then_inc(s_h2T, 1)
                g = s - 1
                if has(g):
                    b = g // GPB
                    pe.wait_ge(s_zghi, g + 1)
                    pe.wait_ge(s_zglo, g + 1)
                    need(pe, s_x1, g)
                    if isinstance(g, int):
                        pe.wait_ge(s_wo, 3 * min(g // GPB + 1, B))
                    else:
                        pe.wait_ge(s_wo, 3 * B)
                    for t in range(TG):
                        ts = slice(t * P, (t + 1) * P)
                        product(pe, bank(BO)[:, t, :], [(zghi[q][:, k, ts], zglo[q][:, k, ts], wohi[:, b, k, :],
                                                         wolo[:, b, k, :]) for k in range(KD)],
                                s_o if t == TG - 1 else None)
                g = s - 2
                if has(g):
                    pe.wait_ge(s_h2Ts, g + 1)
                    need(pe, s_lgs, g)
                    pe.wait_ge(s_h32, KD * (min(g + 4, GROUPS) if isinstance(g, int) else g + 4))
                    for t in range(TG):
                        for k in range(KD):
                            mm = pe.matmul(psum[:, BX, t * E:(t + 1) * E], h2T[r][:, k, t * P:(t + 1) * P], rw[:, k, :],
                                           start=(k == 0), stop=(k == KD - 1))
                    mm.then_inc(s_lg, 1)

            sweep(pe, step)

            pe.wait_ge(s_ohd, 2)
            pe.wait_ge(s_rc, 11)
            ohf = OH[:].rearrange("p j e -> p (j e)")
            pe.matmul(psum[:, 0, :], before[:], ohf, start=True, stop=True).then_inc(s_cnt, 1)
            pe.matmul(psum[:, 1, :], onesb[:], ohf, start=True, stop=True).then_inc(s_cnt, 1)
            for n in range(J // JC):
                pe.wait_ge(s_oh, 2 * n + 2)
                pe.wait_ge(s_ohp, n + 1)
                pe.wait_ge(s_ohj, n + 1)
                for j in range(n * JC, n * JC + JC):
                    mm = pe.matmul(psum[:, 2, 0:2 * NC], ohlo[:, j, :], ohcp[:, j].rearrange("p a c -> p (a c)"),
                                   start=(j == 0), stop=(j == J - 1))
            mm.then_inc(s_slots, 1)

            def rows(e, c):
                t0, n, _ = CHUNKS[c]
                q = NCH * e + c
                pe.wait_ge(s_gat[c], 16 * n * (e + 1))
                need(pe, s_thi, KD * q)
                need(pe, s_tlo, KD * q)
                for k in range(KD):
                    for i in range(n):
                        tr = pe.transpose(psum[:, 6 + k, i * P:(i + 1) * P], xg[:, t0 + i, k * P:(k + 1) * P], ident[:])
                tr.then_inc(s_tr, 1)

            def up(e, c):
                _, _, n = CHUNKS[c]
                q, r = NCH * e + c, c % 2
                pe.wait_ge(s_thi, KD * (q + 1))
                pe.wait_ge(s_tlo, KD * (q + 1))
                pe.wait_ge(s_w1hi, KD * (e + 1))
                pe.wait_ge(s_w1lo, KD * (e + 1))
                for m in range(KF):
                    ms = slice(m * P, (m + 1) * P)
                    need(pe, s_gelu, KF * q + m + 1 - 4)
                    product(pe, psum[:, m % 4, 0:n], [(W1hi[:, k, ms], W1lo[:, k, ms], hThi[r][:, k, 0:n],
                                                       hTlo[r][:, k, 0:n]) for k in range(KD)], s_w1ps)

            def down(e, c):
                t0, nt, n = CHUNKS[c]
                q, r = NCH * e + c, c % 2
                pe.wait_ge(s_glo, KF * (q + 1))
                pe.wait_ge(s_w2hi, 2 * (e + 1))
                pe.wait_ge(s_w2lo, 2 * (e + 1))
                for i in range(nt):
                    T = ET * e + TILES_BEFORE[c] + i
                    cols = slice(i * P, min((i + 1) * P, n))
                    M = cols.stop - cols.start
                    need(pe, s_yb, T - 1)
                    product(pe, psum[0:M, 4 + (TILES_BEFORE[c] + i) % 2, 0:D],
                            [(ghi[r][:, m, cols], glo[r][:, m, cols], W2hi[:, m, :], W2lo[:, m, :])
                             for m in range(KF)], s_w2ps)

            def expert(e, first, last):
                for c in range(NCH):
                    up(e, c)
                    if c + 1 < NCH:
                        rows(e, c + 1)
                    elif not last:
                        rows(e + 1, 0)
                    if c > 0:
                        down(e, c - 1)
                    elif not first:
                        down(e - 1, NCH - 1)

            pe.wait_ge(s_idx, 1)
            rows(0, 0)
            expert(0, True, False)
            with pe.Fori(1, E - 1) as e:
                expert(e, False, False)
            expert(E - 1, False, True)
            down(E - 1, NCH - 1)

        @block.vector
        def _(v):
            v.wait_ge(s_modps, 1)
            for j, n in ((0, 1), (3, 2)):
                src = psum[0:B, n, 0:D] if j == 0 else psum[0:B, n, D:2 * D]
                i = 0 if j == 0 else 1
                v.tensor_copy(modraw[:, i, :], src).then_inc(s_modt, 1)
                v.tensor_scalar(sgn[:, i, :], src, 0.0, 2.0, ALU.is_ge, ALU.mult).then_inc(s_modt, 1)
            v.tensor_copy(modr[:, 1, :], psum[0:B, 1, D:2 * D]).then_inc(s_modrow, 1)
            v.tensor_scalar(modr[:, 2, :], psum[0:B, 2, 0:D], 1.0, None, ALU.add).then_inc(s_modrow, 1)
            v.wait_ge(s_modt, 4)
            v.scalar_tensor_tensor(out=mag[:], in0=modraw[:], scalar=-1.0, in1=modraw[:], op0=ALU.mult, op1=ALU.max)\
                .then_inc(s_modt, 1)
            v.wait_ge(s_modt, 5)
            v.tensor_scalar(mag[:], mag[:], 0.25, None, ALU.max).then_inc(s_modt, 1)
            v.wait_ge(s_modt, 6)
            for i, j in ((0, 0), (1, 3)):
                v.scalar_tensor_tensor(out=modr[:, j, :], in0=sgn[:, i, :], scalar=1.0, in1=mag[:, i, :],
                                       op0=ALU.subtract, op1=ALU.mult).then_inc(s_modrow, 1)
            v.wait_ge(s_modcps, 1)
            mc = psum[:, 3, 0:2 * KD * B].rearrange("p (j m b) -> p j m b", j=2, m=KD)
            v.tensor_copy(modc[:, 0], mc[:, 0]).then_inc(s_modc, 1)
            v.tensor_scalar(modc[:, 1], mc[:, 1], 1.0, None, ALU.add).then_inc(s_modc, 1)
            for w in range(3):
                v.wait_ge(s_whi, w + 1)
                v.tensor_tensor(wlo[:, w], wraw[:, w], f32(whi[:, w]), ALU.subtract).then_inc(s_wlo, 1)

            def step(s, r):
                q = 1 - r
                g = s
                if has(g):
                    v.wait_ge(s_v, g + 1)
                    need(v, s_state, KD * g)
                    if isinstance(g, int) and g == 0:
                        v.wait_ge(s_lamt, KD)
                        v.wait_ge(s_pc, 4)
                    for k in range(KD):
                        if r == 1:
                            init = state[:, k, GT - 1:GT]
                        else:
                            new = (g // 2) % (GPB // 2)
                            if isinstance(g, int):
                                at = 2 * GT - min(new, 1)
                            else:
                                at = 2 * GT - new
                            init = state[:, k, bass.ds(at, 1)]
                        v.tensor_tensor_scan(state[:, k, r * GT:(r + 1) * GT], lamt[:, k, :], bank(BV)[:, k, :],
                                             init, ALU.mult, ALU.add).then_inc(s_state, 1)
                    v.wait_ge(s_q, g + 1)
                    v.wait_ge(s_state, KD * (g + 1))
                    need(v, s_yT, g - 1)
                    v.tensor_tensor(ysb[r][:], bank(BQ), state[:, :, r * GT:(r + 1) * GT], ALU.mult).then_inc(s_y, 1)
                g = s - 1
                if has(g):
                    v.wait_ge(s_z, KD * (g + 1))
                    v.wait_ge(s_gate, g + 1)
                    need(v, s_zghi, g - 1)
                    v.tensor_tensor(zg[q][:], z[q][:], gate[q][:], ALU.mult).then_inc(s_zg, 1)
                    v.wait_ge(s_zghi, g + 1)
                    need(v, s_o, g - 1)
                    v.tensor_tensor(zglo[q][:], zg[q][:], f32(zghi[q][:]), ALU.subtract).then_inc(s_zglo, 1)
                g = s
                if has(g):
                    v.wait_ge(s_yT, g + 1)
                    stats(v, "y", g, r, [bank(BY)[:, t, :] for t in range(TG)])
                g = s + 1
                if has(g):
                    v.wait_ge(s_hhi, g + 1)
                    need(v, s_g, g - 1)
                    v.tensor_tensor(hlo[q][:], h32[q][:], f32(hhi[q][:]), ALU.subtract).then_inc(s_hlo, 1)
                g = s - 1
                if has(g):
                    v.wait_ge(s_o, g + 1)
                    need(v, s_x1c, g - 1)
                    v.tensor_tensor(x1[q][:], X[:, bass.ds(TG * g, TG), :], bank(BO), ALU.add).then_inc(s_x1, 1)
                    v.wait_ge(s_x1, g + 1)
                    stats(v, "h", g, q, [x1[q][:, t, :] for t in range(TG)])
                g = s - 2
                if has(g):
                    v.wait_ge(s_lg, g + 1)
                    v.tensor_tensor(LG[:, bass.ds(TG * g, TG), :],
                                    psum[:, BX, 0:TG * E].rearrange("p (t e) -> p t e", t=TG),
                                    rb[:].unsqueeze(1).broadcast_to([P, TG, E]), ALU.add).then_inc(s_lgs, 1)
                g = s + 2
                if has(g):
                    v.wait_ge(s_x, 16 * (TG * g // 4 + 1))
                    stats(v, "x", g, r, [X[:, TG * g + t, :] for t in range(TG)])

            sweep(v, step)

            chain = [0]

            def link(ins):
                ins.then_inc(s_rv, 1)
                chain[0] += 1
                v.wait_ge(s_rv, chain[0])

            def over_e(ap):
                return ap.unsqueeze(2).broadcast_to([P, ap.shape[1], E])

            v.wait_ge(s_lgs, GROUPS)
            for r in range(2):
                v.wait_ge(s_h2out[r], 16 * (GROUPS // 2))
            v.wait_ge(s_zero, 16)
            v.wait_ge(s_w2lo, 2)
            v.wait_ge(s_h2Ts, GROUPS)
            link(v.tensor_reduce(rm["m1"][:], LG[:], AX_X, ALU.max))
            v.wait_ge(s_rc, 11)
            for n, lg in (("1", LG[:]), ("2", rt["lg2"][:])):
                if n == "2":
                    link(v.scalar_tensor_tensor(out=rt["lg2"][:], in0=rt["oh1"][:], scalar=NEG, in1=LG[:],
                                                op0=ALU.mult, op1=ALU.add))
                    link(v.tensor_reduce(rm["m2"][:], rt["lg2"][:], AX_X, ALU.max))
                    v.tensor_tensor(rm["dl"][:], rm["m2"][:], rm["m1"][:], ALU.subtract).then_inc(s_dl, 1)
                link(v.tensor_tensor(rt["eq" + n][:], lg, over_e(rm["m" + n][:]), ALU.is_equal))
                link(v.tensor_tensor(rt["sc" + n][:], rt["eq" + n][:], erank[:].unsqueeze(1).broadcast_to([P, TILES, E]),
                                     ALU.mult))
                link(v.tensor_reduce(rm["i" + n][:], rt["sc" + n][:], AX_X, ALU.max))
                link(v.tensor_tensor(rt["oh" + n][:], rt["sc" + n][:], over_e(rm["i" + n][:]), ALU.is_equal))
                k = int(n) - 1
                v.tensor_copy(OH[:, k * TILES:(k + 1) * TILES, :], rt["oh" + n][:]).then_inc(s_ohd, 1)
            v.wait_ge(s_ohd, 2)
            link(v.tensor_tensor(ohe[:], OH[:], eio[:].unsqueeze(1).broadcast_to([P, J, E]), ALU.mult))
            link(v.tensor_reduce(e10[:], ohe[:], AX_X, ALU.add))
            v.wait_ge(s_exp, 1)
            link(v.tensor_scalar(rm["se"][:], rm["ex"][:], 1.0, None, ALU.add))
            link(v.reciprocal(gate1[:], rm["se"][:]))
            link(v.tensor_tensor(gate2[:], rm["ex"][:], gate1[:], ALU.mult))
            v.wait_ge(s_cnt, 2)
            tot = psum[:, 1, :].rearrange("p (j e) -> p j e", e=E)
            for e in range(E):
                v.tensor_tensor_scan(csum[:, :, e], onesj[:], tot[:, :, e], 0.0, ALU.mult, ALU.add).then_inc(s_cs, 1)
            v.wait_ge(s_cs, E)
            link(v.tensor_tensor(posa[:], psum[:, 0, :].rearrange("p (j e) -> p j e", e=E), csum[:], ALU.add))
            link(v.tensor_tensor(posb[:], posa[:], tot, ALU.subtract))
            link(v.tensor_tensor(posc[:], posb[:], OH[:], ALU.mult))
            link(v.tensor_reduce(pos[:], posc[:], AX_X, ALU.add))
            link(v.tensor_copy(posi[:], pos[:]))
            link(v.tensor_scalar(hii[:], posi[:], 7, None, ALU.arith_shift_right))
            link(v.tensor_scalar(loi[:], posi[:], P - 1, None, ALU.bitwise_and))
            link(v.tensor_copy(hif[:], hii[:]))
            link(v.tensor_copy(lof[:], loi[:]))
            link(v.tensor_scalar(kept[:], pos[:], float(CAP), -4.0 * NC, ALU.is_lt, ALU.mult))
            link(v.tensor_tensor(colf[:], hif[:], e10[:], ALU.add))
            link(v.tensor_tensor(coff[:], colf[:], kept[:], ALU.add))
            link(v.tensor_scalar(col[:], coff[:], 4.0 * NC, None, ALU.add))
            for n in range(J // JC):
                js = slice(n * JC, n * JC + JC)
                v.tensor_tensor(oheq[:, js, :], io[:, 0:NC].unsqueeze(1).broadcast_to([P, JC, NC]),
                                col[:, js].unsqueeze(2).broadcast_to([P, JC, NC]), ALU.is_equal).then_inc(s_oh, 1)
                v.tensor_tensor(ohlo[:, js, :], io[:].unsqueeze(1).broadcast_to([P, JC, P]),
                                lof[:, js].unsqueeze(2).broadcast_to([P, JC, P]), ALU.is_equal).then_inc(s_oh, 1)
            v.wait_ge(s_slots, 1)
            link(v.tensor_copy(tabp[:], psum[:, 2, 0:2 * NC]))
            link(v.tensor_scalar(tabj[:], tabp[:, NC:2 * NC], -1.0, float(P), ALU.add, ALU.mult))
            link(v.tensor_tensor(tabv[:], tabj[:], tabp[:, 0:NC], ALU.add))
            link(v.tensor_copy(tabi[:], tabv[:]))
            link(v.tensor_scalar(gidx[:].rearrange("p e t -> p (e t)"), tabi[:], TOKENS - 1, None, ALU.bitwise_and))
            link(v.tensor_scalar(tabe[:], tabp[:, NC:2 * NC], 0.5, 4.0 * TOKENS, ALU.is_lt, ALU.mult))
            link(v.tensor_tensor(tabs[:], tabv[:], tabe[:], ALU.add))
            v.tensor_copy(sidx[:].rearrange("p e t -> p (e t)"), tabs[:]).then_inc(s_idx, 1)

            def rows_lo(e, c):
                _, _, n = CHUNKS[c]
                q = NCH * e + c
                v.wait_ge(s_thi, KD * (q + 1))
                need(v, s_w1ps, KF * (q - 1))
                for k in range(KD):
                    v.tensor_tensor(hTlo[c % 2][:, k, 0:n], psum[:, 6 + k, 0:n], f32(hThi[c % 2][:, k, 0:n]),
                                    ALU.subtract).then_inc(s_tlo, 1)

            def outputs(e, c):
                t0, nt, n = CHUNKS[c]
                need(v, s_sca[c], 16 * nt * e)
                for i in range(nt):
                    T = ET * e + TILES_BEFORE[c] + i
                    M = min(P, n - i * P)
                    v.wait_ge(s_w2ps, T + 1)
                    v.tensor_tensor(yb[0:M, t0 + i, :], psum[0:M, 4 + (TILES_BEFORE[c] + i) % 2, 0:D], b2r[0:M, e, :],
                                    ALU.add).then_inc(s_yb, 1)

            def expert(e, first, last):
                for c in range(NCH):
                    _, _, n = CHUNKS[c]
                    q, r = NCH * e + c, c % 2
                    need(v, s_w2ps, ET * e + TILES_BEFORE[c - 1] if c >= 1 else ET * (e - 1) + TILES_BEFORE[NCH - 1])
                    for m in range(KF):
                        v.wait_ge(s_gelu, KF * q + m + 1)
                        v.tensor_copy(ghi[r][:, m, 0:n], g32[m % NG][:, 0:n]).then_inc(s_ghi, 1)
                        v.wait_ge(s_ghi, KF * q + m + 1)
                        v.tensor_tensor(glo[r][:, m, 0:n], g32[m % NG][:, 0:n], f32(ghi[r][:, m, 0:n]), ALU.subtract)\
                            .then_inc(s_glo, 1)
                    if c == NCH - 1 and not last:
                        for k in range(KD):
                            v.wait_ge(s_w1hi, KD * (e + 1) + k + 1)
                            v.tensor_tensor(W1lo[:, k, :], W1raw[:, k, :], f32(W1hi[:, k, :]), ALU.subtract)\
                                .then_inc(s_w1lo, 1)
                    if c + 1 < NCH:
                        rows_lo(e, c + 1)
                    elif not last:
                        rows_lo(e + 1, 0)
                    if c > 0:
                        outputs(e, c - 1)
                    elif not first:
                        outputs(e - 1, NCH - 1)
                    if c == 0 and not first:
                        for k in range(2):
                            half = slice(k * KF // 2, (k + 1) * KF // 2)
                            v.wait_ge(s_w2hi, 2 * e + k + 1)
                            v.tensor_tensor(W2lo[:, half, :], W2raw[:, half, :], f32(W2hi[:, half, :]), ALU.subtract)\
                                .then_inc(s_w2lo, 1)

            v.wait_ge(s_idx, 1)
            v.wait_ge(s_ybz, 1)
            v.wait_ge(s_b2, 16)
            rows_lo(0, 0)
            expert(0, True, False)
            expert(1, False, False)
            with v.Fori(2, E - 1) as e:
                expert(e, False, False)
            expert(E - 1, False, True)
            outputs(E - 1, NCH - 1)

            def add_y(g, r):
                v.wait_ge(s_yin[r], 32 * (g // 2 + 1))
                need(v, s_yw, g - 1)
                for t in range(NT):
                    v.wait_ge(s_yg, NT * g + t + 1)
                    v.scalar_tensor_tensor(out=ys[r][:, t, :], in0=y1[r][:, t, :], scalar=gate2[:, bass.ds(NT * g + t, 1)],
                                           in1=yg[r][:, t, :], op0=ALU.mult, op1=ALU.add).then_inc(s_ys, 1)

            def finish(g, r):
                v.wait_ge(s_yw, g + 1)
                need(v, s_out[r], 16 * (g // 2))
                v.tensor_tensor(yo[r][:], yw[r][:], X[:, bass.ds(NT * g, NT), :], ALU.add).then_inc(s_yo, 1)

            add_y(0, 0)
            add_y(1, 1)
            finish(0, 0)
            add_y(2, 0)
            finish(1, 1)
            add_y(3, 1)
            with v.Fori(2, TILES // NT // 2) as i:
                finish(2 * i - 2, 0)
                add_y(2 * i, 0)
                finish(2 * i - 1, 1)
                add_y(2 * i + 1, 1)
            for g in (TILES // NT - 2, TILES // NT - 1):
                finish(g, g % 2)


def kernel(**inputs):
    import numpy as _np
    import concourse.bacc as _bacc
    from concourse import mybir as _mybir
    from concourse.bass_utils import run_bass_kernel_spmd as _run

    a = {k: _np.asarray(v) for k, v in inputs.items()}
    D = a["L0_attn_x"].shape[-1]
    K = D // P

    def rows_by_chunk(m):
        return m.reshape(K, P, -1).transpose(1, 0, 2)

    heads = a["L0_attn_beta"].shape[0]
    E, F = a["L0_ffn_b1"].shape
    arrays = {
        "x": a["L0_attn_x"],
        "attn_wT": _np.stack([rows_by_chunk(a["L0_attn_W" + n].T) for n in "qvgo"], axis=1),
        "ln_gamma": a["L0_attn_ln_gamma"].reshape(K, P).T,
        "ln_beta": a["L0_attn_ln_beta"].reshape(K, P).T,
        "beta_ch": _np.repeat(a["L0_attn_beta"], D // heads).reshape(K, P).T,
        "router_w": rows_by_chunk(a["L0_ffn_Wg"]),
        "router_b": a["L0_ffn_bg"],
        "w1": a["L0_ffn_W1"],
        "b1": a["L0_ffn_b1"].reshape(E, F // P, P).transpose(2, 0, 1),
        "w2": a["L0_ffn_W2"],
        "b2": a["L0_ffn_b2"],
        "cT": rows_by_chunk(a["L0_c"].T),
        "wmod": a["L0_wmod"],
    }
    nc = _bacc.Bacc("TRN2", target_bir_lowering=False, num_devices=1)
    args = {}
    for name in arrays:
        arrays[name] = _np.ascontiguousarray(arrays[name])
        args[name] = nc.dram_tensor(name, arrays[name].shape, _mybir.dt.from_np(arrays[name].dtype),
                                    kind="ExternalInput").ap()
    out = nc.dram_tensor("out", a["L0_attn_x"].shape, F32, kind="ExternalOutput").ap()
    adaln_block(nc, out=out, **args)
    r = _run(nc, [arrays], core_ids=[0])
    return r.results[0]["out"]
```

```python
from contextlib import ExitStack

import concourse.bass as bass
from concourse import mybir

F32 = mybir.dt.float32
F32R = mybir.dt.float32r
BF16 = mybir.dt.bfloat16
I32 = mybir.dt.int32
U32 = mybir.dt.uint32
ALU = mybir.AluOpType
ACT = mybir.ActivationFunctionType
AX_X = mybir.AxisListType.X

P = 128


def adaln_block(nc, x, attn_wT, ln_gamma, ln_beta, beta_ch, router_w, router_b, w1, b1, w2, b2, cT, wmod, out):
    B, S, D = x.shape
    E, _, F = w1.shape
    TOKENS = B * S
    KD = D // P
    KF = F // P
    TILES = TOKENS // P
    TG = 2
    GT = TG * P
    GROUPS = TILES // TG
    GPB = S // GT
    XFIRST = 8
    EPS = 1e-5
    TOPK = 2
    CAP = -((-12 * TOKENS * TOPK) // (10 * E))
    ET = -(-CAP // P)
    J = TOPK * TILES
    LAST_COLS = CAP + CAP % 2 - (ET - 1) * P
    CHUNKS = [(0, 2, 2 * P), (2, 3, 3 * P), (5, 2, 2 * P), (7, 3, 2 * P + LAST_COLS)]
    NCH = len(CHUNKS)
    SPARE = NCH - 1
    TILES_BEFORE = [sum(n for _, n, _ in CHUNKS[:c]) for c in range(NCH + 1)]
    assert TILES_BEFORE[-1] == ET
    MAXC = [max(CHUNKS[c][2] for c in range(NCH) if c % 2 == r) for r in range(2)]
    NEG = -3.0e38

    x_t = x.rearrange("b (t p) d -> p (b t) d", p=P)
    DR = 2 * D + 2
    rows_dram = nc.dram_tensor("token_rows", [TOKENS, DR], F32, kind="Internal").ap()
    acc_dram = nc.dram_tensor("acc_rows", [TOKENS + ET * P, D], F32, kind="Internal").ap()
    mod_dram = nc.dram_tensor("mod_rows", [B, 4 * D], F32, kind="Internal").ap()
    rows_t = rows_dram.rearrange("(t p) d -> p t d", p=P)
    acc_t = acc_dram.rearrange("(t p) d -> p t d", p=P)

    keep = ExitStack()
    with keep:
        def sem(name):
            return keep.enter_context(nc.semaphore(name))

        def sb(name, shape, dt=F32, stack=keep):
            return stack.enter_context(nc.sbuf_tensor(name, shape, dt))

        psum = keep.enter_context(nc.psum_tensor("psum", [P, 8, 512], F32))

        X = sb("X", [P, TILES, D])
        LG = sb("LG", [P, TILES, E])
        gates = sb("gates", [P, TILES, TOPK])
        GB = sb("GB", [P, B, D])
        W1raw = sb("W1raw", [P, KD, F])
        W2raw = sb("W2raw", [P, KF, D])
        b1c = sb("b1c", [P, E, KF])
        b2r = sb("b2r", [P, E, D])
        ident = sb("ident", [P, P])
        load = sb("load", [P, E], I32)
        choice = sb("choice", [P, E, ET, TOPK])
        gidx = sb("gidx", [P, E, ET], I32)
        sidx = sb("sidx", [P, E, ET], I32)

        NC = E * ET
        onesj = sb("onesj", [P, J], F32)
        ioi = sb("ioi", [P, P], I32)
        io = sb("io", [P, P], F32)
        eio = sb("eio", [P, E], F32)
        erank = sb("erank", [P, E], F32)
        pci = sb("pci", [P, 1], I32)
        pcol = sb("pcol", [P, 1], F32)
        jp1 = sb("jp1", [P, J], F32)
        before = sb("before", [P, P], BF16)
        onesb = sb("onesb", [P, P], BF16)
        sparei = sb("sparei", [P, NC], I32)
        spare = sb("spare", [P, NC])

        early = ExitStack()
        wraw = sb("wraw", [P, 4, KD, D], F32, early)
        wos = sb("wos", [P, KD, D], F32, early)
        wm = sb("wm", [P, KD, 6 * D], F32, early)
        modr = sb("modr", [B, 4, D], F32, early)
        mag = sb("mag", [B, 2, D], F32, early)
        modraw = sb("modraw", [B, 2, D], F32, early)
        sgn = sb("sgn", [B, 2, D], F32, early)
        early.close()

        W1hi = sb("W1hi", [P, KD, F], F32R)
        W1lo = sb("W1lo", [P, KD, F], F32R)
        W2hi = sb("W2hi", [P, KF, D], F32R)
        W2lo = sb("W2lo", [P, KF, D], F32R)

        sa_ = ExitStack()
        zeros = sb("zeros", [P, 256], F32, sa_)
        ct = sb("ct", [P, KD, B], F32, sa_)
        sct = sb("sct", [P, KD, B], F32, sa_)
        lamraw = sb("lamraw", [P, KD], F32, sa_)
        whi = sb("whi", [P, 3, KD, D], F32R, sa_)
        wlo = sb("wlo", [P, 3, KD, D], F32R, sa_)
        wohi = sb("wohi", [P, B, KD, D], F32R, sa_)
        wolo = sb("wolo", [P, B, KD, D], F32R, sa_)
        MB = sb("MB", [P, B, 3, D], F32, sa_)
        modc = sb("modc", [P, 2, KD, B], F32, sa_)
        gcol = sb("gcol", [P, KD], F32, sa_)
        bcol = sb("bcol", [P, KD], F32, sa_)
        go = sb("go", [P, 1], F32, sa_)
        lam = sb("lam", [P, KD], F32, sa_)
        lamt = sb("lamt", [P, KD, GT], F32, sa_)
        neghalf = sb("neghalf", [P, 2, TG], F32, sa_)
        rw = sb("rw", [P, KD, E], F32, sa_)
        rb = sb("rb", [P, E], F32, sa_)
        state = sb("state", [P, KD, 2 * GT + 1], F32, sa_)

        def two(name, shape, dt=F32):
            return [sb(f"{name}{r}", shape, dt, sa_) for r in range(2)]

        st = {n: two(f"st_{n}", [P, TG, 6]) for n in "xyh"}
        mvs = {n: two(f"mv_{n}", [P, len(n), TG, 2]) for n in ("xy", "h")}
        ves = {n: two(f"ve_{n}", [P, len(n), TG]) for n in ("xy", "h")}
        nms = {n: two(f"nm_{n}", [P, len(n), TG]) for n in ("xy", "h")}
        rss = {n: two(f"rs_{n}", [P, len(n), TG]) for n in ("xy", "h")}
        nrs = {"xy": two("nr_xy", [P, 2, TG])}

        def of(tiles, n, r):
            return tiles["h" if n == "h" else "xy"][r][:, 1 if n == "y" else 0]
        xn = two("xn", [P, TG, D])
        h32 = two("h32_", [P, KD, GT])
        hhi = two("hhi", [P, KD, GT], F32R)
        hlo = two("hlo", [P, KD, GT], F32R)
        ysb = two("ysb", [P, KD, GT])
        gate = two("gate_", [P, KD, GT])
        yn = two("yn", [P, TG, D])
        z = two("z", [P, KD, GT])
        zg = two("zg", [P, KD, GT])
        zghi = two("zghi", [P, KD, GT], F32R)
        zglo = two("zglo", [P, KD, GT], F32R)
        xn2 = two("xn2_", [P, TG, D])
        x1 = two("x1_", [P, TG, D])
        h2 = two("h2_", [P, TG, D])
        h2T = two("h2T", [P, KD, GT])
        sa_.close()


        sr = ExitStack()
        rt = {n: sb(f"rt_{n}", [P, TILES, E], F32, sr) for n in ("eq1", "sc1", "oh1", "lg2", "eq2", "sc2", "oh2")}
        rm = {n: sb(f"rm_{n}", [P, TILES], F32, sr) for n in ("m1", "i1", "m2", "i2", "dl", "ex", "se")}
        OH = sb("OH", [P, J, E], BF16, sr)
        csum = sb("csum", [P, J, E], F32, sr)
        posa = sb("posa", [P, J, E], F32, sr)
        posb = sb("posb", [P, J, E], F32, sr)
        posc = sb("posc", [P, J, E], F32, sr)
        ohe = sb("ohe", [P, J, E], F32, sr)
        pos = sb("pos", [P, J], F32, sr)
        e10 = sb("e10", [P, J], F32, sr)
        kept = sb("kept", [P, J], F32, sr)
        posi = sb("posi", [P, J], I32, sr)
        hii = sb("hii", [P, J], I32, sr)
        loi = sb("loi", [P, J], I32, sr)
        lof = sb("lof", [P, J], F32, sr)
        hif = sb("hif", [P, J], F32, sr)
        colf = sb("colf", [P, J], F32, sr)
        coff = sb("coff", [P, J], F32, sr)
        col = sb("col", [P, J], F32, sr)
        JC = 16
        ohlo = sb("ohlo", [P, J, P], BF16, sr)
        oheq = sb("oheq", [P, J, NC], BF16, sr)
        ohcp = sb("ohcp", [P, J, 2, NC], BF16, sr)
        tabp = sb("tabp", [P, 2 * NC], F32, sr)
        tabj, tabv, tabe, tabo, tabg, tabs = (sb(n, [P, NC], F32, sr) for n in (
            "tabj", "tabv", "tabe", "tabo", "tabg", "tabs"))
        tabi = sb("tabi", [P, NC], I32, sr)
        sr.close()

        sf = ExitStack()
        xg = sb("xg", [P, ET, DR], F32, sf)
        hThi = [sb(f"hThi{r}", [P, KD, MAXC[r]], F32R, sf) for r in range(2)]
        hTlo = [sb(f"hTlo{r}", [P, KD, MAXC[r]], F32R, sf) for r in range(2)]
        ghi = [sb(f"ghi{r}", [P, KF, MAXC[r]], F32R, sf) for r in range(2)]
        glo = [sb(f"glo{r}", [P, KF, MAXC[r]], F32R, sf) for r in range(2)]
        NG = 4
        g32 = [sb(f"g32_{r}", [P, max(MAXC)], F32, sf) for r in range(NG)]
        yu = [sb(f"yu{r}", [P, D], F32, sf) for r in range(2)]
        yb = sb("yb", [P, ET, D], F32, sf)
        gp = sb("gp", [P, ET, TOPK], F32, sf)
        gs = sb("gs", [P, ET], F32, sf)
        left_out = [sb(f"left_out{n}", [P, 1], F32, sf) for n in range(3)]
        gcur = sb("gcur", [P, ET], I32, sf)
        scur = sb("scur", [P, ET], I32, sf)
        sf.close()

        s_x = [sem(f"x_in{r}") for r in range(2)]
        s_attnw = sem("attn_weights_in")
        s_mod_in = sem("mod_inputs_in")
        s_modrest_in = sem("mod_rest_in")
        s_beta = sem("beta_in")
        s_small = sem("small_inputs_in")
        s_modout = sem("mod_rows_out")
        s_mb = sem("mod_broadcast_in")
        s_w1 = sem("w1_in")
        s_w2 = sem("w2_in")
        s_b2 = sem("b2_in")
        s_zero = sem("spare_rows_zeroed")
        s_gbout = sem("gb_rows_out")
        s_gateout = sem("gates_out")
        s_h2out = [sem(f"h2_out{r}") for r in range(2)]
        s_x1c = [sem(f"x1_out{r}") for r in range(2)]
        s_gat = [sem(f"gathered{c}") for c in range(NCH)]
        s_sca = [sem(f"scattered{c}") for c in range(NCH)]
        s_out = sem("out")
        (s_pc, s_sct, s_modps, s_modcps, s_modrow, s_modc, s_lam, s_lamt, s_whi, s_wlo, s_wo, s_wohi, s_zeros,
         s_w1hi, s_w1lo, s_w2hi, s_w2lo) = (sem(n) for n in (
            "pool_constants", "silu_c", "mod_rows_psum", "mod_cols_psum", "mod_rows", "mod_cols", "decay", "decay_tile",
            "attn_w_hi", "attn_w_lo", "wo_scaled_lo", "wo_hi", "zero_tile", "w1_hi", "w1_lo", "w2_hi", "w2_lo"))
        s_st = {n: sem(f"stats_{n}") for n in "xyh"}
        s_mv = {n: sem(f"meanvar_{n}") for n in "xyh"}
        s_rs = {n: sem(f"rstd_{n}") for n in ("xy", "h")}
        (s_xn, s_xT, s_h32, s_hhi, s_hlo, s_v, s_q, s_g, s_state, s_y, s_gate, s_yT, s_yn, s_ynT, s_z, s_zg, s_zghi,
         s_zglo, s_o, s_x1, s_xn2, s_h2m, s_h2, s_h2T, s_h2Ts, s_lg, s_lgs) = (sem(n) for n in (
            "xn", "xT", "h32", "h_hi", "h_lo", "v_psum", "q_psum", "g_psum", "state", "y", "gate", "yT", "yn", "ynT",
            "z", "zg", "zg_hi", "zg_lo", "o_psum", "x1", "xn2", "h2_scaled", "h2", "h2T_psum", "h2T", "logits_psum",
            "logits"))
        s_go = sem("constants_ready")
        s_tick = sem("waits_held")
        s_modt, s_rc, s_dl, s_ohd, s_cs, s_ybz = (sem(n) for n in (
            "mod_parts", "routing_constants", "logit_delta", "chosen_experts", "tile_sums", "y_tile_cleared"))
        (s_rv, s_exp, s_cnt, s_oh, s_ohp, s_ohj, s_slots, s_idx) = (sem(n) for n in (
            "routing_steps", "exp_delta", "counts_psum", "onehots", "onehots_p", "onehots_j", "slots_psum", "index_tables"))
        (s_tr, s_thi, s_tlo, s_w1ps, s_gelu, s_ghi, s_glo, s_w2ps, s_yb, s_gcur, s_scur) = (sem(n) for n in (
            "rowsT_psum", "rowsT_hi", "rowsT_lo", "w1_psum", "gelu", "gelu_hi", "gelu_lo", "w2_psum", "y_tile",
            "gather_indices", "scatter_indices"))
        s_gates, s_gp, s_gs, s_yu = (sem(n) for n in ("gates", "slot_gate_parts", "slot_gates", "y_with_b2"))

        def need(eng, s, count):
            if not isinstance(count, int) or count > 0:
                eng.wait_ge(s, count)

        def hold(eng):
            eng.sem_inc(s_tick, 1)

        def load_of(eng, e):
            return eng.value_load(load[0:1, bass.ds(e, 1)], min_val=0, max_val=TOPK * TOKENS)

        def f32(ap):
            return ap.bitcast(F32)

        def product(eng, dst, terms, done=None):
            n = len(terms)
            for i, (lh, ll, rh, rl) in enumerate(terms):
                eng.matmul(dst, lh, rh, start=(i == 0), stop=False)
                eng.matmul(dst, lh, rl, start=False, stop=False)
                mm = eng.matmul(dst, ll, rh, start=False, stop=(i == n - 1))
            if done is not None:
                mm.then_inc(done, 1)

        def sweep(eng, step):
            for s in range(-2, 4):
                step(s, s % 2)
            with eng.Fori(2, GROUPS // 2 - 1) as i:
                step(2 * i, 0)
                step(2 * i + 1, 1)
            for s in range(GROUPS - 2, GROUPS + 3):
                step(s, s % 2)

        def has(g):
            return not isinstance(g, int) or 0 <= g < GROUPS

        def stats(eng, n, g, r, src):
            hold(eng)
            for t in range(TG):
                eng.bn_stats(st[n][r][:, t, :], src[t]).then_inc(s_st[n], 1)
            eng.wait_ge(s_st[n], TG * g + TG)
            if n == "h":
                need(eng, s_rs["h"], 3 * (g - 1))
            else:
                need(eng, s_rs["xy"], scaled_x(g - 2) if n == "x" else scaled_y(g - 2))
            hold(eng)
            for t in range(TG):
                eng.bn_aggr(of(mvs, n, r)[:, t, :], st[n][r][:, t, :]).then_inc(s_mv[n], 1)

        def scaled_x(g):
            return 4 * (g + 1)

        def scaled_y(g):
            return 4 * (g + 3)

        def rstd(eng, n, r, kinds, done):
            mv, ve, nm, rs = (tiles[n][r][:, kinds] for tiles in (mvs, ves, nms, rss))
            eng.tensor_scalar(ve, mv[:, :, :, 1], EPS, None, ALU.add).then_inc(s_rs[n], 1)
            eng.tensor_scalar(nm, mv[:, :, :, 0], -1.0, None, ALU.mult).then_inc(s_rs[n], 1)
            eng.wait_ge(s_rs[n], done + 2)
            eng.tensor_tensor(rs, ve, neghalf[:, kinds], ALU.pow).then_inc(s_rs[n], 1)
            if n == "xy":
                eng.wait_ge(s_rs[n], done + 3)
                eng.tensor_tensor(nrs[n][r][:, kinds], nm, rs, ALU.mult).then_inc(s_rs[n], 1)

        BX, BV, BQ, BG, BY, BN, BO, BH = range(8)

        def bank(b):
            return psum[:, b, :].rearrange("p (k n) -> p k n", k=2)

        block = keep.enter_context(nc.Block())

        @block.sync
        def _(sp):
            def load_x(g, r):
                need(sp, s_x[r], 16 * (g // 2))
                sp.dma_start(X[:, bass.ds(TG * g, TG), :], x_t[:, bass.ds(TG * g, TG), :]).then_inc(s_x[r], 16)

            load_x(0, 0)
            load_x(1, 1)
            sp.dma_start(wraw[:], attn_wT).then_inc(s_attnw, 16)
            for dst, src in ((gcol, ln_gamma), (bcol, ln_beta), (rw, router_w), (rb, router_b.partition_broadcast(P)),
                             (b1c, b1)):
                sp.dma_start(dst[:], src).then_inc(s_small, 16)
            for g in range(2, XFIRST):
                load_x(g, g % 2)
            sp.wait_ge(s_modrow, 4)
            sp.dma_start(mod_dram, modr[:].rearrange("b j d -> b (j d)")).then_inc(s_modout, 16)
            sp.wait_ge(s_modout, 16)
            mod_rows = mod_dram.rearrange("b (j d) -> b j d", j=4)
            sp.dma_start(MB[:], mod_rows[:, 0:3, :].partition_broadcast(P)).then_inc(s_mb, 16)
            sp.dma_start(GB[:], mod_rows[:, 3, :].partition_broadcast(P)).then_inc(s_mb, 16)
            with sp.Fori(XFIRST // 2, GROUPS // 2) as i:
                load_x(2 * i, 0)
                load_x(2 * i + 1, 1)
            sp.wait_ge(s_zeros, 1)
            sp.dma_start(acc_t[:, TILES:, :], zeros[:].unsqueeze(1).broadcast_to([P, ET, D])).then_inc(s_zero, 16)
            sp.wait_ge(s_mb, 32)
            sp.dma_start(W1raw[:], w1[0].rearrange("(k p) f -> p k f", p=P)).then_inc(s_w1, 16)
            sp.dma_start(W2raw[:], w2[0].rearrange("(k p) d -> p k d", p=P)).then_inc(s_w2, 16)
            sp.dma_start(b2r[:], b2.partition_broadcast(P)).then_inc(s_b2, 16)

            def store_rows(g, r):
                sp.dma_start(rows_t[:, bass.ds(TG * g, TG), D:2 * D],
                             GB[:, bass.ds(g // GPB, 1), :].broadcast_to([P, TG, D])).then_inc(s_gbout, 16)
                sp.wait_ge(s_x1, g + 1)
                need(sp, s_x1c[r], 16 * (g // 2))
                sp.dma_start(acc_t[:, bass.ds(TG * g, TG), :], x1[r][:]).then_inc(s_x1c[r], 16)
                sp.wait_ge(s_h2, TG * (g + 1))
                need(sp, s_h2out[r], 16 * (g // 2))
                hold(sp)
                sp.dma_start(rows_t[:, bass.ds(TG * g, TG), 0:D], h2[r][:]).then_inc(s_h2out[r], 16)

            store_rows(0, 0)
            store_rows(1, 1)
            with sp.Fori(1, GROUPS // 2) as i:
                store_rows(2 * i, 0)
                store_rows(2 * i + 1, 1)

            sp.wait_ge(s_gates, 2)
            sp.dma_start(rows_t[:, :, 2 * D:], gates[:]).then_inc(s_gateout, 16)

            with sp.Fori(1, E) as e:
                sp.wait_ge(s_w1hi, KD * e)
                sp.wait_ge(s_w1lo, KD * e)
                sp.dma_start(W1raw[:], w1[e].rearrange("(k p) f -> p k f", p=P)).then_inc(s_w1, 16)
                sp.wait_ge(s_w2hi, KD * e)
                sp.wait_ge(s_w2lo, KD * e)
                sp.dma_start(W2raw[:], w2[e].rearrange("(k p) d -> p k d", p=P)).then_inc(s_w2, 16)

            for c, (_, n, _) in enumerate(CHUNKS):
                sp.wait_ge(s_sca[c], 16 * n * E)
            sp.dma_start(out.rearrange("b s d -> (b s) d"), acc_dram[0:TOKENS, :]).then_inc(s_out, 16)
            sp.wait_ge(s_out, 16)

        @block.gpsimd
        def _(pool):
            pool.memset(zeros[:], 0.0).then_inc(s_zeros, 1)
            pool.memset(ident[:], 0.0).then_inc(s_pc, 1)
            pool.wait_ge(s_pc, 1)
            pool.affine_select(out=ident[:], in_=ident[:], compare_op=ALU.not_equal, fill=1.0, base=0,
                               pattern=[[-1, P]], channel_multiplier=1).then_inc(s_pc, 1)
            pool.memset(neghalf[:], -0.5).then_inc(s_pc, 1)
            pool.memset(state[:, :, 2 * GT:2 * GT + 1], 0.0).then_inc(s_pc, 1)
            pool.wait_ge(s_pc, 4)
            pool.memset(go[:], 0.0).then_inc(s_go, 1)
            pool.wait_ge(s_zeros, 1)
            pool.wait_ge(s_lam, 1)
            for k in range(KD):
                pool.tensor_scalar(lamt[:, k, :], zeros[:, 0:GT], lam[:, k:k + 1], 0.0, ALU.add, ALU.add)\
                    .then_inc(s_lamt, 1)

            pool.iota(ioi[:], pattern=[[1, P]], base=0, channel_multiplier=0).then_inc(s_rc, 1)
            pool.iota(pci[:], pattern=[[0, 1]], base=0, channel_multiplier=1).then_inc(s_rc, 1)
            pool.memset(onesb[:], 1.0).then_inc(s_rc, 1)
            pool.memset(before[:], 1.0).then_inc(s_rc, 1)
            pool.memset(onesj[:], 1.0).then_inc(s_rc, 1)
            pool.iota(sparei[:], pattern=[[0, E], [P, ET]], base=P, channel_multiplier=1).then_inc(s_rc, 1)
            pool.wait_ge(s_rc, 6)
            pool.tensor_copy(spare[:], sparei[:]).then_inc(s_rc, 1)
            pool.tensor_copy(io[:], ioi[:]).then_inc(s_rc, 1)
            pool.tensor_copy(pcol[:], pci[:]).then_inc(s_rc, 1)
            pool.affine_select(out=before[:], in_=before[:], compare_op=ALU.is_gt, fill=0.0, base=0,
                               pattern=[[1, P]], channel_multiplier=-1).then_inc(s_rc, 1)
            pool.wait_ge(s_rc, 10)
            pool.tensor_scalar(eio[:], io[:, 0:E], float(ET), 0.0, ALU.mult, ALU.add).then_inc(s_rc, 1)
            pool.tensor_scalar(erank[:], io[:, 0:E], -1.0, float(E), ALU.mult, ALU.add).then_inc(s_rc, 1)
            pool.tensor_scalar(jp1[:], io[:, 0:J], 1.0, 0.0, ALU.add, ALU.add).then_inc(s_rc, 1)
            pool.wait_ge(s_rc, 13)

            def scale_wo(b):
                if b == 0:
                    pool.wait_ge(s_attnw, 16)
                    pool.wait_ge(s_mb, 32)
                need(pool, s_wohi, b)
                for k in range(KD):
                    pool.tensor_tensor(wos[:, k, :], wraw[:, 3, k, :], MB[:, b, 0, :], ALU.mult).then_inc(s_wo, 1)
                pool.wait_ge(s_wohi, b + 1)
                pool.wait_ge(s_wo, 3 * b + 2)
                pool.tensor_tensor(wolo[:, b], wos[:], f32(wohi[:, b]), ALU.subtract).then_inc(s_wo, 1)

            def split_first(i):
                if i < KD:
                    pool.wait_ge(s_w1, 16)
                    pool.wait_ge(s_w1hi, i + 1)
                    pool.tensor_tensor(W1lo[:, i, :], W1raw[:, i, :], f32(W1hi[:, i, :]), ALU.subtract)\
                        .then_inc(s_w1lo, 1)
                else:
                    i -= KD
                    h = slice(i * KF // 2, (i + 1) * KF // 2)
                    pool.wait_ge(s_w2, 16)
                    pool.wait_ge(s_w2hi, i + 1)
                    pool.tensor_tensor(W2lo[:, h, :], W2raw[:, h, :], f32(W2hi[:, h, :]), ALU.subtract)\
                        .then_inc(s_w2lo, 1)

            def step(s, r):
                g, q = s - 2, r
                if has(g):
                    need(pool, s_h2, TG * (g - 1))
                    pool.wait_ge(s_mv["h"], TG * g + TG)
                    hold(pool)
                    rstd(pool, "h", q, slice(0, 1), 3 * g)
                    pool.wait_ge(s_rs["h"], 3 * g + 3)
                    hold(pool)
                    for t in range(TG):
                        pool.tensor_scalar(xn2[q][:, t, :], x1[q][:, t, :], of(nms, "h", q)[:, t:t + 1],
                                           of(rss, "h", q)[:, t:t + 1], ALU.add, ALU.mult).then_inc(s_xn2, 1)
                    if isinstance(g, int) and g == 0:
                        pool.wait_ge(s_mb, 16 * 2)
                    b = g // GPB
                    pool.wait_ge(s_xn2, TG * g + TG)
                    for t in range(TG):
                        pool.tensor_tensor(xn2[q][:, t, :], xn2[q][:, t, :], MB[:, b, 2, :], ALU.mult)\
                            .then_inc(s_h2m, 1)
                    need(pool, s_h2T, g - 1)
                    need(pool, s_h2out[q], 16 * (g // 2))
                    pool.wait_ge(s_h2m, TG * g + TG)
                    for t in range(TG):
                        pool.tensor_tensor(h2[q][:, t, :], xn2[q][:, t, :], MB[:, b, 1, :], ALU.add)\
                            .then_inc(s_h2, 1)
                if has(s + 2):
                    need(pool, s_xn, TG * (s + 1))
                    pool.wait_ge(s_mv["x"], TG * (s + 3))
                if has(s):
                    need(pool, s_yn, TG * (s - 1))
                    pool.wait_ge(s_mv["y"], TG * (s + 1))
                if has(s) or has(s + 2):
                    hold(pool)
                    rstd(pool, "xy", r, slice(0 if has(s + 2) else 1, 2 if has(s) else 1), 4 * (s + 2))
                if isinstance(s, int) and 0 <= s < B:
                    scale_wo(s)

            sweep(pool, step)
            for i in range(4):
                split_first(i)

            for n in range(J // JC):
                js = slice(n * JC, n * JC + JC)
                pool.wait_ge(s_oh, 2 * n + 2)
                pool.tensor_tensor(ohcp[:, js, 1, :], oheq[:, js, :],
                                   jp1[:, js].unsqueeze(2).broadcast_to([P, JC, NC]), ALU.mult).then_inc(s_ohj, 1)

            pool.wait_ge(s_idx, 1)
            pool.memset(yb[:, ET - 1, :], 0.0).then_inc(s_ybz, 1)
            for r in range(2):
                pool.wait_ge(s_h2out[r], 16 * (GROUPS // 2))
            pool.wait_ge(s_gbout, 16 * GROUPS)
            pool.wait_ge(s_gateout, 16)

            def gather(e, c):
                t0, n, _ = CHUNKS[c]
                need(pool, s_gat[c], 16 * n * e)
                pool.tensor_copy(gcur[:, t0:t0 + n], gidx[:, e, t0:t0 + n]).then_inc(s_gcur, 1)
                pool.wait_ge(s_gcur, NCH * e + c + 1)
                need(pool, s_tr, NCH * (e - 1) + c + 1)
                need(pool, s_yb, ET * (e - 1) + TILES_BEFORE[c + 1])
                hold(pool)
                for t in range(t0, t0 + n):
                    pool.indirect_dma_start(
                        out=xg[:, t, :], out_offset=None, in_=rows_dram,
                        in_offset=bass.IndirectOffsetOnAxis(ap=gcur[:, t:t + 1].bitcast(U32), axis=0),
                        bounds_check=TOKENS - 1, oob_is_err=False).then_inc(s_gat[c], 16)

            def scatter(e, c):
                t0, n, _ = CHUNKS[c]
                if c == 0:
                    for b, (_, nb, _) in enumerate(CHUNKS):
                        need(pool, s_sca[b], 16 * nb * e)
                pool.tensor_copy(scur[:, t0:t0 + n], sidx[:, e, t0:t0 + n]).then_inc(s_scur, 1)
                pool.wait_ge(s_scur, NCH * e + c + 1)
                for i in range(n):
                    t = t0 + i
                    pool.wait_ge(s_yb, ET * e + TILES_BEFORE[c] + i + 1)
                    hold(pool)
                    pool.indirect_dma_start(
                        out=acc_dram, out_offset=bass.IndirectOffsetOnAxis(ap=scur[:, t:t + 1].bitcast(U32), axis=0),
                        in_=yb[:, t, :], in_offset=None,
                        bounds_check=TOKENS + ET * P - 1, compute_op=ALU.add).then_inc(s_sca[c], 16)

            def expert(e, first, last):
                for c in range(NCH):
                    if c > 0:
                        scatter(e, c - 1)
                        if not last:
                            gather(e + 1, c - 1)
                    elif not first:
                        scatter(e - 1, NCH - 1)
                        gather(e, NCH - 1)

            for r in range(2):
                pool.wait_ge(s_x1c[r], 16 * (GROUPS // 2))
            pool.wait_ge(s_zero, 16)
            for c in range(NCH):
                gather(0, c)
            expert(0, True, False)
            expert(1, False, False)
            with pool.Fori(2, E - 1) as e:
                expert(e, False, False)
            expert(E - 1, False, True)
            scatter(E - 1, NCH - 1)

        @block.scalar
        def _(act):
            wmod_k = wmod.rearrange("(k p) n -> p k n", p=P)
            act.dma_start(lamraw[:], beta_ch).then_inc(s_beta, 16)
            act.dma_start(ct[:], cT).then_inc(s_mod_in, 16)
            act.dma_start(wm[:, :, 0:2 * D], wmod_k[:, :, 0:2 * D]).then_inc(s_mod_in, 16)
            act.dma_start(wm[:, :, 2 * D:], wmod_k[:, :, 2 * D:]).then_inc(s_modrest_in, 16)
            act.wait_ge(s_beta, 16)
            act.activation(lam[:], lamraw[:], ACT.Sigmoid).then_inc(s_lam, 1)
            act.wait_ge(s_mod_in, 32)
            act.activation(sct[:], ct[:], ACT.Silu).then_inc(s_sct, 1)
            act.wait_ge(s_attnw, 16)
            for w in range(3):
                act.activation(whi[:, w], wraw[:, w], ACT.Copy).then_inc(s_whi, 1)

            def step(s, r):
                q = 1 - r
                g = s + 1
                if has(g):
                    act.wait_ge(s_rs["xy"], scaled_x(g))
                    need(act, s_xT, g - 1)
                    hold(act)
                    for t in range(TG):
                        act.activation(xn[q][:, t, :], X[:, TG * g + t, :], ACT.Identity, bias=of(nrs, "x", q)[:, t:t + 1],
                                       scale=of(rss, "x", q)[:, t:t + 1]).then_inc(s_xn, 1)
                g = s - 1
                if has(g):
                    act.wait_ge(s_ynT, g + 1)
                    need(act, s_zg, g - 1)
                    if isinstance(g, int) and g == 0:
                        act.wait_ge(s_small, 16 * 5)
                    for k in range(KD):
                        act.activation(z[q][:, k, :], bank(BN)[:, k, :], ACT.Identity, bias=bcol[:, k:k + 1],
                                       scale=gcol[:, k:k + 1]).then_inc(s_z, 1)
                g = s - 1
                if has(g):
                    act.wait_ge(s_zg, g + 1)
                    need(act, s_o, g - 1)
                    act.activation(zghi[q][:], zg[q][:], ACT.Copy).then_inc(s_zghi, 1)
                g = s
                if has(g):
                    act.wait_ge(s_g, g + 1)
                    need(act, s_zg, g - 1)
                    act.activation(gate[r][:], bank(BG), ACT.Silu).then_inc(s_gate, 1)
                g = s + 1
                if has(g):
                    b = g // GPB
                    act.wait_ge(s_xT, g + 1)
                    need(act, s_hlo, g - 1)
                    if isinstance(g, int) and g == 0:
                        act.wait_ge(s_modc, 2)
                    hold(act)
                    for k in range(KD):
                        act.activation(h32[q][:, k, :], bank(BX)[:, k, :], ACT.Identity,
                                       bias=modc[:, 0, k, bass.ds(b, 1)], scale=modc[:, 1, k, bass.ds(b, 1)])\
                            .then_inc(s_h32, 1)
                    act.wait_ge(s_h32, KD * (g + 1))
                    need(act, s_g, g - 1)
                    act.activation(hhi[q][:], h32[q][:], ACT.Copy).then_inc(s_hhi, 1)
                g = s
                if has(g):
                    act.wait_ge(s_rs["xy"], scaled_y(g))
                    need(act, s_ynT, g - 1)
                    for t in range(TG):
                        act.activation(yn[r][:, t, :], bank(BY)[:, t, :], ACT.Identity, bias=of(nrs, "y", r)[:, t:t + 1],
                                       scale=of(rss, "y", r)[:, t:t + 1]).then_inc(s_yn, 1)
                g = s - 2
                if has(g):
                    act.wait_ge(s_h2T, g + 1)
                    need(act, s_lg, g - 1)
                    act.activation(h2T[r][:], bank(BH), ACT.Copy).then_inc(s_h2Ts, 1)
                if isinstance(s, int) and 0 <= s < B:
                    act.wait_ge(s_wo, 3 * s + 2)
                    act.activation(wohi[:, s], wos[:], ACT.Copy).then_inc(s_wohi, 1)
                if isinstance(s, int) and GROUPS - 2 <= s < GROUPS + 2:
                    i = s - (GROUPS - 2)
                    if i < KD:
                        act.wait_ge(s_w1, 16)
                        act.activation(W1hi[:, i, :], W1raw[:, i, :], ACT.Copy).then_inc(s_w1hi, 1)
                    else:
                        half = slice((i - KD) * KF // 2, (i - KD + 1) * KF // 2)
                        act.wait_ge(s_w2, 16)
                        act.activation(W2hi[:, half, :], W2raw[:, half, :], ACT.Copy).then_inc(s_w2hi, 1)

            sweep(act, step)

            act.wait_ge(s_dl, 1)
            act.activation(rm["ex"][:], rm["dl"][:], ACT.Exp).then_inc(s_exp, 1)
            act.wait_ge(s_rc, 13)
            for n in range(J // JC):
                js = slice(n * JC, n * JC + JC)
                act.wait_ge(s_oh, 2 * n + 2)
                act.activation(ohcp[:, js, 0, :], oheq[:, js, :], ACT.Copy, scale=pcol[:, 0:1]).then_inc(s_ohp, 1)

            def rows_hi(e, c):
                _, _, n = CHUNKS[c]
                q = NCH * e + c
                act.wait_ge(s_tr, q + 1)
                need(act, s_w1ps, KF * (q - 1))
                for k in range(KD):
                    act.activation(hThi[c % 2][:, k, 0:n], psum[:, 6 + k, 0:n], ACT.Copy).then_inc(s_thi, 1)

            def gelu(e, c):
                _, _, n = CHUNKS[c]
                q = NCH * e + c
                for m in range(KF):
                    act.wait_ge(s_w1ps, KF * q + m + 1)
                    need(act, s_glo, KF * q + m + 1 - NG)
                    hold(act)
                    act.activation(g32[m % NG][:, 0:n], psum[:, m % 4, 0:n], ACT.Gelu_apprx_tanh,
                                   bias=b1c[:, e, m:m + 1]).then_inc(s_gelu, 1)

            def expert(e, first, last):
                for c in range(NCH):
                    if c + 1 < NCH:
                        rows_hi(e, c + 1)
                    elif not last:
                        rows_hi(e + 1, 0)
                    _, _, n = CHUNKS[c]
                    q = NCH * e + c
                    if c != SPARE:
                        gelu(e, c)
                    else:
                        with act.If(load_of(act, e) > CHUNKS[c][0] * P):
                            gelu(e, c)
                        with act.Else():
                            act.wait_ge(s_w1ps, KF * (q + 1))
                            hold(act)
                            act.activation(left_out[0][:], ident[:, 0:1], ACT.Copy).then_inc(s_gelu, KF)
                    if c == NCH - 1 and not last:
                        act.wait_ge(s_w1, 16 * (e + 2))
                        act.wait_ge(s_w1ps, KF * NCH * (e + 1))
                        for k in range(KD):
                            act.activation(W1hi[:, k, :], W1raw[:, k, :], ACT.Copy).then_inc(s_w1hi, 1)
                    if c == 0 and not first:
                        act.wait_ge(s_w2, 16 * (e + 1))
                        act.wait_ge(s_w2ps, ET * e)
                        for k in range(2):
                            half = slice(k * KF // 2, (k + 1) * KF // 2)
                            act.activation(W2hi[:, half, :], W2raw[:, half, :], ACT.Copy).then_inc(s_w2hi, 1)

            act.wait_ge(s_idx, 1)
            rows_hi(0, 0)
            expert(0, True, False)
            with act.Fori(1, E - 1) as e:
                expert(e, False, False)
            expert(E - 1, False, True)

        @block.tensor
        def _(pe):
            def mod_columns():
                pe.wait_ge(s_sct, 1)
                for j in range(2):
                    for m in range(KD):
                        for k in range(KD):
                            mm = pe.matmul(psum[:, BG, (j * KD + m) * B:(j * KD + m + 1) * B],
                                           wm[:, k, j * D + m * P:j * D + (m + 1) * P], sct[:, k, :],
                                           start=(k == 0), stop=(k == KD - 1))
                mm.then_inc(s_modcps, 1)

            def mod_rows():
                pe.wait_ge(s_modrest_in, 16)
                for b, n in ((BO, 1), (BH, 2)):
                    for k in range(KD):
                        mm = pe.matmul(psum[0:B, b, :], sct[:, k, :], wm[:, k, n * 512:(n + 1) * 512],
                                       start=(k == 0), stop=(k == KD - 1))
                mm.then_inc(s_modps, 1)

            mod_columns()
            pe.wait_ge(s_pc, 4)
            pe.wait_ge(s_modc, 2)

            def turn(dst, src, r):
                for k in range(KD):
                    for t in range(TG):
                        last = pe.transpose(dst[:, k, t * P:(t + 1) * P], src[:, t, k * P:(k + 1) * P], ident[:])
                return last

            def project(w, g, r, done, dst):
                for m in range(KD):
                    ms = slice(m * P, (m + 1) * P)
                    product(pe, dst[:, m, :], [(whi[:, w, k, ms], wlo[:, w, k, ms], hhi[r][:, k, :], hlo[r][:, k, :])
                                               for k in range(KD)], done if m == KD - 1 else None)

            def step(s, r):
                q = 1 - r
                g = s
                if has(g):
                    if isinstance(g, int) and g == 0:
                        mod_rows()
                        pe.wait_ge(s_wlo, 3)
                    pe.wait_ge(s_hhi, g + 1)
                    pe.wait_ge(s_hlo, g + 1)
                    need(pe, s_state, KD * g)
                    project(1, g, r, s_v, bank(BV))
                g = s - 1
                if has(g):
                    pe.wait_ge(s_yn, TG * (g + 1))
                    need(pe, s_z, KD * g)
                    turn(bank(BN), yn[q], q).then_inc(s_ynT, 1)
                g = s
                if has(g):
                    need(pe, s_y, g)
                    project(0, g, r, s_q, bank(BQ))
                g = s - 3
                if has(g):
                    pe.wait_ge(s_h2Ts, g + 1)
                    need(pe, s_lgs, g)
                    pe.wait_ge(s_h32, KD * (min(g + 4, GROUPS) if isinstance(g, int) else g + 4))
                    for t in range(TG):
                        for k in range(KD):
                            mm = pe.matmul(psum[:, BX, t * E:(t + 1) * E], h2T[q][:, k, t * P:(t + 1) * P], rw[:, k, :],
                                           start=(k == 0), stop=(k == KD - 1))
                    mm.then_inc(s_lg, 1)
                g = s
                if has(g):
                    need(pe, s_gate, g)
                    project(2, g, r, s_g, bank(BG))
                    pe.wait_ge(s_y, g + 1)
                    need(pe, s_yn, TG * g)
                    turn(bank(BY), ysb[r], r).then_inc(s_yT, 1)
                g = s + 1
                if has(g):
                    pe.wait_ge(s_xn, TG * (g + 1))
                    need(pe, s_h32, KD * g)
                    need(pe, s_lgs, g - 3)
                    turn(bank(BX), xn[q], q).then_inc(s_xT, 1)
                g = s - 1
                if has(g):
                    b = g // GPB
                    pe.wait_ge(s_zghi, g + 1)
                    pe.wait_ge(s_zglo, g + 1)
                    if isinstance(g, int) and g == 0:
                        pe.wait_ge(s_modrow, 4)
                    need(pe, s_x1, g)
                    if isinstance(g, int):
                        pe.wait_ge(s_wo, 3 * min(g // GPB + 1, B))
                    else:
                        pe.wait_ge(s_wo, 3 * B)
                    for t in range(TG):
                        ts = slice(t * P, (t + 1) * P)
                        product(pe, bank(BO)[:, t, :], [(zghi[q][:, k, ts], zglo[q][:, k, ts], wohi[:, b, k, :],
                                                         wolo[:, b, k, :]) for k in range(KD)],
                                s_o if t == TG - 1 else None)
                g = s - 2
                if has(g):
                    pe.wait_ge(s_h2, TG * (g + 1))
                    need(pe, s_h2Ts, g)
                    turn(bank(BH), h2[r], r).then_inc(s_h2T, 1)

            sweep(pe, step)

            pe.wait_ge(s_ohd, 2)
            pe.wait_ge(s_rc, 13)
            ohf = OH[:].rearrange("p j e -> p (j e)")
            pe.matmul(psum[:, 0, :], before[:], ohf, start=True, stop=True).then_inc(s_cnt, 1)
            pe.matmul(psum[:, 1, :], onesb[:], ohf, start=True, stop=True).then_inc(s_cnt, 1)
            for n in range(J // JC):
                pe.wait_ge(s_oh, 2 * n + 2)
                pe.wait_ge(s_ohp, n + 1)
                pe.wait_ge(s_ohj, n + 1)
                for j in range(n * JC, n * JC + JC):
                    mm = pe.matmul(psum[:, 2, 0:2 * NC], ohlo[:, j, :], ohcp[:, j].rearrange("p a c -> p (a c)"),
                                   start=(j == 0), stop=(j == J - 1))
            mm.then_inc(s_slots, 1)

            def rows(e, c):
                t0, n, _ = CHUNKS[c]
                q = NCH * e + c
                pe.wait_ge(s_gat[c], 16 * n * (e + 1))
                need(pe, s_thi, KD * q)
                need(pe, s_tlo, KD * q)
                for k in range(KD):
                    for i in range(n):
                        tr = pe.transpose(psum[:, 6 + k, i * P:(i + 1) * P], xg[:, t0 + i, k * P:(k + 1) * P], ident[:])
                tr.then_inc(s_tr, 1)

            def up(e, c, held):
                _, _, n = CHUNKS[c]
                q, r = NCH * e + c, c % 2
                pe.wait_ge(s_thi, KD * (q + 1))
                pe.wait_ge(s_tlo, KD * (q + 1))
                pe.wait_ge(s_w1hi, KD * (e + 1))
                pe.wait_ge(s_w1lo, KD * (e + 1))
                def hidden(w1_product):
                    for m in range(KF):
                        need(pe, s_gelu, KF * q + m + 1 - 4)
                        w1_product(psum[:, m % 4, 0:n], slice(m * P, (m + 1) * P))

                def two_tiles(dst, ms):
                    full(dst, ms, 2 * P)

                def full(dst, ms, w=n):
                    product(pe, dst[:, 0:w], [(W1hi[:, k, ms], W1lo[:, k, ms], hThi[r][:, k, 0:w], hTlo[r][:, k, 0:w])
                                              for k in range(KD)], s_w1ps)

                first, _, _ = CHUNKS[c]
                if c != SPARE:
                    hidden(full)
                else:
                    with pe.If(held > first * P):
                        with pe.If(held > (first + 2) * P):
                            hidden(full)
                        with pe.Else():
                            hidden(two_tiles)
                    with pe.Else():
                        need(pe, s_gelu, KF * q + 1 - 4)
                        pe.matmul(psum[:, 0, 0:8], W1hi[:, 0, 0:P], hThi[r][:, 0, 0:8], start=True, stop=True)\
                            .then_inc(s_w1ps, KF)

            def down(e, c, held):
                t0, nt, n = CHUNKS[c]
                q, r = NCH * e + c, c % 2
                pe.wait_ge(s_glo, KF * (q + 1))
                pe.wait_ge(s_w2hi, 2 * (e + 1))
                pe.wait_ge(s_w2lo, 2 * (e + 1))
                for i in range(nt):
                    T = ET * e + TILES_BEFORE[c] + i
                    cols = slice(i * P, min((i + 1) * P, n))
                    M = cols.stop - cols.start
                    need(pe, s_yu, T - 1)
                    dst = psum[0:M, 4 + (TILES_BEFORE[c] + i) % 2, 0:D]

                    def full():
                        product(pe, dst, [(ghi[r][:, m, cols], glo[r][:, m, cols], W2hi[:, m, :], W2lo[:, m, :])
                                          for m in range(KF)], s_w2ps)

                    if c != SPARE:
                        full()
                    else:
                        with pe.If(held > (t0 + i) * P):
                            full()
                        with pe.Else():
                            pe.matmul(dst[:, 0:8], ghi[r][:, 0, cols], W2hi[:, 0, 0:8], start=True, stop=True)\
                                .then_inc(s_w2ps, 1)

            def expert(e, first, last):
                held = load_of(pe, e)
                for c in range(NCH):
                    if c + 1 < NCH:
                        rows(e, c + 1)
                    elif not last:
                        rows(e + 1, 0)
                    up(e, c, held)
                    if c > 0:
                        down(e, c - 1, held)
                    elif not first:
                        down(e - 1, NCH - 1, load_of(pe, e - 1))

            pe.wait_ge(s_idx, 1)
            rows(0, 0)
            expert(0, True, False)
            with pe.Fori(1, E - 1) as e:
                expert(e, False, False)
            expert(E - 1, False, True)
            down(E - 1, NCH - 1, load_of(pe, E - 1))

        @block.vector
        def _(v):
            def mod_rows():
                v.wait_ge(s_modps, 1)
                for j, n in ((0, BO), (3, BH)):
                    src = psum[0:B, n, 0:D] if j == 0 else psum[0:B, n, D:2 * D]
                    i = 0 if j == 0 else 1
                    v.tensor_copy(modraw[:, i, :], src).then_inc(s_modt, 1)
                    v.tensor_scalar(sgn[:, i, :], src, 0.0, 2.0, ALU.is_ge, ALU.mult).then_inc(s_modt, 1)
                v.tensor_copy(modr[:, 1, :], psum[0:B, BO, D:2 * D]).then_inc(s_modrow, 1)
                v.tensor_scalar(modr[:, 2, :], psum[0:B, BH, 0:D], 1.0, None, ALU.add).then_inc(s_modrow, 1)
                v.wait_ge(s_modt, 4)
                v.scalar_tensor_tensor(out=mag[:], in0=modraw[:], scalar=-1.0, in1=modraw[:], op0=ALU.mult, op1=ALU.max)\
                    .then_inc(s_modt, 1)
                v.wait_ge(s_modt, 5)
                v.tensor_scalar(mag[:], mag[:], 0.25, None, ALU.max).then_inc(s_modt, 1)
                v.wait_ge(s_modt, 6)
                for i, j in ((0, 0), (1, 3)):
                    v.scalar_tensor_tensor(out=modr[:, j, :], in0=sgn[:, i, :], scalar=1.0, in1=mag[:, i, :],
                                           op0=ALU.subtract, op1=ALU.mult).then_inc(s_modrow, 1)

            def mod_columns():
                v.wait_ge(s_modcps, 1)
                mc = psum[:, BG, 0:2 * KD * B].rearrange("p (j m b) -> p j m b", j=2, m=KD)
                v.tensor_copy(modc[:, 0], mc[:, 0]).then_inc(s_modc, 1)
                v.tensor_scalar(modc[:, 1], mc[:, 1], 1.0, None, ALU.add).then_inc(s_modc, 1)

            def attn_w_lo():
                for w in range(3):
                    v.wait_ge(s_whi, w + 1)
                    v.tensor_tensor(wlo[:, w], wraw[:, w], f32(whi[:, w]), ALU.subtract).then_inc(s_wlo, 1)

            def step(s, r):
                q = 1 - r
                g = s
                if has(g):
                    v.wait_ge(s_v, g + 1)
                    need(v, s_state, KD * g)
                    if isinstance(g, int) and g == 0:
                        v.wait_ge(s_lamt, KD)
                        v.wait_ge(s_pc, 4)
                    for k in range(KD):
                        if r == 1:
                            init = state[:, k, GT - 1:GT]
                        else:
                            new = (g // 2) % (GPB // 2)
                            if isinstance(g, int):
                                at = 2 * GT - min(new, 1)
                            else:
                                at = 2 * GT - new
                            init = state[:, k, bass.ds(at, 1)]
                        v.tensor_tensor_scan(state[:, k, r * GT:(r + 1) * GT], lamt[:, k, :], bank(BV)[:, k, :],
                                             init, ALU.mult, ALU.add).then_inc(s_state, 1)
                    v.wait_ge(s_q, g + 1)
                    v.wait_ge(s_state, KD * (g + 1))
                    need(v, s_yT, g - 1)
                    v.tensor_tensor(ysb[r][:], bank(BQ), state[:, :, r * GT:(r + 1) * GT], ALU.mult).then_inc(s_y, 1)
                g = s - 1
                if has(g):
                    v.wait_ge(s_z, KD * (g + 1))
                    v.wait_ge(s_gate, g + 1)
                    need(v, s_zghi, g - 1)
                    v.tensor_tensor(zg[q][:], z[q][:], gate[q][:], ALU.mult).then_inc(s_zg, 1)
                g = s - 3
                if has(g):
                    v.wait_ge(s_lg, g + 1)
                    v.tensor_tensor(LG[:, bass.ds(TG * g, TG), :],
                                    psum[:, BX, 0:TG * E].rearrange("p (t e) -> p t e", t=TG),
                                    rb[:].unsqueeze(1).broadcast_to([P, TG, E]), ALU.add).then_inc(s_lgs, 1)
                g = s + 2
                if has(g):
                    v.wait_ge(s_x[r], 16 * (g // 2 + 1))
                    stats(v, "x", g, r, [X[:, TG * g + t, :] for t in range(TG)])
                g = s - 1
                if has(g):
                    v.wait_ge(s_zghi, g + 1)
                    need(v, s_o, g - 1)
                    v.tensor_tensor(zglo[q][:], zg[q][:], f32(zghi[q][:]), ALU.subtract).then_inc(s_zglo, 1)
                g = s
                if has(g):
                    v.wait_ge(s_yT, g + 1)
                    stats(v, "y", g, r, [bank(BY)[:, t, :] for t in range(TG)])
                if isinstance(s, int) and s == -1:
                    mod_columns()
                    attn_w_lo()
                g = s + 1
                if has(g):
                    v.wait_ge(s_hhi, g + 1)
                    need(v, s_g, g - 1)
                    v.tensor_tensor(hlo[q][:], h32[q][:], f32(hhi[q][:]), ALU.subtract).then_inc(s_hlo, 1)
                if isinstance(s, int) and s == -1:
                    mod_rows()
                g = s - 1
                if has(g):
                    v.wait_ge(s_o, g + 1)
                    need(v, s_x1c[q], 16 * (g // 2))
                    need(v, s_xn2, TG * (g - 1))
                    v.tensor_tensor(x1[q][:], X[:, bass.ds(TG * g, TG), :], bank(BO), ALU.add).then_inc(s_x1, 1)
                    v.wait_ge(s_x1, g + 1)
                    stats(v, "h", g, q, [x1[q][:, t, :] for t in range(TG)])

            sweep(v, step)

            chain = [0]

            def link(ins):
                ins.then_inc(s_rv, 1)
                chain[0] += 1
                v.wait_ge(s_rv, chain[0])

            def over_e(ap):
                return ap.unsqueeze(2).broadcast_to([P, ap.shape[1], E])

            v.wait_ge(s_lgs, GROUPS)
            for r in range(2):
                v.wait_ge(s_h2out[r], 16 * (GROUPS // 2))
            v.wait_ge(s_zero, 16)
            for r in range(2):
                v.wait_ge(s_x1c[r], 16 * (GROUPS // 2))
            v.wait_ge(s_h2Ts, GROUPS)
            link(v.tensor_reduce(rm["m1"][:], LG[:], AX_X, ALU.max))
            v.wait_ge(s_rc, 13)
            for n, lg in (("1", LG[:]), ("2", rt["lg2"][:])):
                if n == "2":
                    link(v.scalar_tensor_tensor(out=rt["lg2"][:], in0=rt["oh1"][:], scalar=NEG, in1=LG[:],
                                                op0=ALU.mult, op1=ALU.add))
                    link(v.tensor_reduce(rm["m2"][:], rt["lg2"][:], AX_X, ALU.max))
                    v.tensor_tensor(rm["dl"][:], rm["m2"][:], rm["m1"][:], ALU.subtract).then_inc(s_dl, 1)
                link(v.tensor_tensor(rt["eq" + n][:], lg, over_e(rm["m" + n][:]), ALU.is_equal))
                link(v.tensor_tensor(rt["sc" + n][:], rt["eq" + n][:], erank[:].unsqueeze(1).broadcast_to([P, TILES, E]),
                                     ALU.mult))
                link(v.tensor_reduce(rm["i" + n][:], rt["sc" + n][:], AX_X, ALU.max))
                link(v.tensor_tensor(rt["oh" + n][:], rt["sc" + n][:], over_e(rm["i" + n][:]), ALU.is_equal))
                k = int(n) - 1
                v.tensor_copy(OH[:, k * TILES:(k + 1) * TILES, :], rt["oh" + n][:]).then_inc(s_ohd, 1)
            v.wait_ge(s_ohd, 2)
            link(v.tensor_tensor(ohe[:], OH[:], eio[:].unsqueeze(1).broadcast_to([P, J, E]), ALU.mult))
            link(v.tensor_reduce(e10[:], ohe[:], AX_X, ALU.add))
            v.wait_ge(s_exp, 1)
            link(v.tensor_scalar(rm["se"][:], rm["ex"][:], 1.0, None, ALU.add))
            v.reciprocal(gates[:, :, 0], rm["se"][:]).then_inc(s_gates, 1)
            v.wait_ge(s_gates, 1)
            v.tensor_tensor(gates[:, :, 1], rm["ex"][:], gates[:, :, 0], ALU.mult).then_inc(s_gates, 1)
            v.wait_ge(s_cnt, 2)
            tot = psum[:, 1, :].rearrange("p (j e) -> p j e", e=E)
            for e in range(E):
                v.tensor_tensor_scan(csum[:, :, e], onesj[:], tot[:, :, e], 0.0, ALU.mult, ALU.add).then_inc(s_cs, 1)
            v.wait_ge(s_cs, E)
            link(v.tensor_tensor(posa[:], psum[:, 0, :].rearrange("p (j e) -> p j e", e=E), csum[:], ALU.add))
            link(v.tensor_copy(load[:], csum[:, J - 1, :]))
            link(v.tensor_tensor(posb[:], posa[:], tot, ALU.subtract))
            link(v.tensor_tensor(posc[:], posb[:], OH[:], ALU.mult))
            link(v.tensor_reduce(pos[:], posc[:], AX_X, ALU.add))
            link(v.tensor_copy(posi[:], pos[:]))
            link(v.tensor_scalar(hii[:], posi[:], 7, None, ALU.arith_shift_right))
            link(v.tensor_scalar(loi[:], posi[:], P - 1, None, ALU.bitwise_and))
            link(v.tensor_copy(hif[:], hii[:]))
            link(v.tensor_copy(lof[:], loi[:]))
            link(v.tensor_scalar(kept[:], pos[:], float(CAP), -4.0 * NC, ALU.is_lt, ALU.mult))
            link(v.tensor_tensor(colf[:], hif[:], e10[:], ALU.add))
            link(v.tensor_tensor(coff[:], colf[:], kept[:], ALU.add))
            link(v.tensor_scalar(col[:], coff[:], 4.0 * NC, None, ALU.add))
            for n in range(J // JC):
                js = slice(n * JC, n * JC + JC)
                v.tensor_tensor(oheq[:, js, :], io[:, 0:NC].unsqueeze(1).broadcast_to([P, JC, NC]),
                                col[:, js].unsqueeze(2).broadcast_to([P, JC, NC]), ALU.is_equal).then_inc(s_oh, 1)
                v.tensor_tensor(ohlo[:, js, :], io[:].unsqueeze(1).broadcast_to([P, JC, P]),
                                lof[:, js].unsqueeze(2).broadcast_to([P, JC, P]), ALU.is_equal).then_inc(s_oh, 1)
            v.wait_ge(s_slots, 1)
            link(v.tensor_copy(tabp[:], psum[:, 2, 0:2 * NC]))
            link(v.tensor_scalar(tabj[:], tabp[:, NC:2 * NC], -1.0, float(P), ALU.add, ALU.mult))
            link(v.tensor_tensor(tabv[:], tabj[:], tabp[:, 0:NC], ALU.add))
            link(v.tensor_copy(tabi[:], tabv[:]))
            link(v.tensor_scalar(gidx[:].rearrange("p e t -> p (e t)"), tabi[:], TOKENS - 1, None, ALU.bitwise_and))
            v.tensor_scalar(choice[:, :, :, 0].rearrange("p e t -> p (e t)"), tabv[:], float(TOKENS), None, ALU.is_lt)\
                .then_inc(s_rv, 1)
            v.tensor_scalar(choice[:, :, :, 1].rearrange("p e t -> p (e t)"), tabv[:], float(TOKENS), None, ALU.is_ge)\
                .then_inc(s_rv, 1)
            v.tensor_copy(tabg[:], gidx[:].rearrange("p e t -> p (e t)")).then_inc(s_rv, 1)
            chain[0] += 3
            link(v.tensor_scalar(tabe[:], tabp[:, NC:2 * NC], 0.5, None, ALU.is_lt))
            link(v.tensor_tensor(tabo[:], tabe[:], spare[:], ALU.mult))
            link(v.tensor_tensor(tabs[:], tabg[:], tabo[:], ALU.add))
            v.tensor_copy(sidx[:].rearrange("p e t -> p (e t)"), tabs[:]).then_inc(s_idx, 1)

            def rows_lo(e, c):
                _, _, n = CHUNKS[c]
                q = NCH * e + c
                v.wait_ge(s_thi, KD * (q + 1))
                need(v, s_w1ps, KF * (q - 1))
                for k in range(KD):
                    v.tensor_tensor(hTlo[c % 2][:, k, 0:n], psum[:, 6 + k, 0:n], f32(hThi[c % 2][:, k, 0:n]),
                                    ALU.subtract).then_inc(s_tlo, 1)

            def outputs(e, c):
                t0, nt, n = CHUNKS[c]
                q = NCH * e + c
                ts = slice(t0, t0 + nt)
                need(v, s_sca[c], 16 * nt * e)
                v.wait_ge(s_gat[c], 16 * nt * (e + 1))
                v.tensor_tensor(gp[:, ts, :], xg[:, ts, 2 * D:], choice[:, e, ts, :], ALU.mult).then_inc(s_gp, 1)
                v.wait_ge(s_gp, q + 1)
                v.tensor_reduce(gs[:, ts], gp[:, ts, :], AX_X, ALU.add).then_inc(s_gs, 1)
                for i in range(nt):
                    T = ET * e + TILES_BEFORE[c] + i
                    u = yu[(TILES_BEFORE[c] + i) % 2]
                    M = min(P, n - i * P)
                    v.wait_ge(s_w2ps, T + 1)
                    v.tensor_tensor(u[0:M, :], psum[0:M, 4 + (TILES_BEFORE[c] + i) % 2, 0:D], b2r[0:M, e, :],
                                    ALU.add).then_inc(s_yu, 1)
                    v.wait_ge(s_yu, T + 1)
                    v.wait_ge(s_gs, q + 1)
                    v.scalar_tensor_tensor(out=yb[0:M, t0 + i, :], in0=u[0:M, :], scalar=gs[0:M, t0 + i:t0 + i + 1],
                                           in1=xg[0:M, t0 + i, D:2 * D], op0=ALU.mult, op1=ALU.mult).then_inc(s_yb, 1)

            def split(e, c):
                _, _, n = CHUNKS[c]
                q, r = NCH * e + c, c % 2
                for m in range(KF):
                    v.wait_ge(s_gelu, KF * q + m + 1)
                    v.tensor_copy(ghi[r][:, m, 0:n], g32[m % NG][:, 0:n]).then_inc(s_ghi, 1)
                    v.wait_ge(s_ghi, KF * q + m + 1)
                    v.tensor_tensor(glo[r][:, m, 0:n], g32[m % NG][:, 0:n], f32(ghi[r][:, m, 0:n]), ALU.subtract)\
                        .then_inc(s_glo, 1)

            def expert(e, first, last):
                for c in range(NCH):
                    if c + 1 < NCH:
                        rows_lo(e, c + 1)
                    elif not last:
                        rows_lo(e + 1, 0)
                    _, _, n = CHUNKS[c]
                    q, r = NCH * e + c, c % 2
                    need(v, s_w2ps, ET * e + TILES_BEFORE[c - 1] if c >= 1 else ET * (e - 1) + TILES_BEFORE[NCH - 1])
                    if c != SPARE:
                        split(e, c)
                    else:
                        with v.If(load_of(v, e) > CHUNKS[c][0] * P):
                            split(e, c)
                        with v.Else():
                            v.wait_ge(s_gelu, KF * (q + 1))
                            v.tensor_copy(left_out[1][:], ident[:, 0:1]).then_inc(s_ghi, KF)
                            v.tensor_copy(left_out[2][:], ident[:, 0:1]).then_inc(s_glo, KF)
                    if c == NCH - 1 and not last:
                        for k in range(KD):
                            v.wait_ge(s_w1hi, KD * (e + 1) + k + 1)
                            v.tensor_tensor(W1lo[:, k, :], W1raw[:, k, :], f32(W1hi[:, k, :]), ALU.subtract)\
                                .then_inc(s_w1lo, 1)
                    if c > 0:
                        outputs(e, c - 1)
                    elif not first:
                        outputs(e - 1, NCH - 1)
                    if c == 0 and not first:
                        for k in range(2):
                            half = slice(k * KF // 2, (k + 1) * KF // 2)
                            v.wait_ge(s_w2hi, 2 * e + k + 1)
                            v.tensor_tensor(W2lo[:, half, :], W2raw[:, half, :], f32(W2hi[:, half, :]), ALU.subtract)\
                                .then_inc(s_w2lo, 1)

            v.wait_ge(s_idx, 1)
            v.wait_ge(s_ybz, 1)
            v.wait_ge(s_b2, 16)
            rows_lo(0, 0)
            expert(0, True, False)
            expert(1, False, False)
            with v.Fori(2, E - 1) as e:
                expert(e, False, False)
            expert(E - 1, False, True)
            outputs(E - 1, NCH - 1)


def kernel(**inputs):
    import numpy as _np
    import concourse.bacc as _bacc
    from concourse import mybir as _mybir
    from concourse.bass_utils import run_bass_kernel_spmd as _run

    a = {k: _np.asarray(v) for k, v in inputs.items()}
    D = a["L0_attn_x"].shape[-1]
    K = D // P

    def rows_by_chunk(m):
        return m.reshape(K, P, -1).transpose(1, 0, 2)

    heads = a["L0_attn_beta"].shape[0]
    E, F = a["L0_ffn_b1"].shape
    arrays = {
        "x": a["L0_attn_x"],
        "attn_wT": _np.stack([rows_by_chunk(a["L0_attn_W" + n].T) for n in "qvgo"], axis=1),
        "ln_gamma": a["L0_attn_ln_gamma"].reshape(K, P).T,
        "ln_beta": a["L0_attn_ln_beta"].reshape(K, P).T,
        "beta_ch": _np.repeat(a["L0_attn_beta"], D // heads).reshape(K, P).T,
        "router_w": rows_by_chunk(a["L0_ffn_Wg"]),
        "router_b": a["L0_ffn_bg"],
        "w1": a["L0_ffn_W1"],
        "b1": a["L0_ffn_b1"].reshape(E, F // P, P).transpose(2, 0, 1),
        "w2": a["L0_ffn_W2"],
        "b2": a["L0_ffn_b2"],
        "cT": rows_by_chunk(a["L0_c"].T),
        "wmod": a["L0_wmod"],
    }
    nc = _bacc.Bacc("TRN2", target_bir_lowering=False, num_devices=1)
    args = {}
    for name in arrays:
        arrays[name] = _np.ascontiguousarray(arrays[name])
        args[name] = nc.dram_tensor(name, arrays[name].shape, _mybir.dt.from_np(arrays[name].dtype),
                                    kind="ExternalInput").ap()
    out = nc.dram_tensor("out", a["L0_attn_x"].shape, F32, kind="ExternalOutput").ap()
    adaln_block(nc, out=out, **args)
    r = _run(nc, [arrays], core_ids=[0])
    return r.results[0]["out"]
```

```python
from contextlib import ExitStack

import concourse.bass as bass
from concourse import mybir

F32 = mybir.dt.float32
F32R = mybir.dt.float32r
BF16 = mybir.dt.bfloat16
I32 = mybir.dt.int32
U32 = mybir.dt.uint32
ALU = mybir.AluOpType
ACT = mybir.ActivationFunctionType
AX_X = mybir.AxisListType.X

P = 128
TOPK = 2


def capacity(tokens, experts):
    return -((-12 * tokens * TOPK) // (10 * experts))


def spare_rows(x, w1):
    return P * -(-capacity(x.shape[0] * x.shape[1], w1.shape[0]) // P)


def adaln_block(nc, x, attn_wT, ln_gamma, ln_beta, beta_ch, router_w, router_b, w1, b1, w2, b2, cT, wmod, out):
    B, S, D = x.shape
    E, _, F = w1.shape
    TOKENS = B * S
    KD = D // P
    KF = F // P
    TILES = TOKENS // P
    TG = 2
    GT = TG * P
    GROUPS = TILES // TG
    GPB = S // GT
    XFIRST = 8
    EPS = 1e-5
    CAP = capacity(TOKENS, E)
    ET = spare_rows(x, w1) // P
    J = TOPK * TILES
    LAST_COLS = CAP + CAP % 2 - (ET - 1) * P
    CHUNKS = [(0, 2, 2 * P), (2, 3, 3 * P), (5, 2, 2 * P), (7, 3, 2 * P + LAST_COLS)]
    NCH = len(CHUNKS)
    SPARE = NCH - 1
    TILES_BEFORE = [sum(n for _, n, _ in CHUNKS[:c]) for c in range(NCH + 1)]
    assert TILES_BEFORE[-1] == ET
    TA = TILES - 3 * TG
    MAXC = [max(CHUNKS[c][2] for c in range(NCH) if c % 2 == r) for r in range(2)]
    NEG = -3.0e38

    assert GPB == 4 and TILES % (2 * TG) == 0

    x_t = x.rearrange("b (t p) d -> p (b t) d", p=P)
    DR = 2 * D + 2
    rows_dram = nc.dram_tensor("token_rows", [TOKENS, DR], F32, kind="Internal").ap()
    assert out.shape == (TOKENS + spare_rows(x, w1), D)
    mod_dram = nc.dram_tensor("mod_rows", [B, 4 * D], F32, kind="Internal").ap()
    rows_t = rows_dram.rearrange("(t p) d -> p t d", p=P)
    out_t = out.rearrange("(t p) d -> p t d", p=P)

    keep = ExitStack()
    with keep:
        def sem(name):
            return keep.enter_context(nc.semaphore(name))

        def sb(name, shape, dt=F32, stack=keep):
            return stack.enter_context(nc.sbuf_tensor(name, shape, dt))

        psum = keep.enter_context(nc.psum_tensor("psum", [P, 8, 512], F32))

        sx = ExitStack()
        X = sb("X", [P, TILES, D], F32, sx)
        sx.close()
        NC = E * ET
        rt = {n: sb(f"rt_{n}", [P, TILES, E]) for n in ("eq", "sc", "lg2")}
        rm = {n: sb(f"rm_{n}", [P, TILES]) for n in ("m1", "i1", "m2", "i2", "dl", "ex", "se")}
        OH = sb("OH", [P, J, E], BF16)
        JC = 8
        iob = sb("iob", [P, P, JC], BF16)
        tabc, tabv, tabe, tabo, tabg, tabs = (sb(n, [P, NC]) for n in ("tabc", "tabv", "tabe", "tabo", "tabg", "tabs"))
        tabi = sb("tabi", [P, NC], I32)
        xg = sb("xg", [P, ET, DR])
        taken = P * JC // 2 + 3 * TILES * E + 7 * TILES + J * E // 2 + 7 * NC + ET * DR
        sb("rest_of_x", [P, TILES * D - taken])

        LG = sb("LG", [P, TILES, E])
        gates = sb("gates", [P, TILES, TOPK])
        GB = sb("GB", [P, B, D])
        W1raw = sb("W1raw", [P, KD, F])
        W2raw = sb("W2raw", [P, KF, D])
        b1c = sb("b1c", [P, E, KF])
        b2r = sb("b2r", [P, E, D])
        ident = sb("ident", [P, P])
        load = sb("load", [P, E], I32)
        choice = sb("choice", [P, E, ET, TOPK])
        gidx = sb("gidx", [P, E, ET], I32)
        sidx = sb("sidx", [P, E, ET], I32)

        onesj = sb("onesj", [P, J])
        minus1 = sb("minus1", [P, TILES])
        warm = sb("warm", [P, 1])
        ioi = sb("ioi", [P, P], I32)
        io = sb("io", [P, P])
        erank = sb("erank", [P, E])
        pci = sb("pci", [P, 1], I32)
        pcol = sb("pcol", [P, 1])
        jp1 = sb("jp1", [P, J], BF16)
        before = sb("before", [P, P], BF16)
        onesb = sb("onesb", [P, P], BF16)
        sparei = sb("sparei", [P, NC], I32)
        spare = sb("spare", [P, NC])

        early = ExitStack()
        wraw = sb("wraw", [P, 4, KD, D], F32, early)
        wos = sb("wos", [P, KD, D], F32, early)
        wm = sb("wm", [P, KD, 6 * D], F32, early)
        modr = sb("modr", [B, 4, D], F32, early)
        mag = sb("mag", [B, 2, D], F32, early)
        modraw = sb("modraw", [B, 2, D], F32, early)
        sgn = sb("sgn", [B, 2, D], F32, early)
        early.close()

        W1hi = sb("W1hi", [P, KD, F], F32R)
        W1lo = sb("W1lo", [P, KD, F], F32R)
        W2hi = sb("W2hi", [P, KF, D], F32R)
        W2lo = sb("W2lo", [P, KF, D], F32R)

        sa_ = ExitStack()
        zeros = sb("zeros", [P, 256], F32, sa_)
        ct = sb("ct", [P, KD, B], F32, sa_)
        sct = sb("sct", [P, KD, B], F32, sa_)
        lamraw = sb("lamraw", [P, KD], F32, sa_)
        whi = sb("whi", [P, 3, KD, D], F32R, sa_)
        wlo = sb("wlo", [P, 3, KD, D], F32R, sa_)
        wohi = sb("wohi", [P, B, KD, D], F32R, sa_)
        wolo = sb("wolo", [P, B, KD, D], F32R, sa_)
        MB = sb("MB", [P, B, 3, D], F32, sa_)
        modc = sb("modc", [P, 2, KD, B], F32, sa_)
        gcol = sb("gcol", [P, KD], F32, sa_)
        bcol = sb("bcol", [P, KD], F32, sa_)
        lam = sb("lam", [P, KD], F32, sa_)
        lamt = sb("lamt", [P, KD, GT], F32, sa_)
        neghalf = sb("neghalf", [P, 2, TG], F32, sa_)
        rw = sb("rw", [P, KD, E], F32, sa_)
        rb = sb("rb", [P, E], F32, sa_)
        state = sb("state", [P, KD, 2 * GT + 1], F32, sa_)

        def two(name, shape, dt=F32):
            return [sb(f"{name}{r}", shape, dt, sa_) for r in range(2)]

        st = {n: two(f"st_{n}", [P, TG, 6]) for n in "xyh"}
        mvs = {n: two(f"mv_{n}", [P, len(n), TG, 2]) for n in ("xy", "h")}
        ves = {n: two(f"ve_{n}", [P, len(n), TG]) for n in ("xy", "h")}
        nms = {n: two(f"nm_{n}", [P, len(n), TG]) for n in ("xy", "h")}
        rss = {n: two(f"rs_{n}", [P, len(n), TG]) for n in ("xy", "h")}
        nrs = {"xy": two("nr_xy", [P, 2, TG])}

        def of(tiles, n, r):
            return tiles["h" if n == "h" else "xy"][r][:, 1 if n == "y" else 0]

        xn = two("xn", [P, TG, D])
        h32 = two("h32_", [P, KD, GT])
        hhi = two("hhi", [P, KD, GT], F32R)
        hlo = two("hlo", [P, KD, GT], F32R)
        ysb = two("ysb", [P, KD, GT])
        gate = two("gate_", [P, KD, GT])
        yn = two("yn", [P, TG, D])
        z = two("z", [P, KD, GT])
        zg = two("zg", [P, KD, GT])
        zghi = two("zghi", [P, KD, GT], F32R)
        zglo = two("zglo", [P, KD, GT], F32R)
        xn2 = two("xn2_", [P, TG, D])
        x1 = two("x1_", [P, TG, D])
        h2 = two("h2_", [P, TG, D])
        h2T = two("h2T", [P, KD, GT])
        sa_.close()

        sr = ExitStack()
        csum = sb("csum", [P, J + 1, E], F32, sr)
        posa = sb("posa", [P, J, E], F32, sr)
        posb = sb("posb", [P, J, E], F32, sr)
        pos = sb("pos", [P, J], F32, sr)
        e10 = sb("e10", [P, J], F32, sr)
        past = sb("past", [P, J], F32, sr)
        colb = sb("colb", [P, J], F32, sr)
        posi = sb("posi", [P, J], I32, sr)
        hii = sb("hii", [P, J], I32, sr)
        hif = sb("hif", [P, J], F32, sr)
        lof = sb("lof", [P, J], BF16, sr)
        col = sb("col", [P, J], BF16, sr)
        ohlo = sb("ohlo", [P, J // JC, P, JC], BF16, sr)
        oheq = sb("oheq", [P, J // JC, NC, JC], BF16, sr)
        ohcp = sb("ohcp", [P, J // JC, 2, NC, JC], BF16, sr)
        sr.close()

        sf = ExitStack()
        hThi = [sb(f"hThi{r}", [P, KD, MAXC[r]], F32R, sf) for r in range(2)]
        hTlo = [sb(f"hTlo{r}", [P, KD, MAXC[r]], F32R, sf) for r in range(2)]
        ghi = [sb(f"ghi{r}", [P, KF, MAXC[r]], F32R, sf) for r in range(2)]
        glo = [sb(f"glo{r}", [P, KF, MAXC[r]], F32R, sf) for r in range(2)]
        NG = 4
        g32 = [sb(f"g32_{r}", [P, max(MAXC)], F32, sf) for r in range(NG)]
        yu = [sb(f"yu{r}", [P, D], F32, sf) for r in range(2)]
        yb = sb("yb", [P, ET, D], F32, sf)
        gp = sb("gp", [P, ET, TOPK], F32, sf)
        gs = sb("gs", [P, ET], F32, sf)
        left_out = [sb(f"left_out{n}", [P, 1], F32, sf) for n in range(3)]
        gcur = sb("gcur", [P, ET], I32, sf)
        scur = sb("scur", [P, ET], I32, sf)
        sf.close()

        s_x = [sem(f"x_in{r}") for r in range(2)]
        s_attnw = sem("attn_weights_in")
        s_mod_in = sem("mod_inputs_in")
        s_modrest_in = sem("mod_rest_in")
        s_beta = sem("beta_in")
        s_small = sem("small_inputs_in")
        s_modout = sem("mod_rows_out")
        s_ga = sem("ga_broadcast_in")
        s_mb = sem("mod_broadcast_in")
        s_w1 = sem("w1_in")
        s_w2 = sem("w2_in")
        s_b2 = sem("b2_in")
        s_zero = sem("spare_rows_zeroed")
        s_gbout = sem("gb_rows_out")
        s_gateout = sem("gates_out")
        s_h2out = [sem(f"h2_out{r}") for r in range(2)]
        s_x1c = [sem(f"x1_out{r}") for r in range(2)]
        s_gat = [sem(f"gathered{c}") for c in range(NCH)]
        s_sca = [sem(f"scattered{c}") for c in range(NCH)]
        (s_pc, s_sct, s_modps, s_modcps, s_modrow, s_modc, s_lam, s_lamt, s_whi, s_wlo, s_wo, s_wohi, s_zeros,
         s_w1hi, s_w1lo, s_w2hi, s_w2lo) = (sem(n) for n in (
            "pool_constants", "silu_c", "mod_rows_psum", "mod_cols_psum", "mod_rows", "mod_cols", "decay", "decay_tile",
            "attn_w_hi", "attn_w_lo", "wo_scaled_lo", "wo_hi", "zero_tile", "w1_hi", "w1_lo", "w2_hi", "w2_lo"))
        s_st = {n: sem(f"stats_{n}") for n in "xyh"}
        s_mv = {n: sem(f"meanvar_{n}") for n in "xyh"}
        s_rs = {n: sem(f"rstd_{n}") for n in ("xy", "h")}
        (s_xn, s_xT, s_h32, s_hhi, s_hlo, s_v, s_q, s_g, s_state, s_y, s_gate, s_yT, s_yn, s_ynT, s_z, s_zg, s_zghi,
         s_zglo, s_o, s_x1, s_xn2, s_h2m, s_h2, s_h2T, s_h2Ts, s_lg, s_lgs) = (sem(n) for n in (
            "xn", "xT", "h32", "h_hi", "h_lo", "v_psum", "q_psum", "g_psum", "state", "y", "gate", "yT", "yn", "ynT",
            "z", "zg", "zg_hi", "zg_lo", "o_psum", "x1", "xn2", "h2_scaled", "h2", "h2T_psum", "h2T", "logits_psum",
            "logits"))
        s_tick = sem("waits_held")
        s_modt, s_rc, s_dl, s_ohd, s_cs, s_ybz = (sem(n) for n in (
            "mod_parts", "routing_constants", "logit_delta", "chosen_experts", "tile_sums", "y_tile_cleared"))
        (s_rv, s_exp, s_cnt, s_oh, s_ohp, s_ohj, s_slots, s_idx) = (sem(n) for n in (
            "routing_steps", "exp_delta", "counts_psum", "onehots", "onehots_p", "onehots_j", "slots_psum",
            "index_tables"))
        s_iob = sem("column_numbers")
        s_ohj1 = sem("onehots_j_odd")
        s_warm = sem("gelu_table_loaded")
        s_gidx = sem("gather_table")
        (s_tr, s_thi, s_tlo, s_w1ps, s_gelu, s_ghi, s_glo, s_w2ps, s_yb, s_gcur, s_scur) = (sem(n) for n in (
            "rowsT_psum", "rowsT_hi", "rowsT_lo", "w1_psum", "gelu", "gelu_hi", "gelu_lo", "w2_psum", "y_tile",
            "gather_indices", "scatter_indices"))
        s_gates, s_gp, s_gs, s_yu = (sem(n) for n in ("gates", "slot_gate_parts", "slot_gates", "y_with_b2"))

        def need(eng, s, count):
            if not isinstance(count, int) or count > 0:
                eng.wait_ge(s, count)

        def hold(eng):
            eng.sem_inc(s_tick, 1)

        def load_of(eng, e):
            return eng.value_load(load[0:1, bass.ds(e, 1)], min_val=0, max_val=TOPK * TOKENS)

        def f32(ap):
            return ap.bitcast(F32)

        def product(eng, dst, terms, done=None):
            n = len(terms)
            for i, (lh, ll, rh, rl) in enumerate(terms):
                eng.matmul(dst, lh, rh, start=(i == 0), stop=False)
                eng.matmul(dst, lh, rl, start=False, stop=False)
                mm = eng.matmul(dst, ll, rh, start=False, stop=(i == n - 1))
            if done is not None:
                mm.then_inc(done, 1)

        def sweep(eng, step):
            for s in range(-2, 4):
                step(s, s % 2)
            with eng.Fori(2, GROUPS // 2 - 1) as i:
                step(2 * i, 0)
                step(2 * i + 1, 1)
            for s in range(GROUPS - 2, GROUPS + 3):
                step(s, s % 2)

        def has(g):
            return not isinstance(g, int) or 0 <= g < GROUPS

        def stats(eng, n, g, r, src):
            hold(eng)
            for t in range(TG):
                eng.bn_stats(st[n][r][:, t, :], src[t]).then_inc(s_st[n], 1)
            eng.wait_ge(s_st[n], TG * g + TG)
            if n == "h":
                need(eng, s_rs["h"], 3 * (g - 1))
            else:
                need(eng, s_rs["xy"], scaled_x(g - 2) if n == "x" else scaled_y(g - 2))
            hold(eng)
            for t in range(TG):
                eng.bn_aggr(of(mvs, n, r)[:, t, :], st[n][r][:, t, :]).then_inc(s_mv[n], 1)

        def scaled_x(g):
            return 4 * (g + 1)

        def scaled_y(g):
            return 4 * (g + 3)

        def rstd(eng, n, r, kinds, done):
            mv, ve, nm, rs = (tiles[n][r][:, kinds] for tiles in (mvs, ves, nms, rss))
            eng.tensor_scalar(ve, mv[:, :, :, 1], EPS, None, ALU.add).then_inc(s_rs[n], 1)
            eng.tensor_scalar(nm, mv[:, :, :, 0], -1.0, None, ALU.mult).then_inc(s_rs[n], 1)
            eng.wait_ge(s_rs[n], done + 2)
            eng.tensor_tensor(rs, ve, neghalf[:, kinds], ALU.pow).then_inc(s_rs[n], 1)
            if n == "xy":
                eng.wait_ge(s_rs[n], done + 3)
                eng.tensor_tensor(nrs[n][r][:, kinds], nm, rs, ALU.mult).then_inc(s_rs[n], 1)

        def h2_rows(eng, g, q):
            eng.wait_ge(s_rs["h"], 3 * g + 3)
            hold(eng)
            for t in range(TG):
                eng.tensor_scalar(xn2[q][:, t, :], x1[q][:, t, :], of(nms, "h", q)[:, t:t + 1],
                                   of(rss, "h", q)[:, t:t + 1], ALU.add, ALU.mult).then_inc(s_xn2, 1)
            if isinstance(g, int) and g == 0:
                eng.wait_ge(s_mb, 16 * 2)
            b = g // GPB
            eng.wait_ge(s_xn2, TG * g + TG)
            for t in range(TG):
                eng.tensor_tensor(xn2[q][:, t, :], xn2[q][:, t, :], MB[:, b, 2, :], ALU.mult)\
                    .then_inc(s_h2m, 1)
            need(eng, s_h2T, g - 1)
            need(eng, s_h2out[q], 16 * (g // 2))
            eng.wait_ge(s_h2m, TG * g + TG)
            for t in range(TG):
                eng.tensor_tensor(h2[q][:, t, :], xn2[q][:, t, :], MB[:, b, 1, :], ALU.add)\
                    .then_inc(s_h2, 1)

        BX, BV, BQ, BG, BY, BN, BO, BH = range(8)

        def bank(b):
            return psum[:, b, :].rearrange("p (k n) -> p k n", k=2)

        block = keep.enter_context(nc.Block())

        @block.sync
        def _(sp):
            def load_x(g, r):
                need(sp, s_x[r], 16 * (g // 2))
                sp.dma_start(X[:, bass.ds(TG * g, TG), :], x_t[:, bass.ds(TG * g, TG), :]).then_inc(s_x[r], 16)

            for g in range(2):
                load_x(g, g % 2)
            sp.dma_start(wraw[:], attn_wT).then_inc(s_attnw, 16)
            for dst, src in ((gcol, ln_gamma), (bcol, ln_beta), (rw, router_w), (rb, router_b.partition_broadcast(P)),
                             (b1c, b1)):
                sp.dma_start(dst[:], src).then_inc(s_small, 16)
            for g in range(2, XFIRST):
                load_x(g, g % 2)
            mod_rows = mod_dram.rearrange("b (j d) -> b j d", j=4)
            sp.wait_ge(s_modrow, 1)
            sp.dma_start(mod_rows[:, 0, :], modr[:, 0, :]).then_inc(s_modout, 16)
            sp.wait_ge(s_modout, 16)
            sp.dma_start(MB[:, :, 0, :], mod_rows[:, 0, :].partition_broadcast(P)).then_inc(s_ga, 16)
            sp.wait_ge(s_modrow, 4)
            sp.dma_start(mod_rows[:, 1:4, :], modr[:, 1:4, :]).then_inc(s_modout, 16)
            sp.wait_ge(s_modout, 32)
            sp.dma_start(MB[:, :, 1:3, :], mod_rows[:, 1:3, :].partition_broadcast(P)).then_inc(s_mb, 16)
            sp.dma_start(GB[:], mod_rows[:, 3, :].partition_broadcast(P)).then_inc(s_mb, 16)
            with sp.Fori(XFIRST // 2, GROUPS // 2) as i:
                load_x(2 * i, 0)
                load_x(2 * i + 1, 1)
            sp.wait_ge(s_zeros, 1)
            sp.dma_start(out_t[:, TILES:, :], zeros[:].unsqueeze(1).broadcast_to([P, ET, D])).then_inc(s_zero, 16)
            sp.wait_ge(s_mb, 32)
            sp.dma_start(W1raw[:], w1[0].rearrange("(k p) f -> p k f", p=P)).then_inc(s_w1, 16)
            sp.dma_start(W2raw[:], w2[0].rearrange("(k p) d -> p k d", p=P)).then_inc(s_w2, 16)
            sp.dma_start(b2r[:], b2.partition_broadcast(P)).then_inc(s_b2, 16)

            def store_rows(g, r):
                sp.dma_start(rows_t[:, bass.ds(TG * g, TG), D:2 * D],
                             GB[:, bass.ds(g // GPB, 1), :].broadcast_to([P, TG, D])).then_inc(s_gbout, 16)
                sp.wait_ge(s_x1, g + 1)
                need(sp, s_x1c[r], 16 * (g // 2))
                sp.dma_start(out_t[:, bass.ds(TG * g, TG), :], x1[r][:]).then_inc(s_x1c[r], 16)
                sp.wait_ge(s_h2, TG * (g + 1))
                need(sp, s_h2out[r], 16 * (g // 2))
                hold(sp)
                sp.dma_start(rows_t[:, bass.ds(TG * g, TG), 0:D], h2[r][:]).then_inc(s_h2out[r], 16)

            store_rows(0, 0)
            store_rows(1, 1)
            with sp.Fori(1, GROUPS // 2) as i:
                store_rows(2 * i, 0)
                store_rows(2 * i + 1, 1)

            sp.wait_ge(s_gates, 3)
            sp.dma_start(rows_t[:, :, 2 * D:], gates[:]).then_inc(s_gateout, 16)

            for c, (_, n, _) in enumerate(CHUNKS):
                sp.wait_ge(s_gat[c], 16 * n)
            with sp.Fori(1, E) as e:
                sp.wait_ge(s_w1hi, KD * e)
                sp.wait_ge(s_w1lo, KD * e)
                sp.dma_start(W1raw[:], w1[e].rearrange("(k p) f -> p k f", p=P)).then_inc(s_w1, 16)
                sp.wait_ge(s_w2hi, KD * e)
                sp.wait_ge(s_w2lo, KD * e)
                sp.dma_start(W2raw[:], w2[e].rearrange("(k p) d -> p k d", p=P)).then_inc(s_w2, 16)

            for c, (t0, n, _) in enumerate(CHUNKS):
                if c != SPARE:
                    sp.wait_ge(s_sca[c], 16 * n * E)
                else:
                    sp.wait_ge(s_sca[c], 16 * n * (E - 1))
                    with sp.If(load_of(sp, E - 1) > t0 * P):
                        sp.wait_ge(s_sca[c], 16 * n * E)

        @block.gpsimd
        def _(pool):
            pool.memset(zeros[:], 0.0).then_inc(s_zeros, 1)
            pool.memset(ident[:], 0.0).then_inc(s_pc, 1)
            pool.wait_ge(s_pc, 1)
            pool.affine_select(out=ident[:], in_=ident[:], compare_op=ALU.not_equal, fill=1.0, base=0,
                               pattern=[[-1, P]], channel_multiplier=1).then_inc(s_pc, 1)
            pool.memset(neghalf[:], -0.5).then_inc(s_pc, 1)
            pool.memset(state[:, :, 2 * GT:2 * GT + 1], 0.0).then_inc(s_pc, 1)

            def decay_tile():
                pool.wait_ge(s_zeros, 1)
                pool.wait_ge(s_lam, 1)
                for k in range(KD):
                    pool.tensor_scalar(lamt[:, k, :], zeros[:, 0:GT], lam[:, k:k + 1], 0.0, ALU.add, ALU.add)\
                        .then_inc(s_lamt, 1)

            def routing_constants():
                pool.iota(ioi[:], pattern=[[1, P]], base=0, channel_multiplier=0).then_inc(s_rc, 1)
                pool.iota(pci[:], pattern=[[0, 1]], base=0, channel_multiplier=1).then_inc(s_rc, 1)
                pool.memset(onesb[:], 1.0).then_inc(s_rc, 1)
                pool.memset(before[:], 1.0).then_inc(s_rc, 1)
                pool.memset(onesj[:], 1.0).then_inc(s_rc, 1)
                pool.memset(minus1[:], -1.0).then_inc(s_rc, 1)
                pool.iota(sparei[:], pattern=[[0, E], [P, ET]], base=P, channel_multiplier=1).then_inc(s_rc, 1)
                pool.wait_ge(s_rc, 7)
                pool.tensor_copy(spare[:], sparei[:]).then_inc(s_rc, 1)
                pool.tensor_copy(io[:], ioi[:]).then_inc(s_rc, 1)
                pool.tensor_copy(pcol[:], pci[:]).then_inc(s_rc, 1)
                pool.affine_select(out=before[:], in_=before[:], compare_op=ALU.is_gt, fill=0.0, base=0,
                                   pattern=[[1, P]], channel_multiplier=-1).then_inc(s_rc, 1)
                pool.wait_ge(s_rc, 11)
                pool.tensor_scalar(erank[:], io[:, 0:E], -1.0, float(E), ALU.mult, ALU.add).then_inc(s_rc, 1)
                pool.tensor_scalar(jp1[:], io[:, 0:J], 1.0, 0.0, ALU.add, ALU.add).then_inc(s_rc, 1)
                pool.wait_ge(s_rc, 13)

            def scale_wo(b):
                if b == 0:
                    pool.wait_ge(s_attnw, 16)
                    pool.wait_ge(s_ga, 16)
                need(pool, s_wohi, b)
                for k in range(KD):
                    pool.tensor_tensor(wos[:, k, :], wraw[:, 3, k, :], MB[:, b, 0, :], ALU.mult).then_inc(s_wo, 1)
                pool.wait_ge(s_wohi, b + 1)
                pool.wait_ge(s_wo, 3 * b + 2)
                pool.tensor_tensor(wolo[:, b], wos[:], f32(wohi[:, b]), ALU.subtract).then_inc(s_wo, 1)

            def split_first(i):
                if i < KD:
                    pool.wait_ge(s_w1, 16)
                    pool.wait_ge(s_w1hi, i + 1)
                    pool.tensor_tensor(W1lo[:, i, :], W1raw[:, i, :], f32(W1hi[:, i, :]), ALU.subtract)\
                        .then_inc(s_w1lo, 1)
                else:
                    i -= KD
                    h = slice(i * KF // 2, (i + 1) * KF // 2)
                    pool.wait_ge(s_w2, 16)
                    pool.wait_ge(s_w2hi, i + 1)
                    pool.tensor_tensor(W2lo[:, h, :], W2raw[:, h, :], f32(W2hi[:, h, :]), ALU.subtract)\
                        .then_inc(s_w2lo, 1)

            def step(s, r):
                g, q = s - 2, r
                if has(g):
                    need(pool, s_h2, TG * (g - 1))
                    pool.wait_ge(s_mv["h"], TG * g + TG)
                    hold(pool)
                    rstd(pool, "h", q, slice(0, 1), 3 * g)
                    if not (isinstance(g, int) and g == GROUPS - 1):
                        h2_rows(pool, g, q)
                if has(s + 2):
                    need(pool, s_xn, TG * (s + 1))
                    pool.wait_ge(s_mv["x"], TG * (s + 3))
                if has(s):
                    need(pool, s_yn, TG * (s - 1))
                    pool.wait_ge(s_mv["y"], TG * (s + 1))
                if has(s) or has(s + 2):
                    hold(pool)
                    rstd(pool, "xy", r, slice(0 if has(s + 2) else 1, 2 if has(s) else 1), 4 * (s + 2))
                if isinstance(s, int) and s == -2:
                    decay_tile()
                if isinstance(s, int) and s == -1:
                    routing_constants()
                if isinstance(s, int) and 0 <= s < B:
                    scale_wo(s)

            sweep(pool, step)
            for i in range(4):
                split_first(i)

            pool.wait_ge(s_exp, 1)
            pool.tensor_scalar(rm["se"][:], rm["ex"][:], 1.0, None, ALU.add).then_inc(s_gates, 1)
            pool.wait_ge(s_gates, 1)
            pool.tensor_tensor(gates[:, :, 0], rm["se"][:], minus1[:], ALU.pow).then_inc(s_gates, 1)
            pool.wait_ge(s_gates, 2)
            pool.tensor_tensor(gates[:, :, 1], rm["ex"][:], gates[:, :, 0], ALU.mult).then_inc(s_gates, 1)
            for n in range(0, J // JC, 2):
                js = slice(n * JC, n * JC + JC)
                pool.wait_ge(s_oh, 2 * n + 1)
                pool.tensor_tensor(ohcp[:, n, 1], oheq[:, n], jp1[:, js].unsqueeze(1).broadcast_to([P, NC, JC]),
                                   ALU.mult).then_inc(s_ohj, 1)

            pool.wait_ge(s_gidx, 1)
            for r in range(2):
                pool.wait_ge(s_h2out[r], 16 * (GROUPS // 2))
            pool.wait_ge(s_gbout, 16 * GROUPS)
            pool.wait_ge(s_gateout, 16)

            def gather(e, c):
                t0, n, _ = CHUNKS[c]
                need(pool, s_gat[c], 16 * n * e)
                pool.tensor_copy(gcur[:, t0:t0 + n], gidx[:, e, t0:t0 + n]).then_inc(s_gcur, 1)
                pool.wait_ge(s_gcur, NCH * e + c + 1)
                need(pool, s_tr, NCH * (e - 1) + c + 1)
                need(pool, s_yb, ET * (e - 1) + TILES_BEFORE[c + 1])
                hold(pool)
                for t in range(t0, t0 + n):
                    pool.indirect_dma_start(
                        out=xg[:, t, :], out_offset=None, in_=rows_dram,
                        in_offset=bass.IndirectOffsetOnAxis(ap=gcur[:, t:t + 1].bitcast(U32), axis=0),
                        bounds_check=TOKENS - 1, oob_is_err=False).then_inc(s_gat[c], 16)

            def scatter(e, c):
                t0, n, _ = CHUNKS[c]
                if isinstance(e, int) and e == 0:
                    pool.wait_ge(s_idx, 1)
                if c == 0:
                    for b, (_, nb, _) in enumerate(CHUNKS):
                        need(pool, s_sca[b], 16 * nb * e)
                pool.tensor_copy(scur[:, t0:t0 + n], sidx[:, e, t0:t0 + n]).then_inc(s_scur, 1)
                pool.wait_ge(s_scur, NCH * e + c + 1)
                for i in range(n):
                    t = t0 + i
                    pool.wait_ge(s_yb, ET * e + TILES_BEFORE[c] + i + 1)
                    hold(pool)
                    pool.indirect_dma_start(
                        out=out, out_offset=bass.IndirectOffsetOnAxis(ap=scur[:, t:t + 1].bitcast(U32), axis=0),
                        in_=yb[:, t, :], in_offset=None,
                        bounds_check=TOKENS + ET * P - 1, compute_op=ALU.add).then_inc(s_sca[c], 16)

            def expert(e, first, last):
                for c in range(NCH):
                    if c > 0:
                        if not last:
                            gather(e + 1, c - 1)
                        scatter(e, c - 1)
                    elif not first:
                        gather(e, NCH - 1)
                        scatter(e - 1, NCH - 1)

            for r in range(2):
                pool.wait_ge(s_x1c[r], 16 * (GROUPS // 2))
            pool.wait_ge(s_zero, 16)
            for c in range(NCH):
                gather(0, c)
                if c == 0:
                    pool.memset(yb[:, ET - 1, :], 0.0).then_inc(s_ybz, 1)
            expert(0, True, False)
            expert(1, False, False)
            with pool.Fori(2, E - 1) as e:
                expert(e, False, False)
            expert(E - 1, False, True)
            with pool.If(load_of(pool, E - 1) > CHUNKS[SPARE][0] * P):
                scatter(E - 1, SPARE)

        @block.scalar
        def _(act):
            wmod_k = wmod.rearrange("(k p) n -> p k n", p=P)
            act.dma_start(lamraw[:], beta_ch).then_inc(s_beta, 16)
            act.dma_start(wm[:, :, 0:2 * D], wmod_k[:, :, 0:2 * D]).then_inc(s_mod_in, 16)
            act.dma_start(ct[:], cT).then_inc(s_mod_in, 16)
            act.dma_start(wm[:, :, 2 * D:], wmod_k[:, :, 2 * D:]).then_inc(s_modrest_in, 16)
            act.wait_ge(s_beta, 16)
            act.activation(lam[:], lamraw[:], ACT.Sigmoid).then_inc(s_lam, 1)
            act.wait_ge(s_mod_in, 32)
            act.activation(sct[:], ct[:], ACT.Silu).then_inc(s_sct, 1)

            def step(s, r):
                q = 1 - r
                if isinstance(s, int) and s == GROUPS + 1:
                    for i in range(KD):
                        act.wait_ge(s_w1, 16)
                        act.activation(W1hi[:, i, :], W1raw[:, i, :], ACT.Copy).then_inc(s_w1hi, 1)
                    for i in range(2):
                        half = slice(i * KF // 2, (i + 1) * KF // 2)
                        act.wait_ge(s_w2, 16)
                        act.activation(W2hi[:, half, :], W2raw[:, half, :], ACT.Copy).then_inc(s_w2hi, 1)
                if isinstance(s, int) and s == -1:
                    act.wait_ge(s_attnw, 16)
                    for w in (1, 0, 2):
                        act.activation(whi[:, w], wraw[:, w], ACT.Copy).then_inc(s_whi, 1)
                g = s - 1
                if has(g):
                    act.wait_ge(s_ynT, g + 1)
                    need(act, s_zg, g - 1)
                    if isinstance(g, int) and g == 0:
                        act.wait_ge(s_small, 16 * 5)
                    for k in range(KD):
                        act.activation(z[q][:, k, :], bank(BN)[:, k, :], ACT.Identity, bias=bcol[:, k:k + 1],
                                       scale=gcol[:, k:k + 1]).then_inc(s_z, 1)
                g = s + 1
                if has(g):
                    act.wait_ge(s_rs["xy"], scaled_x(g))
                    need(act, s_xT, g - 1)
                    hold(act)
                    for t in range(TG):
                        act.activation(xn[q][:, t, :], X[:, TG * g + t, :], ACT.Identity,
                                       bias=of(nrs, "x", q)[:, t:t + 1],
                                       scale=of(rss, "x", q)[:, t:t + 1]).then_inc(s_xn, 1)
                g = s - 1
                if has(g):
                    act.wait_ge(s_zg, g + 1)
                    need(act, s_o, g - 1)
                    act.activation(zghi[q][:], zg[q][:], ACT.Copy).then_inc(s_zghi, 1)
                g = s + 1
                if has(g):
                    b = g // GPB
                    act.wait_ge(s_xT, g + 1)
                    need(act, s_hlo, g - 1)
                    if isinstance(g, int) and g == 0:
                        act.wait_ge(s_modc, 2)
                    hold(act)
                    for k in range(KD):
                        act.activation(h32[q][:, k, :], bank(BX)[:, k, :], ACT.Identity,
                                       bias=modc[:, 0, k, bass.ds(b, 1)], scale=modc[:, 1, k, bass.ds(b, 1)])\
                            .then_inc(s_h32, 1)
                    act.wait_ge(s_h32, KD * (g + 1))
                    need(act, s_g, g - 1)
                    act.activation(hhi[q][:], h32[q][:], ACT.Copy).then_inc(s_hhi, 1)
                g = s
                if has(g):
                    act.wait_ge(s_g, g + 1)
                    need(act, s_zg, g - 1)
                    act.activation(gate[r][:], bank(BG), ACT.Silu).then_inc(s_gate, 1)
                g = s
                if has(g):
                    act.wait_ge(s_rs["xy"], scaled_y(g))
                    need(act, s_ynT, g - 1)
                    for t in range(TG):
                        act.activation(yn[r][:, t, :], bank(BY)[:, t, :], ACT.Identity,
                                       bias=of(nrs, "y", r)[:, t:t + 1],
                                       scale=of(rss, "y", r)[:, t:t + 1]).then_inc(s_yn, 1)
                g = s - 2
                if has(g):
                    act.wait_ge(s_h2T, g + 1)
                    need(act, s_lg, g - 1)
                    act.activation(h2T[r][:], bank(BH), ACT.Copy).then_inc(s_h2Ts, 1)
                if isinstance(s, int) and 0 <= s < B:
                    act.wait_ge(s_wo, 3 * s + 2)
                    act.activation(wohi[:, s], wos[:], ACT.Copy).then_inc(s_wohi, 1)

            sweep(act, step)

            act.wait_ge(s_rc, 13)
            act.activation(iob[:], io[:].unsqueeze(2).broadcast_to([P, P, JC]), ACT.Copy).then_inc(s_iob, 1)
            act.wait_ge(s_dl, 1)
            act.activation(rm["ex"][:], rm["dl"][:], ACT.Exp).then_inc(s_exp, 1)
            for n in range(J // JC):
                act.wait_ge(s_oh, 2 * n + 1)
                act.activation(ohcp[:, n, 0], oheq[:, n], ACT.Copy, scale=pcol[:, 0:1]).then_inc(s_ohp, 1)

            act.activation(warm[:], ident[:, 0:1], ACT.Gelu_apprx_tanh).then_inc(s_warm, 1)

            def rows_hi(e, c):
                _, _, n = CHUNKS[c]
                q = NCH * e + c
                act.wait_ge(s_tr, q + 1)
                need(act, s_w1ps, KF * (q - 1))
                for k in range(KD):
                    act.activation(hThi[c % 2][:, k, 0:n], psum[:, 6 + k, 0:n], ACT.Copy).then_inc(s_thi, 1)

            def gelu(e, c):
                _, _, n = CHUNKS[c]
                q = NCH * e + c
                for m in range(KF):
                    act.wait_ge(s_w1ps, KF * q + m + 1)
                    need(act, s_glo, KF * q + m + 1 - NG)
                    hold(act)
                    act.activation(g32[m % NG][:, 0:n], psum[:, m % 4, 0:n], ACT.Gelu_apprx_tanh,
                                   bias=b1c[:, e, m:m + 1]).then_inc(s_gelu, 1)

            def expert(e, first, last):
                for c in range(NCH):
                    q = NCH * e + c
                    if first and c == 0:
                        gelu(e, c)
                    if c + 1 < NCH:
                        rows_hi(e, c + 1)
                    elif not last:
                        rows_hi(e + 1, 0)
                    if first and c == 0:
                        pass
                    elif c != SPARE:
                        gelu(e, c)
                    else:
                        with act.If(load_of(act, e) > CHUNKS[c][0] * P):
                            gelu(e, c)
                        with act.Else():
                            act.wait_ge(s_w1ps, KF * (q + 1))
                            hold(act)
                            act.activation(left_out[0][:], ident[:, 0:1], ACT.Copy).then_inc(s_gelu, KF)
                    if c == NCH - 1 and not last:
                        act.wait_ge(s_w1, 16 * (e + 2))
                        act.wait_ge(s_w1ps, KF * NCH * (e + 1))
                        for k in range(KD):
                            act.activation(W1hi[:, k, :], W1raw[:, k, :], ACT.Copy).then_inc(s_w1hi, 1)
                    if c == 0 and not first:
                        act.wait_ge(s_w2, 16 * (e + 1))
                        act.wait_ge(s_w2ps, ET * e)
                        for k in range(2):
                            half = slice(k * KF // 2, (k + 1) * KF // 2)
                            act.activation(W2hi[:, half, :], W2raw[:, half, :], ACT.Copy).then_inc(s_w2hi, 1)

            act.wait_ge(s_idx, 1)
            rows_hi(0, 0)
            expert(0, True, False)
            with act.Fori(1, E - 1) as e:
                expert(e, False, False)
            expert(E - 1, False, True)

        @block.tensor
        def _(pe):
            def mod_columns():
                pe.wait_ge(s_sct, 1)
                for j in range(2):
                    for m in range(KD):
                        for k in range(KD):
                            mm = pe.matmul(psum[:, BG, (j * KD + m) * B:(j * KD + m + 1) * B],
                                           wm[:, k, j * D + m * P:j * D + (m + 1) * P], sct[:, k, :],
                                           start=(k == 0), stop=(k == KD - 1))
                mm.then_inc(s_modcps, 1)

            def mod_rows(b, n):
                pe.wait_ge(s_modrest_in, 16)
                for k in range(KD):
                    mm = pe.matmul(psum[0:B, b, :], sct[:, k, :], wm[:, k, n * 512:(n + 1) * 512],
                                   start=(k == 0), stop=(k == KD - 1))
                mm.then_inc(s_modps, 1)

            mod_columns()
            pe.wait_ge(s_pc, 4)
            pe.wait_ge(s_modc, 2)

            def turn(dst, src, r):
                for k in range(KD):
                    for t in range(TG):
                        last = pe.transpose(dst[:, k, t * P:(t + 1) * P], src[:, t, k * P:(k + 1) * P], ident[:])
                return last

            def project(w, g, r, done, dst):
                for m in range(KD):
                    ms = slice(m * P, (m + 1) * P)
                    product(pe, dst[:, m, :], [(whi[:, w, k, ms], wlo[:, w, k, ms], hhi[r][:, k, :], hlo[r][:, k, :])
                                               for k in range(KD)], done if m == KD - 1 else None)

            def step(s, r):
                q = 1 - r
                g = s
                if has(g):
                    if isinstance(g, int) and g == 0:
                        mod_rows(BO, 1)
                        pe.wait_ge(s_wlo, 3)
                    pe.wait_ge(s_hhi, g + 1)
                    pe.wait_ge(s_hlo, g + 1)
                    need(pe, s_state, KD * g)
                    project(1, g, r, s_v, bank(BV))
                g = s - 1
                if has(g):
                    pe.wait_ge(s_yn, TG * (g + 1))
                    need(pe, s_z, KD * g)
                    turn(bank(BN), yn[q], q).then_inc(s_ynT, 1)
                g = s
                if has(g):
                    need(pe, s_y, g)
                    project(0, g, r, s_q, bank(BQ))
                    if isinstance(g, int) and g == 0:
                        mod_rows(BH, 2)
                g = s - 3
                if has(g):
                    pe.wait_ge(s_h2Ts, g + 1)
                    need(pe, s_lgs, g)
                    pe.wait_ge(s_h32, KD * (min(g + 4, GROUPS) if isinstance(g, int) else g + 4))
                    for t in range(TG):
                        for k in range(KD):
                            mm = pe.matmul(psum[:, BX, t * E:(t + 1) * E], h2T[q][:, k, t * P:(t + 1) * P], rw[:, k, :],
                                           start=(k == 0), stop=(k == KD - 1))
                    mm.then_inc(s_lg, 1)
                g = s
                if has(g):
                    pe.wait_ge(s_y, g + 1)
                    need(pe, s_yn, TG * g)
                    turn(bank(BY), ysb[r], r).then_inc(s_yT, 1)
                g = s + 1
                if has(g):
                    pe.wait_ge(s_xn, TG * (g + 1))
                    need(pe, s_h32, KD * g)
                    need(pe, s_lgs, g - 3)
                    turn(bank(BX), xn[q], q).then_inc(s_xT, 1)
                g = s
                if has(g):
                    need(pe, s_gate, g)
                    project(2, g, r, s_g, bank(BG))
                g = s - 1
                if has(g):
                    b = g // GPB
                    pe.wait_ge(s_zghi, g + 1)
                    pe.wait_ge(s_zglo, g + 1)
                    if isinstance(g, int) and g == 0:
                        pe.wait_ge(s_modrow, 2)
                    need(pe, s_x1, g)
                    if isinstance(g, int):
                        pe.wait_ge(s_wo, 3 * min(g // GPB + 1, B))
                    else:
                        pe.wait_ge(s_wo, 3 * B)
                    for t in range(TG):
                        ts = slice(t * P, (t + 1) * P)
                        product(pe, bank(BO)[:, t, :], [(zghi[q][:, k, ts], zglo[q][:, k, ts], wohi[:, b, k, :],
                                                         wolo[:, b, k, :]) for k in range(KD)],
                                s_o if t == TG - 1 else None)
                g = s - 2
                if has(g):
                    pe.wait_ge(s_h2, TG * (g + 1))
                    need(pe, s_h2Ts, g)
                    turn(bank(BH), h2[r], r).then_inc(s_h2T, 1)

            sweep(pe, step)

            pe.wait_ge(s_ohd, 4)
            pe.wait_ge(s_rc, 13)
            ohf = OH[:].rearrange("p j e -> p (j e)")
            pe.matmul(psum[:, 0, :], before[:], ohf, start=True, stop=True).then_inc(s_cnt, 1)
            pe.matmul(psum[:, 1, :], onesb[:], ohf, start=True, stop=True).then_inc(s_cnt, 1)
            for n in range(J // JC):
                pe.wait_ge(s_oh, 2 * n + 2)
                pe.wait_ge(s_ohp, n + 1)
                pe.wait_ge(s_ohj if n % 2 == 0 else s_ohj1, n // 2 + 1)
                for j in range(JC):
                    mm = pe.matmul(psum[:, 2, 0:2 * NC], ohlo[:, n, :, j],
                                   ohcp[:, n, :, :, j].rearrange("p a c -> p (a c)"),
                                   start=(n == 0 and j == 0), stop=(n == J // JC - 1 and j == JC - 1))
            mm.then_inc(s_slots, 1)

            def rows(e, c):
                t0, n, _ = CHUNKS[c]
                q = NCH * e + c
                pe.wait_ge(s_gat[c], 16 * n * (e + 1))
                need(pe, s_thi, KD * q)
                need(pe, s_tlo, KD * q)
                for k in range(KD):
                    for i in range(n):
                        tr = pe.transpose(psum[:, 6 + k, i * P:(i + 1) * P], xg[:, t0 + i, k * P:(k + 1) * P], ident[:])
                tr.then_inc(s_tr, 1)

            def up(e, c, held):
                _, _, n = CHUNKS[c]
                q, r = NCH * e + c, c % 2
                pe.wait_ge(s_thi, KD * (q + 1))
                pe.wait_ge(s_tlo, KD * (q + 1))
                pe.wait_ge(s_w1hi, KD * (e + 1))
                pe.wait_ge(s_w1lo, KD * (e + 1))

                def hidden(w1_product):
                    for m in range(KF):
                        need(pe, s_gelu, KF * q + m + 1 - 4)
                        w1_product(psum[:, m % 4, 0:n], slice(m * P, (m + 1) * P))

                def two_tiles(dst, ms):
                    full(dst, ms, 2 * P)

                def full(dst, ms, w=n):
                    product(pe, dst[:, 0:w], [(W1hi[:, k, ms], W1lo[:, k, ms], hThi[r][:, k, 0:w], hTlo[r][:, k, 0:w])
                                              for k in range(KD)], s_w1ps)

                first, _, _ = CHUNKS[c]
                if c != SPARE:
                    hidden(full)
                else:
                    with pe.If(held > first * P):
                        with pe.If(held > (first + 2) * P):
                            hidden(full)
                        with pe.Else():
                            hidden(two_tiles)
                    with pe.Else():
                        need(pe, s_gelu, KF * q + 1 - 4)
                        pe.matmul(psum[:, 0, 0:8], W1hi[:, 0, 0:P], hThi[r][:, 0, 0:8], start=True, stop=True)\
                            .then_inc(s_w1ps, KF)

            def down(e, c, held):
                t0, nt, n = CHUNKS[c]
                q, r = NCH * e + c, c % 2
                pe.wait_ge(s_glo, KF * (q + 1))
                pe.wait_ge(s_w2hi, 2 * (e + 1))
                pe.wait_ge(s_w2lo, 2 * (e + 1))

                def tile(i, stands_for=0):
                    cols = slice(i * P, min((i + 1) * P, n))
                    dst = psum[0:cols.stop - cols.start, 4 + (TILES_BEFORE[c] + i) % 2, 0:D]
                    need(pe, s_yu, ET * e + TILES_BEFORE[c] + i - 1)
                    if not stands_for:
                        product(pe, dst, [(ghi[r][:, m, cols], glo[r][:, m, cols], W2hi[:, m, :], W2lo[:, m, :])
                                          for m in range(KF)], s_w2ps)
                    else:
                        pe.matmul(dst[:, 0:8], ghi[r][:, 0, cols], W2hi[:, 0, 0:8], start=True, stop=True)\
                            .then_inc(s_w2ps, stands_for)

                if c != SPARE:
                    for i in range(nt):
                        tile(i)
                else:
                    with pe.If(held > t0 * P):
                        tile(0)
                        for i in range(1, nt):
                            with pe.If(held > (t0 + i) * P):
                                tile(i)
                            with pe.Else():
                                tile(i, stands_for=1)
                    with pe.Else():
                        tile(0, stands_for=nt)

            def expert(e, first, last):
                held = load_of(pe, e)
                for c in range(NCH):
                    if first and c == 0:
                        up(e, c, held)
                    if c + 1 < NCH:
                        rows(e, c + 1)
                    elif not last:
                        rows(e + 1, 0)
                    if not (first and c == 0):
                        up(e, c, held)
                    if c > 0:
                        down(e, c - 1, held)
                    elif not first:
                        down(e - 1, NCH - 1, load_of(pe, e - 1))

            pe.wait_ge(s_idx, 1)
            rows(0, 0)
            expert(0, True, False)
            with pe.Fori(1, E - 1) as e:
                expert(e, False, False)
            expert(E - 1, False, True)
            down(E - 1, NCH - 1, load_of(pe, E - 1))

        @block.vector
        def _(v):
            def mod_rows(b, n):
                v.wait_ge(s_modps, n + 1)
                src, other = (psum[0:B, b, h * D:(h + 1) * D] for h in (n, 1 - n))
                v.tensor_copy(modraw[:, n, :], src).then_inc(s_modt, 1)
                v.tensor_scalar(sgn[:, n, :], src, 0.0, 2.0, ALU.is_ge, ALU.mult).then_inc(s_modt, 1)
                v.wait_ge(s_modt, 4 * n + 1)
                v.scalar_tensor_tensor(out=mag[:, n, :], in0=modraw[:, n, :], scalar=-1.0, in1=modraw[:, n, :],
                                       op0=ALU.mult, op1=ALU.max).then_inc(s_modt, 1)
                v.wait_ge(s_modt, 4 * n + 3)
                v.tensor_scalar(mag[:, n, :], mag[:, n, :], 0.25, None, ALU.max).then_inc(s_modt, 1)
                v.wait_ge(s_modt, 4 * n + 4)
                v.scalar_tensor_tensor(out=modr[:, 3 * n, :], in0=sgn[:, n, :], scalar=1.0, in1=mag[:, n, :],
                                       op0=ALU.subtract, op1=ALU.mult).then_inc(s_modrow, 1)
                v.tensor_scalar(modr[:, 1 + n, :], other, float(n), None, ALU.add).then_inc(s_modrow, 1)

            def mod_columns():
                v.wait_ge(s_modcps, 1)
                mc = psum[:, BG, 0:2 * KD * B].rearrange("p (j m b) -> p j m b", j=2, m=KD)
                v.tensor_copy(modc[:, 0], mc[:, 0]).then_inc(s_modc, 1)
                v.tensor_scalar(modc[:, 1], mc[:, 1], 1.0, None, ALU.add).then_inc(s_modc, 1)

            def attn_w_lo():
                for n, w in enumerate((1, 0, 2)):
                    v.wait_ge(s_whi, n + 1)
                    v.tensor_tensor(wlo[:, w], wraw[:, w], f32(whi[:, w]), ALU.subtract).then_inc(s_wlo, 1)

            chain = [0]

            def link(ins):
                ins.then_inc(s_rv, 1)
                chain[0] += 1
                v.wait_ge(s_rv, chain[0])

            def select(ts, k):
                T = ts.stop - ts.start
                v.wait_ge(s_rc, 13)
                v.wait_ge(s_lgs, ts.stop // TG)
                lg = (LG if k == 0 else rt["lg2"])[:, ts, :]
                m, i = (rm[f"{n}{k + 1}"][:, ts] for n in "mi")
                oh = OH[:, k * TILES + ts.start:k * TILES + ts.stop, :]
                eq, sc = rt["eq"][:, ts, :], rt["sc"][:, ts, :]
                if k == 1:
                    v.wait_ge(s_ohd, 2 * (ts.start > 0) + 1)
                    link(v.scalar_tensor_tensor(out=lg, in0=OH[:, ts, :], scalar=NEG, in1=LG[:, ts, :],
                                                op0=ALU.mult, op1=ALU.add))
                link(v.tensor_reduce(m, lg, AX_X, ALU.max))
                link(v.tensor_tensor(eq, lg, m.unsqueeze(2).broadcast_to([P, T, E]), ALU.is_equal))
                link(v.tensor_tensor(sc, eq, erank[:].unsqueeze(1).broadcast_to([P, T, E]), ALU.mult))
                link(v.tensor_reduce(i, sc, AX_X, ALU.max))
                v.tensor_tensor(oh, sc, i.unsqueeze(2).broadcast_to([P, T, E]), ALU.is_equal).then_inc(s_ohd, 1)

            def step(s, r):
                q = 1 - r
                if isinstance(s, int) and s == GROUPS:
                    select(slice(0, TA), 0)
                if isinstance(s, int) and s == GROUPS + 1:
                    h2_rows(v, GROUPS - 1, r)
                g = s
                if has(g):
                    v.wait_ge(s_v, g + 1)
                    need(v, s_state, KD * g)
                    if isinstance(g, int) and g == 0:
                        v.wait_ge(s_lamt, KD)
                        v.wait_ge(s_pc, 4)
                    for k in range(KD):
                        if r == 1:
                            init = state[:, k, GT - 1:GT]
                        else:
                            new = (g // 2) % (GPB // 2)
                            if isinstance(g, int):
                                at = 2 * GT - min(new, 1)
                            else:
                                at = 2 * GT - new
                            init = state[:, k, bass.ds(at, 1)]
                        v.tensor_tensor_scan(state[:, k, r * GT:(r + 1) * GT], lamt[:, k, :], bank(BV)[:, k, :],
                                             init, ALU.mult, ALU.add).then_inc(s_state, 1)
                g = s - 1
                if has(g):
                    v.wait_ge(s_z, KD * (g + 1))
                    v.wait_ge(s_gate, g + 1)
                    need(v, s_zghi, g - 1)
                    v.tensor_tensor(zg[q][:], z[q][:], gate[q][:], ALU.mult).then_inc(s_zg, 1)
                g = s
                if has(g):
                    v.wait_ge(s_q, g + 1)
                    v.wait_ge(s_state, KD * (g + 1))
                    need(v, s_yT, g - 1)
                    v.tensor_tensor(ysb[r][:], bank(BQ), state[:, :, r * GT:(r + 1) * GT], ALU.mult).then_inc(s_y, 1)
                g = s - 3
                if has(g):
                    v.wait_ge(s_lg, g + 1)
                    v.tensor_tensor(LG[:, bass.ds(TG * g, TG), :],
                                    psum[:, BX, 0:TG * E].rearrange("p (t e) -> p t e", t=TG),
                                    rb[:].unsqueeze(1).broadcast_to([P, TG, E]), ALU.add).then_inc(s_lgs, 1)
                g = s + 2
                if has(g):
                    v.wait_ge(s_x[r], 16 * (g // 2 + 1))
                    stats(v, "x", g, r, [X[:, TG * g + t, :] for t in range(TG)])
                g = s - 1
                if has(g):
                    v.wait_ge(s_zghi, g + 1)
                    need(v, s_o, g - 1)
                    v.tensor_tensor(zglo[q][:], zg[q][:], f32(zghi[q][:]), ALU.subtract).then_inc(s_zglo, 1)
                if isinstance(s, int) and s == GROUPS:
                    select(slice(0, TA), 1)
                g = s
                if has(g):
                    v.wait_ge(s_yT, g + 1)
                    stats(v, "y", g, r, [bank(BY)[:, t, :] for t in range(TG)])
                if isinstance(s, int) and s == 0:
                    mod_rows(BH, 1)
                if isinstance(s, int) and s == -1:
                    mod_columns()
                    attn_w_lo()
                g = s + 1
                if has(g):
                    v.wait_ge(s_hhi, g + 1)
                    need(v, s_g, g - 1)
                    v.tensor_tensor(hlo[q][:], h32[q][:], f32(hhi[q][:]), ALU.subtract).then_inc(s_hlo, 1)
                if isinstance(s, int) and s == -1:
                    mod_rows(BO, 0)
                g = s - 1
                if has(g):
                    v.wait_ge(s_o, g + 1)
                    need(v, s_x1c[q], 16 * (g // 2))
                    need(v, s_xn2, TG * (g - 1))
                    v.tensor_tensor(x1[q][:], X[:, bass.ds(TG * g, TG), :], bank(BO), ALU.add).then_inc(s_x1, 1)
                    v.wait_ge(s_x1, g + 1)
                    stats(v, "h", g, q, [x1[q][:, t, :] for t in range(TG)])

            sweep(v, step)

            for k in range(TOPK):
                select(slice(TA, TILES), k)
            v.tensor_tensor(rm["dl"][:], rm["m2"][:], rm["m1"][:], ALU.subtract).then_inc(s_dl, 1)
            for r in range(2):
                v.wait_ge(s_h2out[r], 16 * (GROUPS // 2))
                v.wait_ge(s_x1c[r], 16 * (GROUPS // 2))
            v.wait_ge(s_zero, 16)
            v.wait_ge(s_h2Ts, GROUPS)
            v.wait_ge(s_ohd, 4)
            link(v.memset(csum[:, 0, :], 0.0))
            for k in range(TOPK):
                link(v.tensor_scalar(e10[:, k * TILES:(k + 1) * TILES], rm[f"i{k + 1}"][:], -float(ET), float(ET * E),
                                     ALU.mult, ALU.add))
            v.wait_ge(s_cnt, 2)
            tot = psum[:, 1, :].rearrange("p (j e) -> p j e", e=E)
            for e in range(E):
                v.tensor_tensor_scan(csum[:, 1:, e], onesj[:], tot[:, :, e], 0.0, ALU.mult, ALU.add).then_inc(s_cs, 1)
            v.wait_ge(s_cs, E)
            link(v.tensor_tensor(posa[:], psum[:, 0, :].rearrange("p (j e) -> p j e", e=E), csum[:, 0:J, :], ALU.add))
            link(v.tensor_tensor(posb[:], posa[:], OH[:], ALU.mult))
            link(v.tensor_reduce(pos[:], posb[:], AX_X, ALU.add))
            v.tensor_scalar(past[:], pos[:], float(CAP), 4.0 * NC, ALU.is_ge, ALU.mult).then_inc(s_rv, 1)
            chain[0] += 1
            link(v.tensor_copy(posi[:], pos[:]))
            v.tensor_tensor(colb[:], past[:], e10[:], ALU.add).then_inc(s_rv, 1)
            chain[0] += 1
            link(v.tensor_scalar(hii[:], posi[:], 7, None, ALU.arith_shift_right))
            link(v.tensor_copy(hif[:], hii[:]))
            v.tensor_tensor(col[:], hif[:], colb[:], ALU.add).then_inc(s_rv, 1)
            chain[0] += 1
            link(v.scalar_tensor_tensor(out=lof[:], in0=hif[:], scalar=-float(P), in1=pos[:], op0=ALU.mult,
                                        op1=ALU.add))
            v.wait_ge(s_iob, 1)
            for n in range(J // JC):
                js = slice(n * JC, n * JC + JC)
                v.tensor_tensor(oheq[:, n], iob[:, 0:NC, :], col[:, js].unsqueeze(1).broadcast_to([P, NC, JC]),
                                ALU.is_equal).then_inc(s_oh, 1)
                v.tensor_tensor(ohlo[:, n], iob[:], lof[:, js].unsqueeze(1).broadcast_to([P, P, JC]),
                                ALU.is_equal).then_inc(s_oh, 1)
                if n % 2 == 1:
                    v.wait_ge(s_oh, 2 * n + 1)
                    v.tensor_tensor(ohcp[:, n, 1], oheq[:, n], jp1[:, js].unsqueeze(1).broadcast_to([P, NC, JC]),
                                    ALU.mult).then_inc(s_ohj1, 1)
            link(v.tensor_copy(load[:], csum[:, J, :]))
            v.wait_ge(s_slots, 1)
            link(v.tensor_copy(tabc[:], psum[:, 2, 0:NC]))
            link(v.scalar_tensor_tensor(out=tabv[:], in0=psum[:, 2, NC:2 * NC], scalar=float(P), in1=tabc[:],
                                        op0=ALU.mult, op1=ALU.add))
            link(v.tensor_scalar(tabi[:], tabv[:], -float(P), None, ALU.add))
            v.tensor_scalar(gidx[:].rearrange("p e t -> p (e t)"), tabi[:], TOKENS - 1, None, ALU.bitwise_and)\
                .then_inc(s_gidx, 1)
            link(v.tensor_scalar(tabe[:], psum[:, 2, NC:2 * NC], 0.5, None, ALU.is_lt))
            v.wait_ge(s_gidx, 1)
            v.tensor_copy(tabg[:], gidx[:].rearrange("p e t -> p (e t)")).then_inc(s_rv, 1)
            v.tensor_scalar(choice[:, :, :, 0].rearrange("p e t -> p (e t)"), tabv[:], float(TOKENS + P), None,
                            ALU.is_lt).then_inc(s_rv, 1)
            v.tensor_scalar(choice[:, :, :, 1].rearrange("p e t -> p (e t)"), tabv[:], float(TOKENS + P), None,
                            ALU.is_ge).then_inc(s_rv, 1)
            chain[0] += 3
            link(v.tensor_tensor(tabo[:], tabe[:], spare[:], ALU.mult))
            link(v.tensor_tensor(tabs[:], tabg[:], tabo[:], ALU.add))
            v.tensor_copy(sidx[:].rearrange("p e t -> p (e t)"), tabs[:]).then_inc(s_idx, 1)

            def rows_lo(e, c):
                _, _, n = CHUNKS[c]
                q = NCH * e + c
                v.wait_ge(s_thi, KD * (q + 1))
                need(v, s_w1ps, KF * (q - 1))
                for k in range(KD):
                    v.tensor_tensor(hTlo[c % 2][:, k, 0:n], psum[:, 6 + k, 0:n], f32(hThi[c % 2][:, k, 0:n]),
                                    ALU.subtract).then_inc(s_tlo, 1)

            def outputs(e, c):
                t0, nt, n = CHUNKS[c]
                q = NCH * e + c
                ts = slice(t0, t0 + nt)
                need(v, s_sca[c], 16 * nt * e)
                v.wait_ge(s_gat[c], 16 * nt * (e + 1))
                v.tensor_tensor(gp[:, ts, :], xg[:, ts, 2 * D:], choice[:, e, ts, :], ALU.mult).then_inc(s_gp, 1)
                v.wait_ge(s_gp, q + 1)
                v.tensor_reduce(gs[:, ts], gp[:, ts, :], AX_X, ALU.add).then_inc(s_gs, 1)
                for i in range(nt):
                    T = ET * e + TILES_BEFORE[c] + i
                    u = yu[(TILES_BEFORE[c] + i) % 2]
                    M = min(P, n - i * P)
                    v.wait_ge(s_w2ps, T + 1)
                    v.tensor_tensor(u[0:M, :], psum[0:M, 4 + (TILES_BEFORE[c] + i) % 2, 0:D], b2r[0:M, e, :],
                                    ALU.add).then_inc(s_yu, 1)
                    v.wait_ge(s_yu, T + 1)
                    v.wait_ge(s_gs, q + 1)
                    v.scalar_tensor_tensor(out=yb[0:M, t0 + i, :], in0=u[0:M, :], scalar=gs[0:M, t0 + i:t0 + i + 1],
                                           in1=xg[0:M, t0 + i, D:2 * D], op0=ALU.mult, op1=ALU.mult).then_inc(s_yb, 1)

            def split(e, c):
                _, _, n = CHUNKS[c]
                q, r = NCH * e + c, c % 2
                for m in range(KF):
                    v.wait_ge(s_gelu, KF * q + m + 1)
                    v.tensor_copy(ghi[r][:, m, 0:n], g32[m % NG][:, 0:n]).then_inc(s_ghi, 1)
                    v.wait_ge(s_ghi, KF * q + m + 1)
                    v.tensor_tensor(glo[r][:, m, 0:n], g32[m % NG][:, 0:n], f32(ghi[r][:, m, 0:n]), ALU.subtract)\
                        .then_inc(s_glo, 1)

            def expert(e, first, last):
                for c in range(NCH):
                    q = NCH * e + c
                    if first and c == 0:
                        split(e, c)
                    if c + 1 < NCH:
                        rows_lo(e, c + 1)
                    elif not last:
                        rows_lo(e + 1, 0)
                    need(v, s_w2ps, ET * e + TILES_BEFORE[c - 1] if c >= 1 else ET * (e - 1) + TILES_BEFORE[NCH - 1])
                    if first and c == 0:
                        pass
                    elif c != SPARE:
                        split(e, c)
                    else:
                        with v.If(load_of(v, e) > CHUNKS[c][0] * P):
                            split(e, c)
                        with v.Else():
                            v.wait_ge(s_gelu, KF * (q + 1))
                            v.tensor_copy(left_out[1][:], ident[:, 0:1]).then_inc(s_ghi, KF)
                            v.tensor_copy(left_out[2][:], ident[:, 0:1]).then_inc(s_glo, KF)
                    if c == NCH - 1 and not last:
                        for k in range(KD):
                            v.wait_ge(s_w1hi, KD * (e + 1) + k + 1)
                            v.tensor_tensor(W1lo[:, k, :], W1raw[:, k, :], f32(W1hi[:, k, :]), ALU.subtract)\
                                .then_inc(s_w1lo, 1)
                    if c > 0:
                        outputs(e, c - 1)
                    elif not first:
                        outputs(e - 1, NCH - 1)
                    if c == 0 and not first:
                        for k in range(2):
                            half = slice(k * KF // 2, (k + 1) * KF // 2)
                            v.wait_ge(s_w2hi, 2 * e + k + 1)
                            v.tensor_tensor(W2lo[:, half, :], W2raw[:, half, :], f32(W2hi[:, half, :]), ALU.subtract)\
                                .then_inc(s_w2lo, 1)

            v.wait_ge(s_idx, 1)
            v.wait_ge(s_ybz, 1)
            v.wait_ge(s_b2, 16)
            rows_lo(0, 0)
            expert(0, True, False)
            expert(1, False, False)
            with v.Fori(2, E - 1) as e:
                expert(e, False, False)
            expert(E - 1, False, True)
            outputs(E - 1, NCH - 1)


def kernel(**inputs):
    import numpy as _np
    import concourse.bacc as _bacc
    from concourse import mybir as _mybir
    from concourse.bass_utils import run_bass_kernel_spmd as _run

    a = {k: _np.asarray(v) for k, v in inputs.items()}
    D = a["L0_attn_x"].shape[-1]
    K = D // P

    def rows_by_chunk(m):
        return m.reshape(K, P, -1).transpose(1, 0, 2)

    heads = a["L0_attn_beta"].shape[0]
    E, F = a["L0_ffn_b1"].shape
    arrays = {
        "x": a["L0_attn_x"],
        "attn_wT": _np.stack([rows_by_chunk(a["L0_attn_W" + n].T) for n in "qvgo"], axis=1),
        "ln_gamma": a["L0_attn_ln_gamma"].reshape(K, P).T,
        "ln_beta": a["L0_attn_ln_beta"].reshape(K, P).T,
        "beta_ch": _np.repeat(a["L0_attn_beta"], D // heads).reshape(K, P).T,
        "router_w": rows_by_chunk(a["L0_ffn_Wg"]),
        "router_b": a["L0_ffn_bg"],
        "w1": a["L0_ffn_W1"],
        "b1": a["L0_ffn_b1"].reshape(E, F // P, P).transpose(2, 0, 1),
        "w2": a["L0_ffn_W2"],
        "b2": a["L0_ffn_b2"],
        "cT": rows_by_chunk(a["L0_c"].T),
        "wmod": a["L0_wmod"],
    }
    nc = _bacc.Bacc("TRN2", target_bir_lowering=False, num_devices=1)
    args = {}
    for name in arrays:
        arrays[name] = _np.ascontiguousarray(arrays[name])
        args[name] = nc.dram_tensor(name, arrays[name].shape, _mybir.dt.from_np(arrays[name].dtype),
                                    kind="ExternalInput").ap()
    B, S, _ = a["L0_attn_x"].shape
    out = nc.dram_tensor("out", [B * S + spare_rows(a["L0_attn_x"], a["L0_ffn_W1"]), D], F32,
                         kind="ExternalOutput").ap()
    adaln_block(nc, out=out, **args)
    r = _run(nc, [arrays], core_ids=[0])
    return r.results[0]["out"][:B * S].reshape(B, S, D)
```
